# Optimizing a Trainium2 kernel written in Bass

```python
import numpy as np
import jax
import jax.numpy as jnp

def _softmax(x, axis=-1):
    return jax.nn.softmax(x, axis=axis)

def _gelu(x):
    return jax.nn.gelu(x, approximate=True)

def _silu(x):
    return jax.nn.silu(x)

def _sigmoid(x):
    return jax.nn.sigmoid(x)

def _layernorm(x, axis=-1, eps=1e-05):
    m = jnp.mean(x, axis=axis, keepdims=True)
    v = jnp.var(x, axis=axis, keepdims=True)
    return (x - m) / jnp.sqrt(v + eps)

def _scatter_add(tgt, idx, src, axis=0):
    return tgt.at[idx].add(src)

def _segment_sum(src, seg, n):
    return jax.ops.segment_sum(src, seg, n)
kernel_name = 'mk_decoder_postln_d2_seqx_r2_1117a1'

def setup_inputs(seed: int=0):
    np.random.seed(seed)
    _w = jnp.asarray

    def _rec_inputs():
        import jax
        import jax.numpy as jnp
        _rk = jax.random.key(seed)
        x = 7.22e-05 + 1 * jax.random.normal(jax.random.fold_in(_rk, 1), (8, 100, 512), jnp.float32)
        _lenS = 100 - jax.random.randint(jax.random.fold_in(_rk, 7), (8,), 0, max(1, 100 // 4) + 1, jnp.int32)
        _lenS2 = 722 - jax.random.randint(jax.random.fold_in(_rk, 8), (8,), 0, max(1, 722 // 4) + 1, jnp.int32)
        _ctx_1024P = jax.random.normal(jax.random.fold_in(_rk, 11), (8, 16, 512), jnp.float32)
        _ctx_1024c = jax.random.dirichlet(jax.random.fold_in(_rk, 511), 0.3 * jnp.ones((16,), jnp.float32), (8, 722))
        _ctx_1024t = jnp.einsum('bsk,bkd->bsd', _ctx_1024c, _ctx_1024P)
        _ctx_1024t = _ctx_1024t * jax.lax.rsqrt(jnp.mean(jnp.square(_ctx_1024t)) + 1e-12) * 0.953939
        ctx_1024 = 4.13588e-05 + 0.999923 * (_ctx_1024t + 0.3 * jax.random.normal(jax.random.fold_in(_rk, 611), (8, 722, 512), jnp.float32))
        _validS = jnp.arange(100)[None, :] < _lenS[:, None]
        _validS2 = jnp.arange(722)[None, :] < _lenS2[:, None]
        _causal = jnp.tril(jnp.ones((100, 100), dtype=bool))
        mask_BxS2_ik0 = jnp.where(jnp.broadcast_to(_validS2[:, :], (8, 722)), 0, 1).astype(jnp.int32)
        return (x, ctx_1024, mask_BxS2_ik0)
    x, ctx_1024, mask_BxS2_ik0 = _rec_inputs()

    def _L0_attn_setup():
        import jax, jax.numpy as jnp
        import numpy as np
        L, B, D = (2048, 4, 512)
        key = jax.random.key(seed)
        k1, k2, k3, k4 = jax.random.split(key, 4)
        return {'x': jax.random.normal(k1, (L, B, D), dtype=jnp.float32), 'lmlg': jax.random.normal(k2, (D,), dtype=jnp.float32), 'theta': jax.random.normal(k3, (D,), dtype=jnp.float32), 'last_conv_init': jax.random.normal(k4, (D,), dtype=jnp.float32)}
    _L0_attn_all = _L0_attn_setup()
    _L0_attn_in = {k: v for k, v in _L0_attn_all.items() if k in ('lmlg', 'theta', 'last_conv_init')}
    del _L0_attn_all

    def _L0_xattn_setup():
        import jax, jax.numpy as jnp
        import numpy as np
        HEADS = 16
        key = jax.random.key(seed)
        ks = jax.random.split(key, 10)
        B, S, D = (4, 1024, 512)
        s = 1.0 / np.sqrt(D)
        return {'query': jax.random.normal(ks[0], (B, S, D), jnp.float32), 'bank': jax.random.normal(ks[1], (B, S, D), jnp.float32), 'Wq': jax.random.normal(ks[2], (D, D), jnp.float32) * s, 'bq': jax.random.normal(ks[3], (D,), jnp.float32) * 0.02, 'Wk': jax.random.normal(ks[4], (D, D), jnp.float32) * s, 'bk': jax.random.normal(ks[5], (D,), jnp.float32) * 0.02, 'Wv': jax.random.normal(ks[6], (D, D), jnp.float32) * s, 'bv': jax.random.normal(ks[7], (D,), jnp.float32) * 0.02, 'Wo': jax.random.normal(ks[8], (D, D), jnp.float32) * s, 'bo': jax.random.normal(ks[9], (D,), jnp.float32) * 0.02}
    _L0_xattn_all = _L0_xattn_setup()
    _L0_xattn_in = {k: v for k, v in _L0_xattn_all.items() if k in ('Wq', 'bq', 'Wk', 'bk', 'Wv', 'bv', 'Wo', 'bo')}
    del _L0_xattn_all

    def _L0_ffn_setup():
        import jax, jax.numpy as jnp
        import numpy as np
        D_MODEL, D_FF, RANK = (512, 2048, 128)
        B, S = (4, 2048)
        key = jax.random.key(seed)
        ks = jax.random.split(key, 7)
        return {'x': jax.random.normal(ks[0], (B, S, D_MODEL), dtype=jnp.float32), 'U1': jax.random.normal(ks[1], (D_MODEL, RANK), dtype=jnp.float32) * 0.02, 'V1': jax.random.normal(ks[2], (RANK, D_FF), dtype=jnp.float32) * 0.02, 'b1': jnp.zeros((D_FF,), dtype=jnp.float32), 'U2': jax.random.normal(ks[3], (D_FF, RANK), dtype=jnp.float32) * 0.02, 'V2': jax.random.normal(ks[4], (RANK, D_MODEL), dtype=jnp.float32) * 0.02, 'b2': jnp.zeros((D_MODEL,), dtype=jnp.float32)}
    _L0_ffn_all = _L0_ffn_setup()
    _L0_ffn_in = {k: v for k, v in _L0_ffn_all.items() if k in ('U1', 'V1', 'b1', 'U2', 'V2', 'b2')}
    del _L0_ffn_all

    def _L1_attn_setup():
        import jax, jax.numpy as jnp
        import numpy as np
        B, T, C, H = (2, 1024, 512, 16)
        DH = C // H
        EPS = 1e-05

        def _rotary(t_len, d_head):
            inv_freq = 1.0 / 10000.0 ** (jnp.arange(0, d_head, 2, dtype=jnp.float32) / d_head)
            t = jnp.arange(t_len, dtype=jnp.float32)
            freqs = t[:, None] * inv_freq[None, :]
            emb = jnp.concatenate([freqs, freqs], axis=-1)
            return (jnp.cos(emb), jnp.sin(emb))

        def _apply_rope(x, cos, sin):
            d = x.shape[-1]
            x1, x2 = (x[..., :d // 2], x[..., d // 2:])
            x_rot = jnp.concatenate([-x2, x1], axis=-1)
            return x * cos + x_rot * sin

        def _decay_mask(t_len, n_head):
            gammas = 1.0 - 2.0 ** (-5.0 - jnp.arange(n_head, dtype=jnp.float32))
            n = jnp.arange(t_len)[:, None]
            m = jnp.arange(t_len)[None, :]
            dist = n - m
            decay = gammas[:, None, None] ** jnp.maximum(dist, 0).astype(jnp.float32)
            return jnp.where(dist[None] >= 0, decay, 0.0)
        key = jax.random.key(seed)
        ks = jax.random.split(key, 7)
        s = 1.0 / np.sqrt(C)
        return {'x': jax.random.normal(ks[0], (B, T, C), dtype=jnp.float32), 'Wq': jax.random.normal(ks[1], (C, C), dtype=jnp.float32) * s, 'Wk': jax.random.normal(ks[2], (C, C), dtype=jnp.float32) * s, 'Wv': jax.random.normal(ks[3], (C, C), dtype=jnp.float32) * s, 'Wo': jax.random.normal(ks[4], (C, C), dtype=jnp.float32) * s, 'gn_weight': jnp.ones((C,), dtype=jnp.float32), 'gn_bias': jnp.zeros((C,), dtype=jnp.float32)}
    _L1_attn_all = _L1_attn_setup()
    _L1_attn_in = {k: v for k, v in _L1_attn_all.items() if k in ('Wq', 'Wk', 'Wv', 'Wo', 'gn_weight', 'gn_bias')}
    del _L1_attn_all

    def _L1_xattn_setup():
        import jax, jax.numpy as jnp
        import numpy as np
        B, N, N2 = (4, 1024, 512)
        DIM, DIM_Y, H = (512, 512, 16)
        HD = DIM // H
        SCALE = HD ** (-0.5)
        key = jax.random.key(seed)
        ks = jax.random.split(key, 6)
        s = 0.02
        return {'x': jax.random.normal(ks[0], (B, N, DIM), dtype=jnp.float32), 'y': jax.random.normal(ks[1], (B, N2, DIM_Y), dtype=jnp.float32), 'pad_mask': jax.random.randint(ks[2], (B, N2), 0, 2, dtype=jnp.int32), 'Wq': jax.random.normal(ks[3], (DIM, DIM), dtype=jnp.float32) * s, 'Wkv': jax.random.normal(ks[4], (DIM_Y, 2 * DIM), dtype=jnp.float32) * s, 'Wproj': jax.random.normal(ks[5], (DIM, DIM), dtype=jnp.float32) * s, 'bproj': jnp.zeros((DIM,), dtype=jnp.float32)}
    _L1_xattn_all = _L1_xattn_setup()
    _L1_xattn_in = {k: v for k, v in _L1_xattn_all.items() if k in ('Wq', 'Wkv', 'Wproj', 'bproj')}
    del _L1_xattn_all

    def _L1_ffn_setup():
        import jax, jax.numpy as jnp
        import numpy as np
        D_IN, D_HID = (512, 2048)

        def _ternary(key, shape):
            return jax.random.randint(key, shape, -1, 2).astype(jnp.float32)

        def _tlin(x, w, s):
            return jnp.einsum('bsi,oi->bso', x, w) * s
        key = jax.random.key(seed)
        ks = jax.random.split(key, 12)
        inv = lambda fan: 1.0 / np.sqrt(fan).astype(np.float32)
        return {'x': jax.random.normal(ks[0], (4, 1024, D_IN), dtype=jnp.float32), 'w1_w': _ternary(ks[1], (D_HID, D_IN)), 'w1_s': jax.random.uniform(ks[2], (D_HID,), dtype=jnp.float32) * inv(D_IN), 'w2_w': _ternary(ks[3], (D_HID, D_IN)), 'w2_s': jax.random.uniform(ks[4], (D_HID,), dtype=jnp.float32) * inv(D_IN), 'h1_w': _ternary(ks[5], (D_HID, D_HID)), 'h1_s': jax.random.uniform(ks[6], (D_HID,), dtype=jnp.float32) * inv(D_HID), 'h2_w': _ternary(ks[7], (D_HID, D_HID)), 'h2_s': jax.random.uniform(ks[8], (D_HID,), dtype=jnp.float32) * inv(D_HID), 'w3_w': _ternary(ks[9], (D_IN, D_HID)), 'w3_s': jax.random.uniform(ks[10], (D_IN,), dtype=jnp.float32) * inv(D_HID)}
    _L1_ffn_all = _L1_ffn_setup()
    _L1_ffn_in = {k: v for k, v in _L1_ffn_all.items() if k in ('w1_w', 'w1_s', 'w2_w', 'w2_s', 'h1_w', 'h1_s', 'h2_w', 'h2_s', 'w3_w', 'w3_s')}
    del _L1_ffn_all
    return {'x': x, 'ctx_1024': ctx_1024, 'mask_BxS2_ik0': mask_BxS2_ik0, 'L0_attn_lmlg': _L0_attn_in['lmlg'], 'L0_attn_theta': _L0_attn_in['theta'], 'L0_attn_last_conv_init': _L0_attn_in['last_conv_init'], 'L0_xattn_Wq': _L0_xattn_in['Wq'], 'L0_xattn_bq': _L0_xattn_in['bq'], 'L0_xattn_Wk': _L0_xattn_in['Wk'], 'L0_xattn_bk': _L0_xattn_in['bk'], 'L0_xattn_Wv': _L0_xattn_in['Wv'], 'L0_xattn_bv': _L0_xattn_in['bv'], 'L0_xattn_Wo': _L0_xattn_in['Wo'], 'L0_xattn_bo': _L0_xattn_in['bo'], 'L0_ffn_U1': _L0_ffn_in['U1'], 'L0_ffn_V1': _L0_ffn_in['V1'], 'L0_ffn_b1': _L0_ffn_in['b1'], 'L0_ffn_U2': _L0_ffn_in['U2'], 'L0_ffn_V2': _L0_ffn_in['V2'], 'L0_ffn_b2': _L0_ffn_in['b2'], 'L1_attn_Wq': _L1_attn_in['Wq'], 'L1_attn_Wk': _L1_attn_in['Wk'], 'L1_attn_Wv': _L1_attn_in['Wv'], 'L1_attn_Wo': _L1_attn_in['Wo'], 'L1_attn_gn_weight': _L1_attn_in['gn_weight'], 'L1_attn_gn_bias': _L1_attn_in['gn_bias'], 'L1_xattn_Wq': _L1_xattn_in['Wq'], 'L1_xattn_Wkv': _L1_xattn_in['Wkv'], 'L1_xattn_Wproj': _L1_xattn_in['Wproj'], 'L1_xattn_bproj': _L1_xattn_in['bproj'], 'L1_ffn_w1_w': _L1_ffn_in['w1_w'], 'L1_ffn_w1_s': _L1_ffn_in['w1_s'], 'L1_ffn_w2_w': _L1_ffn_in['w2_w'], 'L1_ffn_w2_s': _L1_ffn_in['w2_s'], 'L1_ffn_h1_w': _L1_ffn_in['h1_w'], 'L1_ffn_h1_s': _L1_ffn_in['h1_s'], 'L1_ffn_h2_w': _L1_ffn_in['h2_w'], 'L1_ffn_h2_s': _L1_ffn_in['h2_s'], 'L1_ffn_w3_w': _L1_ffn_in['w3_w'], 'L1_ffn_w3_s': _L1_ffn_in['w3_s']}

def reference(x, ctx_1024, mask_BxS2_ik0, L0_attn_lmlg, L0_attn_theta, L0_attn_last_conv_init, L0_xattn_Wq, L0_xattn_bq, L0_xattn_Wk, L0_xattn_bk, L0_xattn_Wv, L0_xattn_bv, L0_xattn_Wo, L0_xattn_bo, L0_ffn_U1, L0_ffn_V1, L0_ffn_b1, L0_ffn_U2, L0_ffn_V2, L0_ffn_b2, L1_attn_Wq, L1_attn_Wk, L1_attn_Wv, L1_attn_Wo, L1_attn_gn_weight, L1_attn_gn_bias, L1_xattn_Wq, L1_xattn_Wkv, L1_xattn_Wproj, L1_xattn_bproj, L1_ffn_w1_w, L1_ffn_w1_s, L1_ffn_w2_w, L1_ffn_w2_s, L1_ffn_h1_w, L1_ffn_h1_s, L1_ffn_h2_w, L1_ffn_h2_s, L1_ffn_w3_w, L1_ffn_w3_s):
    import jax
    import jax.numpy as jnp

    def _L0_attn_ref(x, lmlg, theta, last_conv_init):
        import jax, jax.numpy as jnp
        import numpy as np
        L, B, D = (2048, 4, 512)
        seq_len, batch, dim = x.shape
        gamma = jnp.exp(-jnp.exp(lmlg))
        c = gamma * jnp.exp(1j * theta)
        n = jnp.arange(seq_len)[:, None]
        filt = c[None, :] ** n
        filt_fft = jnp.fft.fft(filt, n=2 * seq_len, axis=0)
        x_fft = jnp.fft.fft(x, n=2 * seq_len, axis=0)
        conv_filter_x = jnp.fft.ifft(filt_fft[:, None, :] * x_fft, axis=0)[:seq_len]
        last_conv = jax.lax.stop_gradient(jnp.broadcast_to(last_conv_init.astype(conv_filter_x.dtype), (batch, dim)))
        conv_with_past = conv_filter_x + last_conv[None, :, :] * filt[:, None, :] * c[None, None, :]
        return conv_with_past.real * x

    def _L0_xattn_ref(query, bank, Wq, bq, Wk, bk, Wv, bv, Wo, bo):
        import jax, jax.numpy as jnp
        import numpy as np
        HEADS = 16
        B, S, D = query.shape
        H = HEADS
        hd = D // H
        scale = jnp.asarray(np.sqrt(hd), query.dtype)

        def split_heads(x):
            return x.reshape(B, -1, H, hd).transpose(0, 2, 1, 3)
        q = split_heads(query @ Wq + bq)
        k = split_heads(bank @ Wk + bk)
        v = split_heads(bank @ Wv + bv)
        scores = jnp.einsum('bhqd,bhkd->bhqk', q, k) / scale
        attn = jax.nn.softmax(scores, axis=-1)
        out = jnp.einsum('bhqk,bhkd->bhqd', attn, v)
        out = out.transpose(0, 2, 1, 3).reshape(B, -1, D)
        return out @ Wo + bo

    def _L0_ffn_ref(x, U1, V1, b1, U2, V2, b2):
        import jax, jax.numpy as jnp
        import numpy as np
        D_MODEL, D_FF, RANK = (512, 2048, 128)
        B, S = (4, 2048)
        P = jnp.einsum('bsd,dr->bsr', x, U1)
        H = jax.nn.gelu(jnp.einsum('bsr,rf->bsf', P, V1) + b1)
        Q = jnp.einsum('bsf,fr->bsr', H, U2)
        return jnp.einsum('bsr,rd->bsd', Q, V2) + b2

    def _L1_attn_ref(x, Wq, Wk, Wv, Wo, gn_weight, gn_bias):
        import jax, jax.numpy as jnp
        import numpy as np
        B, T, C, H = (2, 1024, 512, 16)
        DH = C // H
        EPS = 1e-05

        def _rotary(t_len, d_head):
            inv_freq = 1.0 / 10000.0 ** (jnp.arange(0, d_head, 2, dtype=jnp.float32) / d_head)
            t = jnp.arange(t_len, dtype=jnp.float32)
            freqs = t[:, None] * inv_freq[None, :]
            emb = jnp.concatenate([freqs, freqs], axis=-1)
            return (jnp.cos(emb), jnp.sin(emb))

        def _apply_rope(x, cos, sin):
            d = x.shape[-1]
            x1, x2 = (x[..., :d // 2], x[..., d // 2:])
            x_rot = jnp.concatenate([-x2, x1], axis=-1)
            return x * cos + x_rot * sin

        def _decay_mask(t_len, n_head):
            gammas = 1.0 - 2.0 ** (-5.0 - jnp.arange(n_head, dtype=jnp.float32))
            n = jnp.arange(t_len)[:, None]
            m = jnp.arange(t_len)[None, :]
            dist = n - m
            decay = gammas[:, None, None] ** jnp.maximum(dist, 0).astype(jnp.float32)
            return jnp.where(dist[None] >= 0, decay, 0.0)
        b, t, c = x.shape

        def proj(W):
            return jnp.einsum('btc,oc->bto', x, W).reshape(b, t, H, DH).transpose(0, 2, 1, 3)
        q, k, v = (proj(Wq), proj(Wk), proj(Wv))
        cos, sin = _rotary(t, DH)
        q = _apply_rope(q, cos, sin)
        k = _apply_rope(k, cos, sin)
        decay = _decay_mask(t, H)
        qk = jnp.einsum('bhtd,bhsd->bhts', q, k) * (1.0 / np.sqrt(DH))
        qk = qk * decay[None]
        out = jnp.einsum('bhts,bhsd->bhtd', qk, v)
        out = out.transpose(0, 2, 1, 3)
        mu = jnp.mean(out, axis=-1, keepdims=True)
        var = jnp.mean((out - mu) ** 2, axis=-1, keepdims=True)
        out = (out - mu) * jax.lax.rsqrt(var + EPS)
        out = out * gn_weight.reshape(H, DH) + gn_bias.reshape(H, DH)
        out = out.reshape(b, t, c)
        return jnp.einsum('btc,oc->bto', out, Wo)

    def _L1_xattn_ref(x, y, pad_mask, Wq, Wkv, Wproj, bproj):
        import jax, jax.numpy as jnp
        import numpy as np
        B, N, N2 = (4, 1024, 512)
        DIM, DIM_Y, H = (512, 512, 16)
        HD = DIM // H
        SCALE = HD ** (-0.5)
        b, n, c = x.shape
        n2 = y.shape[1]
        q = (x @ Wq).reshape(b, n, H, HD).transpose(0, 2, 1, 3)
        kv = (y @ Wkv).reshape(b, n2, 2, H, HD).transpose(2, 0, 3, 1, 4)
        k, v = (kv[0], kv[1])
        scores = jnp.einsum('bhnd,bhmd->bhnm', q * SCALE, k)
        keep = pad_mask.astype(bool)[:, None, None, :]
        scores = jnp.where(keep, scores, -jnp.inf)
        attn = jax.nn.softmax(scores, axis=-1)
        out = jnp.einsum('bhnm,bhmd->bhnd', attn, v)
        out = out.transpose(0, 2, 1, 3).reshape(b, n, c)
        return out @ Wproj + bproj

    def _L1_ffn_ref(x, w1_w, w1_s, w2_w, w2_s, h1_w, h1_s, h2_w, h2_s, w3_w, w3_s):
        import jax, jax.numpy as jnp
        import numpy as np
        D_IN, D_HID = (512, 2048)

        def _ternary(key, shape):
            return jax.random.randint(key, shape, -1, 2).astype(jnp.float32)

        def _tlin(x, w, s):
            return jnp.einsum('bsi,oi->bso', x, w) * s
        h = jax.nn.silu(_tlin(x, w1_w, w1_s)) * _tlin(x, w2_w, w2_s)
        h = jax.nn.gelu(_tlin(h, h1_w, h1_s), approximate=False)
        h = jax.nn.gelu(_tlin(h, h2_w, h2_s), approximate=False)
        return _tlin(h, w3_w, w3_s)
    x = _layernorm(x + _L0_attn_ref(x, L0_attn_lmlg, L0_attn_theta, L0_attn_last_conv_init), axis=-1)
    x = _layernorm(x + _L0_xattn_ref(x, ctx_1024, L0_xattn_Wq, L0_xattn_bq, L0_xattn_Wk, L0_xattn_bk, L0_xattn_Wv, L0_xattn_bv, L0_xattn_Wo, L0_xattn_bo), axis=-1)
    x = _layernorm(x + _L0_ffn_ref(x, L0_ffn_U1, L0_ffn_V1, L0_ffn_b1, L0_ffn_U2, L0_ffn_V2, L0_ffn_b2), axis=-1)
    x = _layernorm(x + _L1_attn_ref(x, L1_attn_Wq, L1_attn_Wk, L1_attn_Wv, L1_attn_Wo, L1_attn_gn_weight, L1_attn_gn_bias), axis=-1)
    x = _layernorm(x + _L1_xattn_ref(x, ctx_1024, mask_BxS2_ik0, L1_xattn_Wq, L1_xattn_Wkv, L1_xattn_Wproj, L1_xattn_bproj), axis=-1)
    x = _layernorm(x + _L1_ffn_ref(x, L1_ffn_w1_w, L1_ffn_w1_s, L1_ffn_w2_w, L1_ffn_w2_s, L1_ffn_h1_w, L1_ffn_h1_s, L1_ffn_h2_w, L1_ffn_h2_s, L1_ffn_w3_w, L1_ffn_w3_s), axis=-1)
    return x

_drawn_inputs = setup_inputs


def setup_inputs(seed=0):
    import zlib

    import numpy as np

    out = dict(_drawn_inputs(seed))
    spreads = {'L0_ffn_b1': (0.0, 0.412),
     'L0_ffn_b2': (0.0, 0.1),
     'L1_attn_gn_weight': (1.0, 0.2),
     'L1_attn_gn_bias': (0.0, 0.1),
     'L1_xattn_bproj': (0.0, 0.1)}
    factors = {'L0_xattn_bq': 5.713,
     'L0_xattn_bk': 8.0,
     'L0_ffn_U1': 2.78,
     'L0_ffn_V1': 2.838,
     'L1_xattn_Wq': 5.556,
     'L1_ffn_w1_w': 8.0,
     'L1_ffn_w1_s': 8.0,
     'L1_ffn_w2_w': 8.0,
     'L1_ffn_w2_s': 8.0,
     'L1_ffn_h1_w': 8.0,
     'L1_ffn_h1_s': 8.0,
     'L1_ffn_h2_w': 8.0,
     'L1_ffn_h2_s': 8.0,
     'L1_ffn_w3_w': 8.0,
     'L1_ffn_w3_s': 8.0}
    for name, (base, spread) in spreads.items():
        noise = np.random.default_rng([zlib.crc32(name.encode()), seed]).standard_normal(out[name].shape)
        drawn = base * np.exp(spread * noise) if base else spread * noise
        out[name] = jnp.asarray(drawn.astype(out[name].dtype))
    for name, factor in factors.items():
        out[name] = (out[name] * factor).astype(out[name].dtype)
    return out
```

```python
import concourse.bass as bass
from concourse import mybir
from contextlib import ExitStack
from collections import namedtuple

NB, T, D = 8, 100, 512
KEYS = 722
H, HD = 16, 32
P = 128
C = D // P
TOK = NB * T
HALF = TOK // 2
G = H // C
FF = 2048
M = FF // P
EPS = 1e-5
SCALE = HD ** -0.5
BLK = 1024
KA = 512
PIECES = ((0, KA), (KA, KEYS - KA))
KC = 128
NKC = -(-KEYS // KC)
PK = NKC * KC
HK = NKC // 2
RANK = 128
TAPS = NB + 1

COLUMNS = [("lmlg", C), ("theta", C), ("init", C), ("bq", C), ("bk", C), ("bv", C), ("gnw", C), ("gnb", C),
           ("b1", M), ("w1s", M), ("w2s", M), ("h1s", M), ("h2s", M), ("w3s", C)]
COL_AT = {}
for _n, _k in COLUMNS:
    COL_AT[_n] = sum(k for _, k in COLUMNS[:len(COL_AT)])
NCOL = sum(k for _, k in COLUMNS)

LN_CONV, LN_ATT0, LN_FFN0, LN_RET, LN_ATT1, LN_FFN1 = (NB * i for i in range(6))

BLOCKS = {}
_n = 0
for _name, _k in [("wk0", 2), ("wv0", 2), ("wq0", 2), ("wo0", 2), ("u1", 1), ("v1", 2), ("u2", 2), ("v2", 1),
                  ("rq", 2), ("rk", 2), ("rv", 2), ("ro", 2), ("wk1", 2), ("wv1", 2), ("wq1", 2), ("wo1", 2),
                  ("w12", M), ("h1", 2 * M), ("h2", 2 * M), ("w3", 2 * C)]:
    BLOCKS[_name] = _n
    _n += _k


Pair = namedtuple("Pair", "hi lo")

LN_LAST = LN_FFN1
CH_DEC, CH_ANG = 7, 16
MASKED = -1e38
LOWEST = -3e38
R_UNITS = 4 * C


def key_rows(j):
    return min(KC, KEYS - j * KC)


def decoder_kernel(nc, d):
    fp32, f32r, i32 = mybir.dt.float32, mybir.dt.float32r, mybir.dt.int32
    ACT, ALU, AX = mybir.ActivationFunctionType, mybir.AluOpType, mybir.AxisListType
    top = [-(-nc.sbuf_base // 64) * 64]
    LIMIT = nc.sbuf_usable_end

    def at(name, shape, dt):
        n = 4
        for x in shape[1:]:
            n *= x
        t = nc.alloc_sbuf_tensor_at(name, shape, dt, offset=top[0])
        top[0] += -(-n // 32) * 32
        assert top[0] <= LIMIT, (name, top[0], LIMIT)
        return t

    def pair(name, shape):
        return Pair(at(name + "_hi", shape, f32r), at(name + "_lo", shape, f32r))

    ctx = ExitStack()
    with ctx:
        def sem(name):
            return ctx.enter_context(nc.semaphore(name))

        raw = at("raw", [P, 2, BLK], fp32)
        x_res = at("x_res", [T, NB, D], fp32)
        ident = at("ident", [P, P], fp32)
        cols = at("cols", [P, NCOL], fp32)
        y = at("y", [T, 2, D], fp32)
        stats = at("stats", [T, 2, 6], fp32)
        mv = at("mv", [T, 2, 2], fp32)
        veps = at("veps", [T, 2, 1], fp32)
        rstd = at("rstd", [T, 2, 1], fp32)
        mhalf = at("mhalf", [P, H], fp32)
        shared_end = top[0]
        xT = pair("xT", [P, C, TOK])
        resid = at("resid", [T, 2, D], fp32)
        rows = at("rows", [T, 3, D], fp32)
        sel = at("sel", [H, C, P], fp32)
        phase_at = top[0]

        wkv_at = top[0]
        wk, wv = pair("wk", [P, C, D]), pair("wv", [P, C, D])
        wqo_at = top[0]
        wqo = pair("wqo", [P, C, D])
        craw_at = top[0]
        ctx_raw = at("ctx_raw", [P, 2, KEYS], fp32)
        cT_at = top[0]
        cT = pair("cT", [P, C, KEYS])
        vv_at = top[0]
        vv = pair("vv", [P, NKC, D])
        kT_at = top[0]
        kT = pair("kT", [P, 2, KEYS])
        conv_at = top[0]
        q_all = at("q_all", [P, C, TOK], fp32)
        p = at("p", [T, 2, PK], fp32)
        maskb = at("maskb", [T, KEYS], fp32)
        mask_raw = at("mask_raw", [T, KEYS], i32)
        rsum = at("rsum", [T, H], fp32)
        rinv = at("rinv", [T, P], fp32)
        nmax = at("nmax", [T, 2], fp32)
        pmax = at("pmax", [T, 2], fp32)
        rT = at("rT", [H, T], fp32)
        att_bq = at("att_bq", [P, C], fp32)
        oT = pair("oT", [P, C, T])
        top[0] = shared_end
        pT = pair("pT", [P, 2, NKC, 2 * T])
        qs = pair("qs", [P, C, T])
        oraw = at("oraw", [P, C, T], fp32)
        assert top[0] <= shared_end + 2 * 4 * C * TOK

        top[0] = conv_at
        cin = at("cin", [P, C, TOK], fp32)
        small = lambda n, *s: at(n, [P, *s], fp32)
        e1, th, thn = small("e1", C), small("th", C), small("thn", C)
        kvec, turns, ang, dec, taps = (small(n, C, TAPS) for n in ("kvec", "turns", "ang", "dec", "taps"))
        past = small("past", C, NB)
        top[0] = shared_end
        acc = at("acc", [P, C, TOK], fp32)

        top[0] = wkv_at
        v1, u2 = pair("v1", [P, FF]), pair("u2", [P, M, RANK])
        assert top[0] <= wqo_at
        top[0] = cT_at
        u1, v2 = pair("u1", [P, C, RANK]), pair("v2", [P, D])
        f_p, f_q = pair("f_p", [P, TOK]), pair("f_q", [P, TOK])
        assert top[0] <= vv_at
        top[0] = vv_at
        f_act, f_g = at("f_act", [P, 4, HALF], fp32), pair("f_g", [P, 4, HALF])
        assert top[0] <= kT_at

        top[0] = wkv_at
        qk = [at("q_rope", [P, C, TOK], fp32), at("k_rope", [P, C, TOK], fp32)]
        kb, xb = pair("kb", [P, C, T]), pair("xb", [P, C, T])
        assert top[0] <= wqo_at
        top[0] = wqo_at
        rqo = pair("rqo", [P, C, D])
        assert top[0] <= craw_at
        ctab, stab = at("ctab", [P, T], fp32), at("stab", [P, T], fp32)
        rotm = at("rotm", [P, P], fp32)
        assert top[0] <= cT_at
        top[0] = cT_at
        qbd = pair("qbd", [P, C, G, T])
        vb = pair("vb", [T, D])
        r_o, r_oT = at("r_o", [P, C, T], fp32), pair("r_oT", [P, C, T])
        assert top[0] <= vv_at
        top[0] = vv_at
        decay = at("decay", [T, H, T], fp32)
        p_raw, pb = at("p_raw", [T, 2, G * T], fp32), pair("pb", [T, 2, G * T])
        gd, gsq = at("gd", [T, D], fp32), at("gsq", [T, D], fp32)
        gsum, gneg, gvar = (at(n, [T, H], fp32) for n in ("gsum", "gneg", "gvar"))
        gsum2, geps, groot = (at(n, [T, H], fp32) for n in ("gsum2", "geps", "groot"))
        assert top[0] <= kT_at
        top[0] = kT_at
        rk, rv = pair("rk", [P, C, D]), pair("rv", [P, C, D])
        cosx, sinx = at("cosx", [P, 2, HALF], fp32), at("sinx", [P, 2, HALF], fp32)

        top[0] = shared_end
        h_act = at("h_act", [P, M, TOK], fp32)
        hid = pair("hid", [P, M, TOK])
        fw = pair("fw", [P, 2, BLK])
        silu, gated = at("silu", [P, 2, HALF], fp32), at("gated", [P, 2, HALF], fp32)

        def ps(name, n):
            return ctx.enter_context(nc.psum_tensor(name, [P, n], fp32))

        psS = [ps("psS0", 2 * KA), ps("psS1", 2 * KA)]
        psT = ps("psT", 2 * KA)
        psO = ps("psO", KA)
        psJ = ps("psJ", KA)
        ln_bank = [psO[:, :], psJ[:, :]]
        tx_bank = [psS[1][:, 0:KA], psS[1][:, KA:2 * KA]]
        bank4 = [t[:, i:i + KA] for i in (0, KA) for t in psS]
        bank4b = [psT[:, 0:KA], psT[:, KA:2 * KA], psO[:, :], psJ[:, :]]

        consts_in, conv_in, small_ready = sem("consts_in"), sem("conv_in"), sem("small_ready")
        raw_in = [sem("raw_in0"), sem("raw_in1")]
        w_hi, w_split = sem("w_hi"), sem("w_split")
        dve_chain, act_chain = sem("dve_chain"), sem("act_chain")
        ln_in, ln_y, ln_stat, ln_mv = sem("ln_in"), sem("ln_y"), sem("ln_stat"), sem("ln_mv")
        ln_eps, ln_rstd, ln_x = sem("ln_eps"), sem("ln_rstd"), sem("ln_x")
        tx_mm, tx_hi, tx_lo = sem("tx_mm"), sem("tx_hi"), sem("tx_lo")
        conv_done = sem("conv_done")
        out_done = sem("out_done")
        ffn0_resid = sem("ffn0_resid")
        def sems(prefix, names):
            return namedtuple("Sems", names)(*[sem(prefix + n) for n in names.split()])

        A = [sems(f"att{L}_", "ctx_in0 ctx_in1 ctx_hi ctx_split k_mm k_hi k_lo v_mm v_hi v_lo q_mm q_done qs_hi qs_done "
                              "s_mm maxed exped t_mm pt_hi pt_lo pv_mm o_copied rinv_done rt_mm rt_copied rb_mm "
                              "o_scaled o_biased o_hi o_lo resid_done mask_in mask_done pad_done") for L in range(2)]
        F = sems("ffn0_", "p_mm p_hi p_lo h_mm h_act h_hi h_lo acc_mm q_hi q_lo")
        R = sems("ret_", "tables_in q_mm q_raw rot_mm cos sin rope zero kb_hi k_ready xb_hi x_ready q_blocks v_mm v_hi "
                         "v_lo s_mm decayed p_hi p_lo pv_mm g_sum g_mean g_dev g_sq g_sum2 g_eps g_root g_norm to_mm "
                         "o_affine o_hi o_lo")
        E = sems("ffn1_", "blk_used w_mm silu gated g_hi g_lo m_mm act conv_hi conv_lo")
        mx_raw, apart = sem("mx_raw"), sem("apart")

        def wait(eng, s, v):
            if isinstance(v, int) and v <= 0:
                return
            eng.wait_ge(s, v)

        def wait_apart(eng, s, v):
            wait(eng, s, v)
            if not isinstance(v, int):
                eng.sem_inc(apart, 1)

        def three(out, st, mv_, first, last, n=None):
            nc.tensor.matmul(out, st[0], mv_[0], start=first, stop=False)
            nc.tensor.matmul(out, st[0], mv_[1], start=False, stop=False)
            return nc.tensor.matmul(out, st[1], mv_[0], start=False, stop=last)

        def col(name, c):
            return cols[:, COL_AT[name] + c:COL_AT[name] + c + 1]

        def cols4(name, n):
            return cols[:, COL_AT[name]:COL_AT[name] + n]

        block = ctx.enter_context(nc.Block())

        @block.sync
        def _(sp):
            def blocks(name, k0, k):
                for i in range(k0, k0 + k):
                    n = BLOCKS[name] + i
                    wait(sp, w_split, n - 1)
                    sp.dma_start(raw[:, n % 2, :], d[name][i]).then_inc(raw_in[n % 2], 16)

            def context(a, b, cs):
                for c in cs:
                    wait(sp, a.ctx_split, 4 * b + c - 1)
                    sp.dma_start(ctx_raw[:, c % 2, :], d["ctxT"][c, :, bass.ds(b * KEYS, KEYS)])\
                      .then_inc((a.ctx_in0, a.ctx_in1)[c % 2], 16)

            def attention_loads(L):
                a = A[L]
                if L == 1:
                    with nc.sync.Fori(1, NB) as b:
                        context(a, b, range(C))
                        sp.wait_ge(a.mask_done, b)
                        sp.dma_start(mask_raw[:, :], d["mask"][bass.ds(b, 1), :].broadcast_to([T, KEYS]))\
                          .then_inc(a.mask_in, 16)
                else:
                    with nc.sync.Fori(1, NB) as b:
                        context(a, b, range(C))

            blocks("wk0", 0, 2)
            sp.dma_start(cols[:, :], d["cols"]).then_inc(conv_in, 16)
            sp.dma_start(kvec[:, :, :], d["kvec"]).then_inc(conv_in, 16)
            sp.dma_start(cin[:, :, :], d["xT"]).then_inc(conv_in, 16)
            context(A[0], 0, (0, 1))
            sp.dma_start(ident[:, :], d["ident"]).then_inc(consts_in, 16)
            sp.dma_start(sel[:, :, :], d["sel"]).then_inc(consts_in, 16)
            for i, n in enumerate(("bo", "b2", "bproj")):
                sp.dma_start(rows[:, i, :], d[n][:, :].broadcast_to([T, D])).then_inc(consts_in, 16)
            blocks("wv0", 0, 1)
            context(A[0], 0, (2,))
            blocks("wv0", 1, 1)
            context(A[0], 0, (3,))
            blocks("wq0", 0, 2)
            blocks("wo0", 0, 2)
            attention_loads(0)
            for n, k in (("u1", 1), ("v1", 2), ("u2", 2), ("v2", 1), ("rq", 2), ("rk", 2), ("rv", 2)):
                blocks(n, 0, k)
            sp.wait_ge(F.h_mm, 2 * M)
            sp.wait_ge(F.acc_mm, 2 * M)
            for t, n in ((ctab, "cos"), (stab, "sin"), (rotm, "rotm"), (decay, "decay")):
                sp.dma_start(t[:], d[n]).then_inc(R.tables_in, 16)
            for n in ("ro", "wk1", "wv1"):
                blocks(n, 0, 2)
            sp.wait_ge(ln_in, LN_RET + NB)
            context(A[1], 0, (0, 1))
            sp.dma_start(mask_raw[:, :], d["mask"][0:1, :].broadcast_to([T, KEYS])).then_inc(A[1].mask_in, 16)
            context(A[1], 0, (2, 3))
            blocks("wq1", 0, 2)
            blocks("wo1", 0, 2)
            attention_loads(1)
            with nc.sync.Fori(0, M // 2 + 2 * M + C) as i:
                for e in range(2):
                    sp.wait_ge(w_split, 2 * i + (BLOCKS["w12"] + e - 1))
                    sp.dma_start(raw[:, e, :], d["ffn"][bass.ds(2 * i + e, 1)].rearrange("a p n -> (a p) n"))\
                      .then_inc(raw_in[e], 16)

            for b in range(NB):
                sp.wait_ge(ln_x, LN_LAST + b + 1)
                sp.dma_start(d["out"][b], x_res[:, b, :]).then_inc(out_done, 16)
            sp.wait_ge(out_done, 16 * NB)

        @block.gpsimd
        def _(pool):
            def split(name, i, hi, lo):
                n = BLOCKS[name] + i
                w = hi.shape[-1] if len(hi.shape) == 2 else hi.shape[-1] * hi.shape[-2]
                src = raw[:, n % 2, 0:w]
                if len(hi.shape) == 3:
                    src = src.rearrange("p (a b) -> p a b", a=hi.shape[1])
                wait_apart(pool, raw_in[n % 2], 16 * (n // 2 + 1))
                nc.gpsimd.tensor_copy(hi, src).then_inc(w_hi, 1)
                wait_apart(pool, w_hi, n + 1)
                nc.gpsimd.tensor_tensor(lo, src, hi, ALU.subtract).then_inc(w_split, 1)

            def split512(name, i, w):
                split(name, i, w.hi[:, 2 * i:2 * i + 2, :], w.lo[:, 2 * i:2 * i + 2, :])

            def split_context(a, b, c):
                wait_apart(pool, (a.ctx_in0, a.ctx_in1)[c % 2], 16 * (2 * b + c // 2 + 1))
                if c == 0:
                    wait_apart(pool, a.k_mm, 2 * C * b)
                nc.gpsimd.tensor_copy(cT.hi[:, c, :], ctx_raw[:, c % 2, :]).then_inc(a.ctx_hi, 1)
                wait_apart(pool, a.ctx_hi, 4 * b + c + 1)
                nc.gpsimd.tensor_tensor(cT.lo[:, c, :], ctx_raw[:, c % 2, :], cT.hi[:, c, :], ALU.subtract)\
                  .then_inc(a.ctx_split, 1)

            def split_queries(a, b):
                src = q_all[:, :, bass.ds(b * T, T)]
                wait_apart(pool, a.s_mm, H * b)
                nc.gpsimd.tensor_copy(qs.hi[:, :, :], src).then_inc(a.qs_hi, 1)
                wait_apart(pool, a.qs_hi, b + 1)
                nc.gpsimd.tensor_tensor(qs.lo[:, :, :], src, qs.hi[:, :, :], ALU.subtract).then_inc(a.qs_done, 1)

            def mask_bias(a, b):
                wait_apart(pool, a.mask_in, 16 * (b + 1))
                wait_apart(pool, a.maxed, H * b)
                nc.gpsimd.tensor_scalar(maskb[:, :], mask_raw[:, :], 0.0, MASKED, ALU.is_equal, ALU.mult)\
                  .then_inc(a.mask_done, 1)

            def root(n, s):
                wait_apart(pool, ln_mv, n + 1)
                nc.gpsimd.tensor_scalar(veps[:, s, :], mv[:, s, 1:2], EPS, None, ALU.add).then_inc(ln_eps, 1)
                wait_apart(pool, ln_eps, n + 1)
                nc.gpsimd.tensor_tensor(rstd[:, s, :], veps[:, s, :], mhalf[0:T, 0:1], ALU.pow).then_inc(ln_rstd, 1)

            def add_bias(row, b, s, n, done):
                wait_apart(pool, ln_y, n - (0 if s is None else 1))
                s = s or 0
                nc.gpsimd.tensor_tensor(resid[:, s, :], x_res[:, b, :],
                                        rows[:, row, :], ALU.add).then_inc(done, 1)

            def attention(L, row, base):
                a = A[L]

                def batch(b, last):
                    if not last:
                        for c in range(C):
                            split_context(a, b + 1, c)
                        split_queries(a, b + 1)
                        if L == 1:
                            mask_bias(a, b + 1)
                    add_bias(row, b, None, base + b, a.resid_done)
                    root(base + b, 0)

                batch(0, False)
                with nc.gpsimd.Fori(1, NB - 1) as b:
                    batch(b, False)
                batch(NB - 1, True)

            nc.gpsimd.memset(mhalf[:, :], -0.5).then_inc(small_ready, 1)
            for i in range(2):
                split512("wk0", i, wk)
            split_context(A[0], 0, 0)
            split_context(A[0], 0, 1)
            split512("wv0", 0, wv)
            split_context(A[0], 0, 2)
            split512("wv0", 1, wv)
            split_context(A[0], 0, 3)
            for i in range(2):
                split512("wq0", i, wqo)
            wait_apart(pool, small_ready, 1)
            for b in range(NB):
                root(LN_CONV + b, b % 2)
            wait_apart(pool, A[0].q_mm, 2 * C)
            for i in range(2):
                split512("wo0", i, wqo)
            wait_apart(pool, A[0].q_done, 2 * C)
            nc.gpsimd.memset(p[:, :, KEYS:PK], 0.0).then_inc(A[0].pad_done, 1)
            nc.gpsimd.memset(rinv[:, H:P], 0.0).then_inc(A[0].pad_done, 1)
            split_queries(A[0], 0)
            attention(0, 0, LN_ATT0)

            wait_apart(pool, A[0].v_mm, NKC * NB)
            wait_apart(pool, A[0].k_mm, 2 * C * NB)
            split("u1", 0, u1.hi[:, :, :], u1.lo[:, :, :])
            for i in range(2):
                sl = slice(BLK * i, BLK * (i + 1))
                split("v1", i, v1.hi[:, sl], v1.lo[:, sl])
            for i in range(2):
                sl = slice(M // 2 * i, M // 2 * (i + 1))
                split("u2", i, u2.hi[:, sl, :], u2.lo[:, sl, :])
            split("v2", 0, v2.hi[:, :], v2.lo[:, :])
            wait_apart(pool, ln_in, LN_ATT0 + NB)
            for i in range(2):
                split512("rq", i, rqo)
            wait_apart(pool, ln_x, LN_ATT0 + NB)
            for n, w in (("rk", rk), ("rv", rv)):
                for i in range(2):
                    split512(n, i, w)
            for u in range(2 * M):
                wait_apart(pool, F.h_act, u + 1)
                wait_apart(pool, F.acc_mm, u - 3)
                nc.gpsimd.tensor_copy(f_g.hi[:, u % 4, :], f_act[:, u % 4, :]).then_inc(F.h_hi, 1)
            for b in range(NB):
                add_bias(1, b, b % 2, LN_FFN0 + b, ffn0_resid)
                root(LN_FFN0 + b, b % 2)

            wait_apart(pool, F.q_lo, 2)
            nc.gpsimd.memset(qbd.hi[:].bitcast(fp32), 0.0).then_inc(R.zero, 1)
            nc.gpsimd.memset(qbd.lo[:].bitcast(fp32), 0.0).then_inc(R.zero, 1)
            wait_apart(pool, R.tables_in, 64)

            def rope_sum(u):
                m, h = u // 2 % C, u % 2
                wait_apart(pool, R.sin, u + 1)
                wait_apart(pool, R.cos, u + 1)
                nc.gpsimd.tensor_tensor(qk[u // (2 * C)][:, m, h * HALF:(h + 1) * HALF], cosx[:, u % 2, :],
                                        sinx[:, u % 2, :], ALU.add).then_inc(R.rope, 1)

            for u in range(R_UNITS):
                m, h = u // 2 % C, u % 2
                wait_apart(pool, R.q_raw, u + 1)
                wait_apart(pool, R.rope, u - 1)
                nc.gpsimd.tensor_tensor(cosx[:, u % 2, :].rearrange("p (b t) -> p b t", t=T),
                                        qk[u // (2 * C)][:, m, h * HALF:(h + 1) * HALF]
                                        .rearrange("p (b t) -> p b t", t=T),
                                        ctab[:, :].unsqueeze(1).to_broadcast([P, NB // 2, T]), ALU.mult)\
                  .then_inc(R.cos, 1)
                if u >= 1:
                    rope_sum(u - 1)
            rope_sum(R_UNITS - 1)
            wait_apart(pool, R.q_mm, 2 * C)
            for i in range(2):
                split512("ro", i, rqo)

            def batch_operands(b):
                ts = bass.ds(b * T, T)
                wait_apart(pool, R.rope, R_UNITS)
                wait_apart(pool, R.s_mm, C * b)
                nc.gpsimd.tensor_copy(kb.hi[:, :, :], qk[1][:, :, ts]).then_inc(R.kb_hi, 1)
                wait_apart(pool, R.v_mm, b)
                nc.gpsimd.tensor_copy(xb.hi[:, :, :], xT.hi[:, :, ts]).then_inc(R.xb_hi, 1)
                nc.gpsimd.tensor_copy(xb.lo[:, :, :], xT.lo[:, :, ts]).then_inc(R.x_ready, 1)
                wait_apart(pool, R.kb_hi, b + 1)
                nc.gpsimd.tensor_tensor(kb.lo[:, :, :], qk[1][:, :, ts], kb.hi[:, :, :], ALU.subtract)\
                  .then_inc(R.k_ready, 1)

            def retention_pool(b, front, back):
                if back:
                    wait_apart(pool, R.g_dev, b)
                    nc.gpsimd.tensor_tensor(gsq[:, :], gd[:, :], gd[:, :], ALU.mult).then_inc(R.g_sq, 1)

                def p_hi(g):
                    wait_apart(pool, R.decayed, C * b + g + 1)
                    wait_apart(pool, R.pv_mm, C * b + g - 1)
                    nc.gpsimd.tensor_copy(pb.hi[:, g % 2, :], p_raw[:, g % 2, :]).then_inc(R.p_hi, 1)

                if front:
                    p_hi(0)
                if back:
                    wait_apart(pool, R.g_sum2, b)
                    nc.gpsimd.tensor_scalar(geps[:, :], gsum2[:, :], 1.0 / HD, EPS, ALU.mult, ALU.add)\
                      .then_inc(R.g_eps, 1)
                    wait_apart(pool, R.g_eps, b)
                    nc.gpsimd.tensor_tensor(groot[:, :], geps[:, :], mhalf[0:T, :], ALU.pow).then_inc(R.g_root, 1)
                if front:
                    p_hi(1)
                    if not (isinstance(b, int) and b == NB - 1):
                        batch_operands(b + 1)
                    p_hi(2)
                    p_hi(3)
                if back:
                    root(LN_RET + b - 1, 0)

            batch_operands(0)
            retention_pool(0, True, False)
            with nc.gpsimd.Fori(1, NB - 1) as b:
                retention_pool(b, True, True)
            retention_pool(NB - 1, True, True)
            retention_pool(NB, False, True)

            wait_apart(pool, ln_in, LN_RET + NB)
            for i in range(2):
                split512("wk1", i, wk)
            for i in range(2):
                split512("wv1", i, wv)
            for c in range(C):
                split_context(A[1], 0, c)
            for i in range(2):
                split512("wq1", i, wqo)
            mask_bias(A[1], 0)
            wait_apart(pool, A[1].q_mm, 2 * C)
            for i in range(2):
                split512("wo1", i, wqo)
            nc.gpsimd.memset(p[:, :, KEYS:PK], 0.0).then_inc(A[1].pad_done, 1)
            nc.gpsimd.memset(rinv[:, H:P], 0.0).then_inc(A[1].pad_done, 1)
            wait_apart(pool, A[1].q_done, 2 * C)
            split_queries(A[1], 0)
            attention(1, 2, LN_ATT1)

            def ffn_split(i, e):
                wait_apart(pool, raw_in[e], 16 * i + 16 * (BLOCKS["w12"] // 2 + 1))
                nc.gpsimd.tensor_copy(fw.hi[:, e, :], raw[:, e, :]).then_inc(w_hi, 1)
                wait_apart(pool, w_hi, 2 * i + (BLOCKS["w12"] + e + 1))
                nc.gpsimd.tensor_tensor(fw.lo[:, e, :], raw[:, e, :], fw.hi[:, e, :], ALU.subtract)\
                  .then_inc(w_split, 1)

            def split_gate(i, e):
                wait_apart(pool, E.w_mm, 4 * i + (2 * e - 2))
                ffn_split(i, e)

            def split_wide(m):
                if isinstance(m, int) and m == 0:
                    wait_apart(pool, E.w_mm, 2 * M)
                    ffn_split(M // 2, 0)
                    ffn_split(M // 2, 1)
                else:
                    wait_apart(pool, E.blk_used, m)
                    ffn_split(m + M // 2, 0)
                    wait_apart(pool, E.m_mm, 2 * m)
                    ffn_split(m + M // 2, 1)

            def gate_hi(i, q):
                wait_apart(pool, E.gated, 4 * i + q + 1)
                nc.gpsimd.tensor_copy(hid.hi[:, 2 * i + q // 2, (q % 2) * HALF:(q % 2 + 1) * HALF],
                                      gated[:, q % 2, :]).then_inc(E.g_hi, 1)

            wait_apart(pool, tx_lo, LN_ATT1 + NB)
            split_gate(0, 0)
            split_gate(0, 1)
            with nc.gpsimd.Fori(1, M // 2) as i:
                for e in range(2):
                    gate_hi(i - 1, 2 * e)
                    gate_hi(i - 1, 2 * e + 1)
                    split_gate(i, e)
            for q in range(4):
                gate_hi(M // 2 - 1, q)
            for stage, steps in enumerate((M, M, C)):
                split_wide(stage * M)
                if stage:
                    for k in range(M):
                        wait_apart(pool, E.conv_hi, (stage - 1) * M + k + 1)
                        nc.gpsimd.tensor_tensor(hid.lo[:, k, :], h_act[:, k, :], hid.hi[:, k, :], ALU.subtract)\
                          .then_inc(E.conv_lo, 1)
                with nc.gpsimd.Fori(stage * M + 1, stage * M + steps) as m:
                    split_wide(m)
            for b in range(NB):
                root(LN_FFN1 + b, b % 2)

        @block.scalar
        def _(act):
            def transposed_hi(n, b):
                act.wait_ge(tx_mm, n + 1)
                nc.scalar.activation(xT.hi[:, :, b * T:(b + 1) * T],
                                     tx_bank[n % 2][:, 0:C * T].rearrange("p (c t) -> p c t", c=C), ACT.Copy)\
                  .then_inc(tx_hi, 1)

            def queries(a, bias):
                for i in range(2 * C):
                    m, h = i // 2, i % 2
                    act.wait_ge(a.q_mm, i + 1)
                    src = psS[i % 2][:, (i // 2 % 2) * KA:(i // 2 % 2) * KA + HALF]
                    dst = q_all[:, m, h * HALF:(h + 1) * HALF]
                    if bias:
                        nc.scalar.activation(dst, src, ACT.Identity, bias=att_bq[:, m:m + 1], scale=SCALE)\
                          .then_inc(a.q_done, 1)
                    else:
                        nc.scalar.activation(dst, src, ACT.Copy, scale=SCALE).then_inc(a.q_done, 1)

            def keys_hi(L, b, g, i):
                a = A[L]
                k0, kn = PIECES[i]
                act.wait_ge(a.k_mm, 8 * b + 2 * g + i + 1)
                dst = kT.hi[:, g % 2, k0:k0 + kn]
                if L == 0:
                    nc.scalar.activation(dst, psJ[:, 0:kn], ACT.Identity, bias=col("bk", g)).then_inc(a.k_hi, 1)
                else:
                    nc.scalar.activation(dst, psJ[:, 0:kn], ACT.Copy).then_inc(a.k_hi, 1)

            def values_hi(a, b, j):
                act.wait_ge(a.v_mm, NKC * b + j + 1)
                if j == 0:
                    wait(act, a.pv_mm, H // 2 * b)
                n = key_rows(j)
                nc.scalar.activation(vv.hi[0:n, j, :], psS[j % 2][0:n, 0:D], ACT.Copy).then_inc(a.v_hi, 1)

            def attention(L):
                a = A[L]

                def exps(b, h):
                    act.wait_ge(a.maxed, H * b + h + 1)
                    src = psS[h % 2][0:T, 0:KEYS] if L == 0 else p[:, h % 2, 0:KEYS]
                    nc.scalar.activation(p[:, h % 2, 0:KEYS], src, ACT.Exp, bias=nmax[:, h % 2:h % 2 + 1],
                                         accum_out=rsum[:, h:h + 1]).then_inc(a.exped, 1)

                def probs_hi(b, h):
                    act.wait_ge(a.t_mm, H * b + h + 1)
                    pr = h // 2
                    if h % 2 == 0:
                        wait(act, a.pv_mm, H // 2 * b + pr - 1)
                    for i in range(2):
                        nc.scalar.activation(
                            pT.hi[:, pr % 2, HK * i:HK * i + HK, (h % 2) * T:(h % 2 + 1) * T],
                            psT[:, KA * i:KA * i + HK * T].rearrange("p (k t) -> p k t", k=HK), ACT.Copy)\
                          .then_inc(a.pt_hi, 1)

                def batch(b, last):
                    for t in range(H + 1):
                        if t >= 1:
                            probs_hi(b, t - 1)
                        if t < H:
                            exps(b, t)
                        g, i = t // 4 + 1, t % 4
                        if i < 2 and g < C and t < 12:
                            keys_hi(L, b, g, i)
                        if t in (14, 15) and not last:
                            keys_hi(L, b + 1, 0, t - 14)
                    if not last:
                        values_hi(a, b + 1, 0)
                        values_hi(a, b + 1, 1)
                    act.wait_ge(a.rt_mm, b + 1)
                    nc.scalar.activation(rT[:, :], psT[0:H, 0:T], ACT.Copy).then_inc(a.rt_copied, 1)
                    if not last:
                        values_hi(a, b + 1, 2)
                        values_hi(a, b + 1, 3)
                    act.wait_ge(a.o_biased if L == 0 else a.o_scaled, b + 1)
                    nc.scalar.activation(oT.hi[:, :, :], oraw[:, :, :], ACT.Copy).then_inc(a.o_hi, 1)
                    if not last:
                        values_hi(a, b + 1, 4)
                        values_hi(a, b + 1, 5)

                if L == 0:
                    act.wait_ge(A[0].pad_done, 2)
                batch(0, False)
                with nc.scalar.Fori(1, NB - 1) as b:
                    batch(b, False)
                batch(NB - 1, True)

            act.wait_ge(conv_in, 48)
            nc.scalar.activation(e1[:, :], cols4("lmlg", C), ACT.Exp).then_inc(act_chain, 1)
            act.wait_ge(dve_chain, CH_DEC)
            nc.scalar.activation(dec[:, :, :], dec[:, :, :], ACT.Exp, scale=-1.0).then_inc(act_chain, 1)
            act.wait_ge(dve_chain, CH_ANG)
            nc.scalar.activation(ang[:, :, :], ang[:, :, :], ACT.Sin).then_inc(act_chain, 1)
            for i in range(2):
                keys_hi(0, 0, 0, i)
            for j in range(NKC):
                values_hi(A[0], 0, j)
            for b in range(NB):
                transposed_hi(LN_CONV + b, b)
            act.wait_ge(tx_lo, NB)
            nc.scalar.activation(att_bq[:, :], cols4("bq", C), ACT.Copy, scale=SCALE).then_inc(act_chain, 1)
            act.wait_ge(act_chain, 4)
            queries(A[0], True)
            attention(0)
            for b in range(NB):
                transposed_hi(LN_ATT0 + b, b)

            for h in range(2):
                act.wait_ge(F.p_mm, h + 1)
                nc.scalar.activation(f_p.hi[:, h * HALF:(h + 1) * HALF], bank4[2 * h][:, 0:HALF], ACT.Copy)\
                  .then_inc(F.p_hi, 1)
            for u in range(2 * M):
                act.wait_ge(F.h_mm, u + 1)
                wait(act, F.h_lo, u - 3)
                nc.scalar.activation(f_act[:, u % 4, :], bank4b[u % 4][:, 0:HALF], ACT.Gelu_apprx_tanh,
                                     bias=col("b1", u // 2)).then_inc(F.h_act, 1)
            for h in range(2):
                act.wait_ge(F.acc_mm, 2 * M - 1 + h)
                nc.scalar.activation(f_q.hi[:, h * HALF:(h + 1) * HALF], bank4[2 * h][:, 0:HALF], ACT.Copy)\
                  .then_inc(F.q_hi, 1)
            for b in range(NB):
                transposed_hi(LN_FFN0 + b, b)

            for u in range(R_UNITS):
                m, h = u // 2 % C, u % 2
                act.wait_ge(R.q_mm, u + 1)
                nc.scalar.activation(qk[u // (2 * C)][:, m, h * HALF:(h + 1) * HALF], bank4[u % 4][:, 0:HALF],
                                     ACT.Copy).then_inc(R.q_raw, 1)

            def retention_act(b, front, back):
                if front:
                    act.wait_ge(R.v_mm, b + 1)
                    wait(act, R.pv_mm, C * b)
                    nc.scalar.activation(vb.hi[:, :], psT[0:T, 0:D], ACT.Copy).then_inc(R.v_hi, 1)
                if back:
                    act.wait_ge(R.to_mm, b)
                    wait(act, R.o_lo, b - 1)
                    for c in range(C):
                        last = nc.scalar.activation(r_o[:, c, :], psJ[:, c * T:(c + 1) * T], ACT.Identity,
                                                    bias=col("gnb", c), scale=col("gnw", c))
                    last.then_inc(R.o_affine, 1)
                    act.wait_ge(R.o_affine, b)
                    nc.scalar.activation(r_oT.hi[:, :, :], r_o[:, :, :], ACT.Copy).then_inc(R.o_hi, 1)

            retention_act(0, True, False)
            with nc.scalar.Fori(1, NB) as b:
                retention_act(b, True, True)
            retention_act(NB, False, True)
            for b in range(NB):
                transposed_hi(LN_RET + b, b)

            for i in range(2):
                keys_hi(1, 0, 0, i)
            for j in range(NKC):
                values_hi(A[1], 0, j)
            queries(A[1], False)
            attention(1)
            for b in range(NB):
                transposed_hi(LN_ATT1 + b, b)

            def silus(i):
                for q in range(4):
                    act.wait_ge(E.w_mm, 4 * i + q + 1)
                    wait_apart(act, E.gated, 4 * i + (q - 1))
                    nc.scalar.activation(silu[:, q % 2, :], bank4[q][:, 0:HALF], ACT.Silu,
                                         scale=cols[:, bass.ds(2 * i + (COL_AT["w1s"] + q // 2), 1)])\
                      .then_inc(E.silu, 1)

            silus(0)
            with nc.scalar.Fori(1, M // 2) as i:
                silus(i)
            for stage, (name, steps, func) in enumerate((("h1s", M // 2, ACT.Gelu), ("h2s", M // 2, ACT.Gelu),
                                                         ("w3s", C // 2, ACT.Copy))):
                with nc.scalar.Fori(0, steps) as i:
                    for q in range(4):
                        wait_apart(act, E.m_mm, 4 * i + (2 * M * stage + q + 1))
                        if stage:
                            act.wait_ge(E.conv_lo, M * stage)
                        nc.scalar.activation(h_act[:, 2 * i + q // 2, (q % 2) * HALF:(q % 2 + 1) * HALF],
                                             bank4[q][:, 0:HALF], func,
                                             scale=cols[:, bass.ds(2 * i + (COL_AT[name] + q // 2), 1)])\
                          .then_inc(E.act, 1)

        @block.vector
        def _(dve):
            link = [0]

            def chain(ins):
                link[0] += 1
                ins.then_inc(dve_chain, 1)
                dve.wait_ge(dve_chain, link[0])

            def norm_stats(n, s, src):
                nc.vector.bn_stats(stats[:, s, :], src).then_inc(ln_stat, 1)
                wait_apart(dve, ln_stat, n + 1)
                nc.vector.bn_aggr(mv[:, s, :], stats[:, s, :]).then_inc(ln_mv, 1)

            def norm_apply(n, s, src, b):
                dve.wait_ge(ln_rstd, n + 1)
                nc.vector.tensor_scalar(x_res[:, b, :], src,
                                        mv[:, s, 0:1], rstd[:, s, :], ALU.subtract, ALU.mult).then_inc(ln_x, 1)

            def transposed_lo(n, b):
                dve.wait_ge(tx_hi, n + 1)
                sl = slice(b * T, (b + 1) * T)
                nc.vector.tensor_tensor(xT.lo[:, :, sl],
                                        tx_bank[n % 2][:, 0:C * T].rearrange("p (c t) -> p c t", c=C),
                                        xT.hi[:, :, sl], ALU.subtract).then_inc(tx_lo, 1)

            def keys_lo(L, b, g, i):
                a = A[L]
                k0, kn = PIECES[i]
                dve.wait_ge(a.k_hi, 8 * b + 2 * g + i + 1)
                hi, lo = kT.hi[:, g % 2, k0:k0 + kn], kT.lo[:, g % 2, k0:k0 + kn]
                if L == 0:
                    nc.vector.scalar_tensor_tensor(lo, psJ[:, 0:kn], col("bk", g), hi, ALU.add, ALU.subtract)\
                      .then_inc(a.k_lo, 1)
                else:
                    nc.vector.tensor_tensor(lo, psJ[:, 0:kn], hi, ALU.subtract).then_inc(a.k_lo, 1)

            def values_lo(a, b, j):
                dve.wait_ge(a.v_hi, NKC * b + j + 1)
                n = key_rows(j)
                nc.vector.tensor_tensor(vv.lo[0:n, j, :], psS[j % 2][0:n, 0:D], vv.hi[0:n, j, :], ALU.subtract)\
                  .then_inc(a.v_lo, 1)

            def attention(L, base):
                a = A[L]

                def head_max(b, h):
                    wait_apart(dve, a.s_mm, H * b + h + 1)
                    m = nmax[:, h % 2:h % 2 + 1]
                    if L == 0:
                        nc.vector.tensor_reduce(m, psS[h % 2][0:T, 0:KEYS], AX.X, ALU.max, negate=True)\
                          .then_inc(a.maxed, 1)
                    else:
                        if h == 0:
                            wait_apart(dve, a.mask_done, b + 1)
                        nc.vector.tensor_tensor_reduce(out=p[:, h % 2, 0:KEYS], in0=psS[h % 2][0:T, 0:KEYS],
                                                       in1=maskb[:, :], scale=1.0, scalar=LOWEST, op0=ALU.add,
                                                       op1=ALU.max, accum_out=pmax[:, h % 2:h % 2 + 1])\
                          .then_inc(mx_raw, 1)
                        dve.wait_ge(mx_raw, H * b + h + 1)
                        nc.vector.tensor_scalar(m, pmax[:, h % 2:h % 2 + 1], -1.0, None, ALU.mult)\
                          .then_inc(a.maxed, 1)

                def probs_lo(b, h):
                    pr = h // 2
                    for i in range(2):
                        dve.wait_ge(a.pt_hi, 2 * (H * b + h) + i + 1)
                        sl = (slice(None), pr % 2, slice(HK * i, HK * i + HK), slice((h % 2) * T, (h % 2 + 1) * T))
                        nc.vector.tensor_tensor(pT.lo[sl],
                                                psT[:, KA * i:KA * i + HK * T].rearrange("p (k t) -> p k t", k=HK),
                                                pT.hi[sl], ALU.subtract).then_inc(a.pt_lo, 1)

                def heads_out(b, pr):
                    dve.wait_ge(a.pv_mm, H // 2 * b + pr + 1)
                    if pr == 0:
                        wait(dve, a.o_lo, b)
                    for e in range(2):
                        g, j = divmod(2 * pr + e, G)
                        cp = nc.vector.tensor_copy(oraw[HD * j:HD * (j + 1), g, :],
                                                   psO[HD * e:HD * (e + 1), T * e:T * (e + 1)])
                    cp.then_inc(a.o_copied, 1)

                def batch(b, last):
                    for t in range(H + 1):
                        if t < H:
                            head_max(b, t)
                        if t >= 1:
                            probs_lo(b, t - 1)
                        g, i = t // 4 + 1, t % 4
                        if i < 2 and g < C and t < 12:
                            keys_lo(L, b, g, i)
                        if t in (14, 15) and not last:
                            keys_lo(L, b + 1, 0, t - 14)
                        if t >= 3 and t % 2 == 1:
                            heads_out(b, (t - 3) // 2)
                    dve.wait_ge(a.exped, H * (b + 1))
                    nc.vector.reciprocal(rinv[:, 0:H], rsum[:, :]).then_inc(a.rinv_done, 1)
                    if not last:
                        values_lo(a, b + 1, 0)
                        values_lo(a, b + 1, 1)
                    heads_out(b, H // 2 - 1)
                    if not last:
                        values_lo(a, b + 1, 2)
                    dve.wait_ge(a.rb_mm, b + 1)
                    dve.wait_ge(a.o_copied, H // 2 * (b + 1))
                    nc.vector.tensor_tensor(oraw[:, :, :], psT[:, 0:C * T].rearrange("p (c t) -> p c t", c=C),
                                            oraw[:, :, :], ALU.mult).then_inc(a.o_scaled, 1)
                    if L == 0:
                        dve.wait_ge(a.o_scaled, b + 1)
                        nc.vector.tensor_tensor(oraw[:, :, :], oraw[:, :, :],
                                                cols4("bv", C).unsqueeze(2).to_broadcast([P, C, T]), ALU.add)\
                          .then_inc(a.o_biased, 1)
                    if not last:
                        values_lo(a, b + 1, 3)
                    dve.wait_ge(a.o_hi, b + 1)
                    nc.vector.tensor_tensor(oT.lo[:, :, :], oraw[:, :, :], oT.hi[:, :, :], ALU.subtract)\
                      .then_inc(a.o_lo, 1)
                    if not last:
                        values_lo(a, b + 1, 4)
                    dve.wait_ge(a.resid_done, b + 1)
                    dve.wait_ge(ln_in, base + b + 1)
                    dve.wait_ge(ln_x, base + b)
                    nc.vector.tensor_tensor(y[:, 0, :], psT[0:T, KA:KA + D], resid[:, 0, :], ALU.add)\
                      .then_inc(ln_y, 1)
                    if not last:
                        values_lo(a, b + 1, 5)
                    dve.wait_ge(ln_y, base + b + 1)
                    norm_stats(base + b, 0, y[:, 0, :])
                    norm_apply(base + b, 0, y[:, 0, :], b)

                batch(0, False)
                with nc.vector.Fori(1, NB - 1) as b:
                    batch(b, False)
                batch(NB - 1, True)

            TWO_PI = (6.28125, 1.9350051879882812e-03, 3.0199159819567e-07)
            MAGIC = 1.5 * 2.0 ** 23

            def reduce_angle(x, n):
                chain(nc.vector.tensor_scalar(n, x, 1.0 / 6.283185307179586, MAGIC, ALU.mult, ALU.add))
                chain(nc.vector.tensor_scalar(n, n, -MAGIC, None, ALU.add))
                for part in TWO_PI:
                    chain(nc.vector.scalar_tensor_tensor(x, n, -part, x, ALU.mult, ALU.add))

            dve.wait_ge(conv_in, 48)
            chain(nc.vector.tensor_copy(th[:, :], cols4("theta", C)))
            reduce_angle(th[:, :], thn[:, :])
            dve.wait_ge(act_chain, 1)
            chain(nc.vector.tensor_tensor(dec[:, :, :], kvec[:, :, :],
                                          e1[:, :].unsqueeze(2).to_broadcast([P, C, TAPS]), ALU.mult))
            assert link[0] == CH_DEC
            chain(nc.vector.tensor_tensor(ang[:, :, :], kvec[:, :, :],
                                          th[:, :].unsqueeze(2).to_broadcast([P, C, TAPS]), ALU.mult))
            reduce_angle(ang[:, :, :], turns[:, :, :])
            chain(nc.vector.tensor_scalar(turns[:, :, :], ang[:, :, :], -1.0, None, ALU.mult))
            chain(nc.vector.tensor_tensor(ang[:, :, :], ang[:, :, :], turns[:, :, :], ALU.max))
            chain(nc.vector.tensor_scalar(ang[:, :, :], ang[:, :, :], -1.0, 1.5707963267948966, ALU.mult, ALU.add))
            assert link[0] == CH_ANG
            dve.wait_ge(act_chain, 3)
            chain(nc.vector.tensor_tensor(taps[:, :, :], dec[:, :, :], ang[:, :, :], ALU.mult))
            chain(nc.vector.tensor_tensor(past[:, :, :], taps[:, :, 1:TAPS],
                                          cols4("init", C).unsqueeze(2).to_broadcast([P, C, NB]), ALU.mult))
            for c in range(C):
                nc.vector.tensor_tensor(acc[:, c, :].rearrange("p (n t) -> p n t", n=NB),
                                        cin[:, c, :].rearrange("p (n t) -> p n t", n=NB),
                                        past[:, c, :].unsqueeze(2).to_broadcast([P, NB, T]), ALU.add)\
                  .then_inc(conv_done, 1)
            for k in range(1, NB):
                for c in range(C):
                    dve.wait_ge(conv_done, C * (k - 1) + c + 1)
                    nc.vector.scalar_tensor_tensor(acc[:, c, k * T:TOK], cin[:, c, 0:TOK - k * T], taps[:, c, k:k + 1],
                                                   acc[:, c, k * T:TOK], ALU.mult, ALU.add).then_inc(conv_done, 1)
            for c in range(C):
                dve.wait_ge(conv_done, C * (NB - 1) + c + 1)
                nc.vector.scalar_tensor_tensor(acc[:, c, :], acc[:, c, :], 1.0, cin[:, c, :], ALU.add, ALU.mult)\
                  .then_inc(conv_done, 1)
            for i in range(2):
                keys_lo(0, 0, 0, i)
            for j in range(NKC):
                values_lo(A[0], 0, j)
            for b in range(NB):
                dve.wait_ge(ln_in, LN_CONV + b + 1)
                wait(dve, ln_x, LN_CONV + b - 1)
                nc.vector.tensor_copy(y[:, b % 2, :], ln_bank[b % 2][0:T, :]).then_inc(ln_y, 1)
                dve.wait_ge(ln_y, LN_CONV + b + 1)
                norm_stats(LN_CONV + b, b % 2, y[:, b % 2, :])
                if b >= 1:
                    norm_apply(LN_CONV + b - 1, (b - 1) % 2, y[:, (b - 1) % 2, :], b - 1)
            norm_apply(LN_CONV + NB - 1, (NB - 1) % 2, y[:, (NB - 1) % 2, :], NB - 1)
            for b in range(NB):
                transposed_lo(LN_CONV + b, b)
            attention(0, LN_ATT0)
            for b in range(NB):
                transposed_lo(LN_ATT0 + b, b)

            def norm(n, b, s, src, other):
                dve.wait_ge(ln_in, n + 1)
                dve.wait_ge(ln_x, n - 1 if s is not None else n)
                s = s or 0
                nc.vector.tensor_tensor(y[:, s, :], src, other, ALU.add).then_inc(ln_y, 1)
                dve.wait_ge(ln_y, n + 1)
                norm_stats(n, s, y[:, s, :])

            def norms(base, bank, other, before, transposed=False):
                for b in range(NB):
                    before(b)
                    norm(base + b, b, b % 2, bank(b), other(b))
                    if b >= 1:
                        norm_apply(base + b - 1, (b - 1) % 2, y[:, (b - 1) % 2, :], b - 1)
                    if transposed and b >= 3:
                        transposed_lo(base + b - 3, b - 3)
                norm_apply(base + NB - 1, (NB - 1) % 2, y[:, (NB - 1) % 2, :], NB - 1)
                if transposed:
                    for b in range(NB - 3, NB):
                        transposed_lo(base + b, b)

            for h in range(2):
                dve.wait_ge(F.p_hi, h + 1)
                sl = slice(h * HALF, (h + 1) * HALF)
                nc.vector.tensor_tensor(f_p.lo[:, sl], bank4[2 * h][:, 0:HALF], f_p.hi[:, sl], ALU.subtract)\
                  .then_inc(F.p_lo, 1)
            for u in range(2 * M):
                dve.wait_ge(F.h_hi, u + 1)
                nc.vector.tensor_tensor(f_g.lo[:, u % 4, :], f_act[:, u % 4, :], f_g.hi[:, u % 4, :], ALU.subtract)\
                  .then_inc(F.h_lo, 1)
            for h in range(2):
                dve.wait_ge(F.q_hi, h + 1)
                sl = slice(h * HALF, (h + 1) * HALF)
                nc.vector.tensor_tensor(f_q.lo[:, sl], bank4[2 * h][:, 0:HALF], f_q.hi[:, sl], ALU.subtract)\
                  .then_inc(F.q_lo, 1)
            norms(LN_FFN0, lambda b: ln_bank[b % 2][0:T, :], lambda b: resid[:, b % 2, :],
                  lambda b: dve.wait_ge(ffn0_resid, b + 1), transposed=True)

            dve.wait_ge(R.tables_in, 64)
            for u in range(R_UNITS):
                dve.wait_ge(R.rot_mm, u + 1)
                wait(dve, R.rope, u - 1)
                nc.vector.tensor_tensor(sinx[:, u % 2, :].rearrange("p (b t) -> p b t", t=T),
                                        bank4b[u % 4][:, 0:HALF].rearrange("p (b t) -> p b t", t=T),
                                        stab[:, :].unsqueeze(1).to_broadcast([P, NB // 2, T]), ALU.mult)\
                  .then_inc(R.sin, 1)

            def query_blocks(b):
                wait(dve, R.s_mm, C * b)
                ts = bass.ds(b * T, T)
                for j in range(G):
                    r = slice(HD * j, HD * (j + 1))
                    last = nc.vector.tensor_copy(qbd.hi[r, :, j, :], qk[0][r, :, ts])
                last.then_inc(R.q_blocks, 1)
                dve.wait_ge(R.q_blocks, 2 * b + 1)
                for j in range(G):
                    r = slice(HD * j, HD * (j + 1))
                    last = nc.vector.tensor_tensor(qbd.lo[r, :, j, :], qk[0][r, :, ts], qbd.hi[r, :, j, :],
                                                   ALU.subtract)
                last.then_inc(R.q_blocks, 1)

            heads = lambda t: t.rearrange("t (h e) -> t h e", h=H)
            spread = lambda t: t[:, :].unsqueeze(2).to_broadcast([T, H, HD])

            def retention_dve(b, front, back):
                def decayed(g):
                    dve.wait_ge(R.s_mm, C * b + g + 1)
                    wait(dve, R.p_lo, C * b + g - 1)
                    nc.vector.tensor_tensor(p_raw[:, g % 2, :], bank4[g][0:T, 0:G * T],
                                            decay[:, G * g:G * (g + 1), :].rearrange("t h s -> t (h s)"), ALU.mult)\
                      .then_inc(R.decayed, 1)

                def p_lo(g):
                    dve.wait_ge(R.p_hi, C * b + g + 1)
                    nc.vector.tensor_tensor(pb.lo[:, g % 2, :], p_raw[:, g % 2, :], pb.hi[:, g % 2, :], ALU.subtract)\
                      .then_inc(R.p_lo, 1)

                if back:
                    dve.wait_ge(R.pv_mm, C * b)
                    nc.vector.tensor_reduce(gsum[:, :], heads(psO[0:T, 0:D]), AX.X, ALU.add).then_inc(R.g_sum, 1)
                    dve.wait_ge(R.g_sum, b)
                    nc.vector.tensor_scalar(gneg[:, :], gsum[:, :], -1.0 / HD, None, ALU.mult).then_inc(R.g_mean, 1)
                    dve.wait_ge(R.g_mean, b)
                    nc.vector.tensor_tensor(heads(gd[:, :]), heads(psO[0:T, 0:D]), spread(gneg), ALU.add)\
                      .then_inc(R.g_dev, 1)
                if front:
                    dve.wait_ge(R.v_hi, b + 1)
                    nc.vector.tensor_tensor(vb.lo[:, :], psT[0:T, 0:D], vb.hi[:, :], ALU.subtract).then_inc(R.v_lo, 1)
                    decayed(0)
                if back:
                    dve.wait_ge(R.g_sq, b)
                    nc.vector.tensor_reduce(gsum2[:, :], heads(gsq[:, :]), AX.X, ALU.add).then_inc(R.g_sum2, 1)
                if front:
                    decayed(1)
                    p_lo(0)
                if back:
                    dve.wait_ge(R.g_root, b)
                    nc.vector.tensor_tensor(heads(gd[:, :]), heads(gd[:, :]), spread(groot), ALU.mult)\
                      .then_inc(R.g_norm, 1)
                if front:
                    p_lo(1)
                if back:
                    dve.wait_ge(R.o_hi, b)
                    nc.vector.tensor_tensor(r_oT.lo[:, :, :], r_o[:, :, :], r_oT.hi[:, :, :], ALU.subtract)\
                      .then_inc(R.o_lo, 1)
                if front:
                    decayed(2)
                    decayed(3)
                    p_lo(2)
                    p_lo(3)
                    if not (isinstance(b, int) and b == NB - 1):
                        query_blocks(b + 1)
                if back:
                    n = LN_RET + b - 1
                    norm(n, b - 1, None, psT[0:T, KA:KA + D], x_res[:, b - 1, :])
                    norm_apply(n, 0, y[:, 0, :], b - 1)

            dve.wait_ge(R.rope, R_UNITS)
            dve.wait_ge(R.zero, 2)
            query_blocks(0)
            retention_dve(0, True, False)
            with nc.vector.Fori(1, NB - 1) as b:
                retention_dve(b, True, True)
            retention_dve(NB - 1, True, True)
            retention_dve(NB, False, True)
            for b in range(NB):
                transposed_lo(LN_RET + b, b)

            for i in range(2):
                keys_lo(1, 0, 0, i)
            for j in range(NKC):
                values_lo(A[1], 0, j)
            attention(1, LN_ATT1)
            for b in range(NB):
                transposed_lo(LN_ATT1 + b, b)

            def gate(i, q, first=False):
                dve.wait_ge(E.silu, 4 * i + q + 1)
                if not (first and q < 2):
                    dve.wait_ge(E.g_lo, 4 * i + q - 1)
                nc.vector.scalar_tensor_tensor(gated[:, q % 2, :], bank4b[q][:, 0:HALF],
                                               cols[:, bass.ds(2 * i + (COL_AT["w2s"] + q // 2), 1)],
                                               silu[:, q % 2, :], ALU.mult, ALU.mult).then_inc(E.gated, 1)

            def gate_lo(i, q):
                dve.wait_ge(E.g_hi, 4 * i + q + 1)
                sl = (slice(None), 2 * i + q // 2, slice((q % 2) * HALF, (q % 2 + 1) * HALF))
                nc.vector.tensor_tensor(hid.lo[sl], gated[:, q % 2, :], hid.hi[sl], ALU.subtract).then_inc(E.g_lo, 1)

            def gates(i, first=False):
                for q in range(4):
                    gate(i, q, first)
                    gate_lo(i, q)

            gates(0, True)
            with nc.vector.Fori(1, M // 2) as i:
                gates(i)
            for stage in range(2):
                for k in range(M):
                    if k == 0:
                        dve.wait_ge(E.m_mm, 2 * M * (stage + 1))
                    if k == M - 1:
                        dve.wait_ge(E.act, 2 * M * (stage + 1))
                    dve.wait_ge(E.act, 2 * M * stage + 2 * k + 2)
                    nc.vector.tensor_copy(hid.hi[:, k, :], h_act[:, k, :]).then_inc(E.conv_hi, 1)
            norms(LN_FFN1, lambda b: ln_bank[b % 2][0:T, :], lambda b: x_res[:, b, :], lambda b: None)

        @block.tensor
        def _(pe):
            def keys(a, b, g, i):
                k0, kn = PIECES[i]
                wait(pe, a.k_lo, 8 * b + 2 * g + i)
                for c in range(C):
                    sl = slice(P * g, P * (g + 1))
                    mm = three(psJ[:, 0:kn], (wk.hi[:, c, sl], wk.lo[:, c, sl]),
                               (cT.hi[:, c, k0:k0 + kn], cT.lo[:, c, k0:k0 + kn]), c == 0, c == C - 1)
                mm.then_inc(a.k_mm, 1)

            def values(a, b, j):
                if j < 2:
                    wait(pe, a.exped, H * b)
                else:
                    pe.wait_ge(a.v_lo, NKC * b + j - 1)
                n, k0 = key_rows(j), KC * j
                for c in range(C):
                    mm = three(psS[j % 2][0:n, 0:D], (cT.hi[:, c, k0:k0 + n], cT.lo[:, c, k0:k0 + n]),
                               (wv.hi[:, c, :], wv.lo[:, c, :]), c == 0, c == C - 1)
                mm.then_inc(a.v_mm, 1)

            def transpose_x(n, b):
                pe.wait_ge(ln_x, n + 1)
                wait(pe, tx_lo, n - 1)
                for c in range(C):
                    mm = nc.tensor.transpose(tx_bank[n % 2][:, c * T:(c + 1) * T], x_res[:, b, c * P:(c + 1) * P],
                                             ident[0:T, 0:T])
                mm.then_inc(tx_mm, 1)

            def queries(a, w):
                for i in range(2 * C):
                    m, h = i // 2, i % 2
                    wait(pe, a.q_done, i - 3)
                    out = psS[i % 2][:, (i // 2 % 2) * KA:(i // 2 % 2) * KA + HALF]
                    for c in range(C):
                        sl, tk = slice(P * m, P * (m + 1)), slice(h * HALF, (h + 1) * HALF)
                        mm = three(out, (w.hi[:, c, sl], w.lo[:, c, sl]), (xT.hi[:, c, tk], xT.lo[:, c, tk]),
                                   c == 0, c == C - 1)
                    mm.then_inc(a.q_mm, 1)

            def attention(L, base):
                a = A[L]

                def scores(b, h):
                    g, j = divmod(h, G)
                    if h == 0:
                        pe.wait_ge(a.qs_done, b + 1)
                    if j == 0:
                        pe.wait_ge(a.k_lo, 8 * b + 2 * g + 2)
                    if h < 2:
                        pe.wait_ge(a.v_lo, NKC * (b + 1))
                    else:
                        pe.wait_ge(a.exped, H * b + h - 1)
                    rows_ = slice(HD * j, HD * (j + 1))
                    for k0, kn in PIECES:
                        mm = three(psS[h % 2][0:T, k0:k0 + kn], (qs.hi[rows_, g, :], qs.lo[rows_, g, :]),
                                   (kT.hi[rows_, g % 2, k0:k0 + kn], kT.lo[rows_, g % 2, k0:k0 + kn]), True, True)
                    mm.then_inc(a.s_mm, 1)

                def transposes(b, h):
                    pe.wait_ge(a.exped, H * b + h + 1)
                    wait(pe, a.pt_lo, 2 * (H * b + h))
                    if h == 0:
                        wait(pe, ln_y, base + b)
                    for k in range(NKC):
                        mm = nc.tensor.transpose(psT[:, KA * (k // HK) + T * (k % HK):KA * (k // HK) + T * (k % HK) + T],
                                                 p[:, h % 2, KC * k:KC * (k + 1)], ident[0:T, 0:T])
                    mm.then_inc(a.t_mm, 1)

                def weighted(b, pr):
                    pe.wait_ge(a.pt_lo, 2 * (H * b + 2 * pr + 2))
                    wait(pe, a.o_copied, H // 2 * b + pr)
                    fs = slice(2 * HD * pr, 2 * HD * (pr + 1))
                    for k in range(NKC):
                        n = key_rows(k)
                        mm = three(psO[0:2 * HD, 0:2 * T], (vv.hi[0:n, k, fs], vv.lo[0:n, k, fs]),
                                   (pT.hi[0:n, pr % 2, k, :], pT.lo[0:n, pr % 2, k, :]), k == 0, k == NKC - 1)
                    mm.then_inc(a.pv_mm, 1)

                def batch(b, last):
                    for t in range(H + 1):
                        if t < H:
                            scores(b, t)
                        if t >= 1:
                            transposes(b, t - 1)
                        g, i = t // 4 + 1, t % 4
                        if i < 2 and g < C and t < 12:
                            keys(a, b, g, i)
                        if t in (14, 15) and not last:
                            if t == 14:
                                pe.wait_ge(a.ctx_split, C * (b + 2))
                            keys(a, b + 1, 0, t - 14)
                        if t >= 3 and t % 2 == 1:
                            weighted(b, (t - 3) // 2)
                    if not last:
                        values(a, b + 1, 0)
                        values(a, b + 1, 1)
                    weighted(b, H // 2 - 1)
                    pe.wait_ge(a.rinv_done, b + 1)
                    nc.tensor.transpose(psT[:, 0:T], rinv[:, :], ident[0:T, 0:T]).then_inc(a.rt_mm, 1)
                    if not last:
                        values(a, b + 1, 2)
                    pe.wait_ge(a.rt_copied, b + 1)
                    for g in range(C):
                        mm = nc.tensor.matmul(psT[:, g * T:(g + 1) * T], sel[:, g, :], rT[:, :], start=True, stop=True)
                    mm.then_inc(a.rb_mm, 1)
                    if not last:
                        values(a, b + 1, 3)
                        values(a, b + 1, 4)
                    pe.wait_ge(a.o_lo, b + 1)
                    for c in range(C):
                        mm = three(psT[0:T, KA:KA + D], (oT.hi[:, c, :], oT.lo[:, c, :]),
                                   (wqo.hi[:, c, :], wqo.lo[:, c, :]), c == 0, c == C - 1)
                    mm.then_inc(ln_in, 1)
                    if not last:
                        values(a, b + 1, 5)

                pe.wait_ge(w_split, BLOCKS[("wo0", "wo1")[L]] + 2)
                batch(0, False)
                with nc.tensor.Fori(1, NB - 1) as b:
                    batch(b, False)
                batch(NB - 1, True)
                for b in range(NB):
                    transpose_x(base + b, b)

            pe.wait_ge(w_split, 2)
            pe.wait_ge(A[0].ctx_split, C)
            for i in range(2):
                keys(A[0], 0, 0, i)
            pe.wait_ge(w_split, 4)
            for j in range(NKC):
                values(A[0], 0, j)
            pe.wait_ge(consts_in, 80)
            for b in range(NB):
                if b == 0:
                    pe.wait_ge(conv_done, C * (NB + 1))
                wait(pe, ln_y, LN_CONV + b - 1)
                if b == 1:
                    pe.wait_ge(A[0].k_lo, 2)
                for c in range(C):
                    mm = nc.tensor.transpose(ln_bank[b % 2][0:T, c * P:(c + 1) * P], acc[:, c, b * T:(b + 1) * T],
                                             ident[:, :])
                mm.then_inc(ln_in, 1)
            for b in range(NB):
                if b == 0:
                    pe.wait_ge(A[0].v_lo, NKC)
                transpose_x(LN_CONV + b, b)
            pe.wait_ge(tx_lo, NB)
            pe.wait_ge(w_split, BLOCKS["wq0"] + 2)
            queries(A[0], wqo)
            attention(0, LN_ATT0)

            pe.wait_ge(tx_lo, LN_ATT0 + NB)
            pe.wait_ge(w_split, BLOCKS["v2"] + 1)
            for h in range(2):
                tk = slice(h * HALF, (h + 1) * HALF)
                for c in range(C):
                    mm = three(bank4[2 * h][:, 0:HALF], (u1.hi[:, c, :], u1.lo[:, c, :]),
                               (xT.hi[:, c, tk], xT.lo[:, c, tk]), c == 0, c == C - 1)
                mm.then_inc(F.p_mm, 1)
            pe.wait_ge(F.p_lo, 2)
            for u in range(2 * M + 2):
                if u < 2 * M:
                    m, h = divmod(u, 2)
                    ms, tk = slice(P * m, P * (m + 1)), slice(h * HALF, (h + 1) * HALF)
                    wait(pe, F.h_act, u - 3)
                    three(bank4b[u % 4][:, 0:HALF], (v1.hi[:, ms], v1.lo[:, ms]), (f_p.hi[:, tk], f_p.lo[:, tk]),
                          True, True).then_inc(F.h_mm, 1)
                if u >= 2:
                    m, h = divmod(u - 2, 2)
                    pe.wait_ge(F.h_lo, u - 1)
                    three(bank4[2 * h][:, 0:HALF], (u2.hi[:, m, :], u2.lo[:, m, :]),
                          (f_g.hi[:, (u - 2) % 4, :], f_g.lo[:, (u - 2) % 4, :]), m == 0, m == M - 1)\
                        .then_inc(F.acc_mm, 1)
            pe.wait_ge(F.q_lo, 2)
            for b in range(NB + 2):
                if b < NB:
                    wait(pe, ln_y, LN_FFN0 + b - 1)
                    tk = slice(b * T, (b + 1) * T)
                    three(ln_bank[b % 2][0:T, :], (f_q.hi[:, tk], f_q.lo[:, tk]), (v2.hi[:, :], v2.lo[:, :]),
                          True, True).then_inc(ln_in, 1)
                if b >= 2:
                    transpose_x(LN_FFN0 + b - 2, b - 2)

            pe.wait_ge(tx_lo, LN_FFN0 + NB)
            pe.wait_ge(w_split, BLOCKS["rk"] + 2)
            pe.wait_ge(R.tables_in, 64)
            for u in range(R_UNITS + 1):
                if u < R_UNITS:
                    m, h = u // 2 % C, u % 2
                    w = (rqo, rk)[u // (2 * C)]
                    wait(pe, R.q_raw, u - 3)
                    for c in range(C):
                        sl, tk = slice(P * m, P * (m + 1)), slice(h * HALF, (h + 1) * HALF)
                        mm = three(bank4[u % 4][:, 0:HALF], (w.hi[:, c, sl], w.lo[:, c, sl]),
                                   (xT.hi[:, c, tk], xT.lo[:, c, tk]), c == 0, c == C - 1)
                    mm.then_inc(R.q_mm, 1)
                if u >= 1:
                    v = u - 1
                    m, h = v // 2 % C, v % 2
                    pe.wait_ge(R.q_raw, v + 1)
                    wait(pe, R.sin, v - 3)
                    nc.tensor.matmul(bank4b[v % 4][:, 0:HALF], rotm[:, :],
                                     qk[v // (2 * C)][:, m, h * HALF:(h + 1) * HALF], start=True, stop=True)\
                      .then_inc(R.rot_mm, 1)

            def retention_pe(b, front, back):
                if front:
                    pe.wait_ge(R.x_ready, b + 1)
                    wait(pe, R.v_lo, b)
                    for c in range(C):
                        mm = three(psT[0:T, 0:D], (xb.hi[:, c, :], xb.lo[:, c, :]), (rv.hi[:, c, :], rv.lo[:, c, :]),
                                   c == 0, c == C - 1)
                    mm.then_inc(R.v_mm, 1)
                    pe.wait_ge(R.k_ready, b + 1)
                    pe.wait_ge(R.q_blocks, 2 * b + 2)
                    for g in range(C):
                        wait(pe, R.decayed, C * b + g - C + 1)
                        three(bank4[g][0:T, 0:G * T], (kb.hi[:, g, :], kb.lo[:, g, :]),
                              (qbd.hi[:, g, :, :], qbd.lo[:, g, :, :]), True, True).then_inc(R.s_mm, 1)
                if back:
                    pe.wait_ge(R.g_norm, b)
                    for c in range(C):
                        mm = nc.tensor.transpose(psJ[:, c * T:(c + 1) * T], gd[:, c * P:(c + 1) * P], ident[0:T, 0:T])
                    mm.then_inc(R.to_mm, 1)
                    pe.wait_ge(R.o_lo, b)
                    wait(pe, ln_y, LN_RET + b - 1)
                    for c in range(C):
                        mm = three(psT[0:T, KA:KA + D], (r_oT.hi[:, c, :], r_oT.lo[:, c, :]),
                                   (rqo.hi[:, c, :], rqo.lo[:, c, :]), c == 0, c == C - 1)
                    mm.then_inc(ln_in, 1)
                if front:
                    for g in range(C):
                        pe.wait_ge(R.p_lo, C * b + g + 1)
                        if g == 0:
                            wait(pe, R.g_dev, b)
                            pe.wait_ge(R.v_lo, b + 1)
                        for j in range(G):
                            hs, ts = slice(HD * (G * g + j), HD * (G * g + j + 1)), slice(T * j, T * (j + 1))
                            mm = three(psO[0:T, hs], (pb.hi[:, g % 2, ts], pb.lo[:, g % 2, ts]),
                                       (vb.hi[:, hs], vb.lo[:, hs]), True, True)
                        mm.then_inc(R.pv_mm, 1)

            pe.wait_ge(w_split, BLOCKS["ro"] + 2)
            pe.wait_ge(R.sin, R_UNITS)
            retention_pe(0, True, False)
            with nc.tensor.Fori(1, NB) as b:
                retention_pe(b, True, True)
            retention_pe(NB, False, True)
            for b in range(NB):
                transpose_x(LN_RET + b, b)

            pe.wait_ge(tx_lo, LN_RET + NB)
            pe.wait_ge(w_split, BLOCKS["wk1"] + 2)
            pe.wait_ge(A[1].ctx_split, C)
            for i in range(2):
                keys(A[1], 0, 0, i)
            pe.wait_ge(w_split, BLOCKS["wv1"] + 2)
            for j in range(NKC):
                values(A[1], 0, j)
            pe.wait_ge(A[1].v_lo, NKC)
            pe.wait_ge(w_split, BLOCKS["wq1"] + 2)
            queries(A[1], wqo)
            attention(1, LN_ATT1)

            pe.wait_ge(tx_lo, LN_ATT1 + NB)

            def gate_units(i):
                for e in range(2):
                    pe.wait_ge(w_split, 2 * i + (BLOCKS["w12"] + e + 1))
                    for h in range(2):
                        q, tk = 2 * e + h, slice(h * HALF, (h + 1) * HALF)
                        if not isinstance(i, int):
                            pe.wait_ge(E.gated, 4 * i + q - 3)
                        for k, bank in ((0, bank4[q]), (C, bank4b[q])):
                            for c in range(C):
                                ws = slice(P * (k + c), P * (k + c + 1))
                                mm = three(bank[:, 0:HALF], (fw.hi[:, e, ws], fw.lo[:, e, ws]),
                                           (xT.hi[:, c, tk], xT.lo[:, c, tk]), c == 0, c == C - 1)
                        mm.then_inc(E.w_mm, 1)

            gate_units(0)
            with nc.tensor.Fori(1, M // 2) as i:
                gate_units(i)
            pe.wait_ge(E.g_lo, 2 * M)
            pe.wait_ge(E.gated, 2 * M)
            for stage, (name, steps) in enumerate((("h1", M // 2), ("h2", M // 2), ("w3", C // 2))):
                def step(i, stage=stage, name=name):
                    for o in range(2):
                        for e in range(2):
                            pe.wait_ge(w_split, 4 * i + (BLOCKS[name] + 2 * o + e + 1))
                            for h in range(2):
                                q, tk = 2 * o + h, slice(h * HALF, (h + 1) * HALF)
                                if e == 0 and (stage or not isinstance(i, int)):
                                    pe.wait_ge(E.act, 4 * i + (2 * M * stage + q - 3))
                                for k in range(M // 2):
                                    kk = M // 2 * e + k
                                    if stage and o == 0 and h == 0:
                                        pe.wait_ge(E.conv_lo, M * (stage - 1) + kk + 1)
                                    ws = slice(P * k, P * (k + 1))
                                    mm = three(bank4[q][:, 0:HALF], (fw.hi[:, e, ws], fw.lo[:, e, ws]),
                                               (hid.hi[:, kk, tk], hid.lo[:, kk, tk]), kk == 0, kk == M - 1)
                                if e == 1:
                                    mm.then_inc(E.m_mm, 1)
                            if e == 0:
                                mm.then_inc(E.blk_used, 1)

                if stage == 0:
                    step(0)
                with nc.tensor.Fori(0 if stage else 1, steps) as i:
                    step(i)
            pe.wait_ge(E.act, 2 * (2 * M + C))
            for b in range(NB):
                wait(pe, ln_y, LN_FFN1 + b - 1)
                for c in range(C):
                    mm = nc.tensor.transpose(ln_bank[b % 2][0:T, c * P:(c + 1) * P], h_act[:, c, b * T:(b + 1) * T],
                                             ident[:, :])
                mm.then_inc(ln_in, 1)


def kernel(**inputs):
    import numpy as np
    import concourse.bacc as bacc
    from concourse.bass_utils import run_bass_kernel_spmd

    f = {k: np.asarray(v) for k, v in inputs.items()}
    feats = lambda w, n: np.ascontiguousarray(w.reshape(w.shape[0] // P, P, n).transpose(1, 0, 2))

    def halves(w):
        return np.ascontiguousarray(feats(w, D).reshape(P, 2, BLK).transpose(1, 0, 2))

    def tiles(w):
        o, i = w.shape
        return w.reshape(o // P, P, i // P, P).transpose(0, 3, 2, 1)

    def padded(w):
        out = np.zeros((1, P, BLK), w.dtype)
        out[0, :, :w.shape[1]] = w
        return out

    x = f["x"].reshape(TOK, D)
    arrays = {}
    arrays["xT"] = np.ascontiguousarray(x.T.reshape(C, P, TOK).transpose(1, 0, 2))
    arrays["ctxT"] = np.ascontiguousarray(f["ctx_1024"].reshape(NB * KEYS, D).T.reshape(C, P, NB * KEYS))
    arrays["mask"] = np.ascontiguousarray(f["mask_BxS2_ik0"])
    names = {"lmlg": "L0_attn_lmlg", "theta": "L0_attn_theta", "init": "L0_attn_last_conv_init", "bq": "L0_xattn_bq",
             "bk": "L0_xattn_bk", "bv": "L0_xattn_bv", "gnw": "L1_attn_gn_weight", "gnb": "L1_attn_gn_bias",
             "b1": "L0_ffn_b1", "w1s": "L1_ffn_w1_s", "w2s": "L1_ffn_w2_s", "h1s": "L1_ffn_h1_s",
             "h2s": "L1_ffn_h2_s", "w3s": "L1_ffn_w3_s"}
    arrays["cols"] = np.ascontiguousarray(np.concatenate([f[names[n]].reshape(k, P).T for n, k in COLUMNS], axis=1))
    for n, m in (("wk0", "L0_xattn_Wk"), ("wv0", "L0_xattn_Wv"), ("wq0", "L0_xattn_Wq"), ("wo0", "L0_xattn_Wo"),
                 ("wq1", "L1_xattn_Wq"), ("wo1", "L1_xattn_Wproj")):
        arrays[n] = halves(f[m])
    arrays["wk1"], arrays["wv1"] = halves(f["L1_xattn_Wkv"][:, :D]), halves(f["L1_xattn_Wkv"][:, D:])
    for n, m in (("rq", "Wq"), ("rk", "Wk"), ("rv", "Wv"), ("ro", "Wo")):
        arrays[n] = halves(f["L1_attn_" + m].T)
    for n, m in (("bo", "L0_xattn_bo"), ("b2", "L0_ffn_b2"), ("bproj", "L1_xattn_bproj")):
        arrays[n] = f[m].reshape(1, D)
    arrays["u1"] = padded(feats(f["L0_ffn_U1"], RANK).reshape(P, C * RANK))
    arrays["v1"] = np.ascontiguousarray(f["L0_ffn_V1"].reshape(P, 2, BLK).transpose(1, 0, 2))
    arrays["u2"] = np.ascontiguousarray(feats(f["L0_ffn_U2"], RANK).reshape(P, 2, BLK).transpose(1, 0, 2))
    arrays["v2"] = padded(f["L0_ffn_V2"])
    w1, w2 = tiles(f["L1_ffn_w1_w"]), tiles(f["L1_ffn_w2_w"])
    blocks = [np.concatenate([w1, w2], axis=2).reshape(M, P, BLK)]
    for m in ("L1_ffn_h1_w", "L1_ffn_h2_w", "L1_ffn_w3_w"):
        w = tiles(f[m])
        blocks.append(w.reshape(w.shape[0], P, 2, BLK).transpose(0, 2, 1, 3).reshape(-1, P, BLK))
    arrays["ffn"] = np.concatenate(blocks)
    arrays["ident"] = np.eye(P, dtype=np.float32)
    arrays["kvec"] = np.ascontiguousarray(np.broadcast_to(np.arange(TAPS, dtype=np.float32), (P, C, TAPS)))
    s = np.zeros((H, C, P), np.float32)
    for h in range(H):
        s[h, h // G, HD * (h % G):HD * (h % G + 1)] = 1.0
    arrays["sel"] = s
    freq = (1.0 / 10000.0 ** (np.arange(0, HD, 2, dtype=np.float32) / HD)).astype(np.float32)
    emb = np.tile(np.arange(T, dtype=np.float32)[None, :] * freq[:, None], (P // len(freq), 1))
    sign = np.where(np.arange(P) % HD < HD // 2, -1.0, 1.0).astype(np.float32)
    arrays["cos"] = np.cos(emb).astype(np.float32)
    arrays["sin"] = (np.sin(emb) * sign[:, None]).astype(np.float32)
    arrays["rotm"] = np.eye(P, dtype=np.float32)[np.arange(P) ^ (HD // 2)]
    gamma = (1.0 - 2.0 ** (-5.0 - np.arange(H, dtype=np.float32))).astype(np.float32)
    dist = np.arange(T)[None, None, :] - np.arange(T)[:, None, None]
    arrays["decay"] = np.where(dist >= 0, SCALE * gamma[None, :, None] ** np.maximum(dist, 0), 0.0).astype(np.float32)
    arrays = {n + "_dram": np.ascontiguousarray(a) for n, a in arrays.items()}

    nc = bacc.Bacc("TRN2", target_bir_lowering=False, num_devices=1)
    d = {}
    for n, a in arrays.items():
        d[n[:-5]] = nc.dram_tensor(n, a.shape, mybir.dt.from_np(a.dtype), kind="ExternalInput").ap()
    d["out"] = nc.dram_tensor("out_dram", (NB, T, D), mybir.dt.float32, kind="ExternalOutput").ap()
    decoder_kernel(nc, d)
    r = run_bass_kernel_spmd(nc, [arrays], core_ids=[0])
    return r.results[0]["out_dram"]
```

```python
import concourse.bass as bass
from concourse import mybir
from contextlib import ExitStack
from collections import namedtuple

NB, T, D = 8, 100, 512
KEYS = 722
H, HD = 16, 32
P = 128
C = D // P
TOK = NB * T
HALF = TOK // 2
G = H // C
FF = 2048
M = FF // P
EPS = 1e-5
SCALE = HD ** -0.5
BLK = 1024
KA = 512
PIECES = ((0, KA), (KA, KEYS - KA))
KC = 128
NKC = -(-KEYS // KC)
PK = NKC * KC
HK = NKC // 2
RANK = 128
TAPS = NB + 1

COLUMNS = [("lmlg", C), ("theta", C), ("init", C), ("bq", C), ("bk", C), ("bv", C), ("gnw", C), ("gnb", C),
           ("b1", M), ("w1s", M), ("w2s", M), ("h1s", M), ("h2s", M), ("w3s", C)]
COL_AT = {}
for _n, _k in COLUMNS:
    COL_AT[_n] = sum(k for _, k in COLUMNS[:len(COL_AT)])
NCOL = sum(k for _, k in COLUMNS)

LN_CONV, LN_ATT0, LN_FFN0, LN_RET, LN_ATT1, LN_FFN1 = (NB * i for i in range(6))

BLOCKS = {}
_n = 0
for _name, _k in [("wk0", 2), ("wv0", 2), ("wq0", 2), ("wo0", 2), ("u1", 1), ("v1", 2), ("u2", 2), ("v2", 1),
                  ("rq", 2), ("rk", 2), ("rv", 2), ("ro", 2), ("wk1", 2), ("wv1", 2), ("wq1", 2), ("wo1", 2),
                  ("w12", M), ("h1", 2 * M), ("h2", 2 * M), ("w3", 2 * C)]:
    BLOCKS[_name] = _n
    _n += _k


Pair = namedtuple("Pair", "hi lo")

LN_LAST = LN_FFN1
CH_DEC, CH_ANG = 7, 16
MASKED = -1e38
LOWEST = -3e38
FFN_PAIRS = M // 2 + 2 * M + C
FFN0_BLOCKS = [("u1", 0), ("v1", 0), ("v1", 1), ("u2", 0), ("u2", 1), ("v2", 0)]
R_UNITS = 4 * C


def key_rows(j):
    return min(KC, KEYS - j * KC)


def decoder_kernel(nc, d):
    fp32, f32r, i32 = mybir.dt.float32, mybir.dt.float32r, mybir.dt.int32
    ACT, ALU, AX = mybir.ActivationFunctionType, mybir.AluOpType, mybir.AxisListType
    top = [-(-nc.sbuf_base // 64) * 64]
    LIMIT = nc.sbuf_usable_end

    def at(name, shape, dt):
        n = 4
        for x in shape[1:]:
            n *= x
        t = nc.alloc_sbuf_tensor_at(name, shape, dt, offset=top[0])
        top[0] += -(-n // 32) * 32
        assert top[0] <= LIMIT, (name, top[0], LIMIT)
        return t

    def pair(name, shape):
        return Pair(at(name + "_hi", shape, f32r), at(name + "_lo", shape, f32r))

    ctx = ExitStack()
    with ctx:
        def sem(name):
            return ctx.enter_context(nc.semaphore(name))

        raw = at("raw", [P, 2, BLK], fp32)
        x_res = at("x_res", [T, NB, D], fp32)
        ident = at("ident", [P, P], fp32)
        cols = at("cols", [P, NCOL], fp32)
        y = at("y", [T, 2, D], fp32)
        stats = at("stats", [T, 2, 6], fp32)
        mv = at("mv", [T, 2, 2], fp32)
        veps = at("veps", [T, 2, 1], fp32)
        rstd = at("rstd", [T, 2, 1], fp32)
        mhalf = at("mhalf", [P, H], fp32)
        shared_end = top[0]
        xT = pair("xT", [P, C, TOK])
        resid = at("resid", [T, 2, D], fp32)
        rows = at("rows", [T, 3, D], fp32)
        sel = at("sel", [H, C, P], fp32)
        phase_at = top[0]

        wkv_at = top[0]
        wk, wv = pair("wk", [P, C, D]), pair("wv", [P, C, D])
        wqo_at = top[0]
        wqo = pair("wqo", [P, C, D])
        craw_at = top[0]
        ctx_raw = at("ctx_raw", [P, 2, KEYS], fp32)
        cT_at = top[0]
        cT = pair("cT", [P, C, KEYS])
        vv_at = top[0]
        vv = pair("vv", [P, NKC, D])
        kT_at = top[0]
        kT = pair("kT", [P, 2, KEYS])
        conv_at = top[0]
        q_all = at("q_all", [P, C, TOK], fp32)
        p = at("p", [T, 2, PK], fp32)
        maskb = at("maskb", [T, KEYS], fp32)
        mask_raw = at("mask_raw", [T, KEYS], i32)
        rsum = at("rsum", [T, H], fp32)
        rinv = at("rinv", [T, P], fp32)
        nmax = at("nmax", [T, 2], fp32)
        pmax = at("pmax", [T, 2], fp32)
        rT = at("rT", [H, T], fp32)
        att_bq = at("att_bq", [P, C], fp32)
        oT = pair("oT", [P, C, T])
        top[0] = shared_end
        pT = pair("pT", [P, 2, NKC, 2 * T])
        qs = pair("qs", [P, C, T])
        oraw = at("oraw", [P, C, T], fp32)
        assert top[0] <= shared_end + 2 * 4 * C * TOK

        top[0] = conv_at
        cin = at("cin", [P, C, TOK], fp32)
        small = lambda n, *s: at(n, [P, *s], fp32)
        e1, th, thn = small("e1", C), small("th", C), small("thn", C)
        kvec, turns, ang, dec, taps = (small(n, C, TAPS) for n in ("kvec", "turns", "ang", "dec", "taps"))
        past = small("past", C, NB)
        top[0] = shared_end
        acc = at("acc", [P, C, TOK], fp32)

        top[0] = wkv_at
        v1, u2 = pair("v1", [P, FF]), pair("u2", [P, M, RANK])
        assert top[0] <= wqo_at
        top[0] = cT_at
        u1, v2 = pair("u1", [P, C, RANK]), pair("v2", [P, D])
        f_p, f_q = pair("f_p", [P, TOK]), pair("f_q", [P, TOK])
        assert top[0] <= vv_at
        top[0] = vv_at
        f_act, f_g = at("f_act", [P, 4, HALF], fp32), pair("f_g", [P, 4, HALF])
        assert top[0] <= kT_at

        top[0] = wkv_at
        qk = [at("q_rope", [P, C, TOK], fp32), at("k_rope", [P, C, TOK], fp32)]
        kb, xb = pair("kb", [P, C, T]), pair("xb", [P, C, T])
        assert top[0] <= wqo_at
        top[0] = wqo_at
        rqo = pair("rqo", [P, C, D])
        assert top[0] <= craw_at
        ctab, stab = at("ctab", [P, T], fp32), at("stab", [P, T], fp32)
        rotm = at("rotm", [P, P], fp32)
        assert top[0] <= cT_at
        top[0] = cT_at
        qbd = pair("qbd", [P, C, G, T])
        vb = pair("vb", [T, D])
        r_o, r_oT = at("r_o", [P, C, T], fp32), pair("r_oT", [P, C, T])
        assert top[0] <= vv_at
        top[0] = vv_at
        decay = at("decay", [T, H, T], fp32)
        p_raw, pb = at("p_raw", [T, 2, G * T], fp32), pair("pb", [T, 2, G * T])
        gd, gsq = at("gd", [T, D], fp32), at("gsq", [T, D], fp32)
        gsum, gneg, gvar = (at(n, [T, H], fp32) for n in ("gsum", "gneg", "gvar"))
        gsum2, geps, groot = (at(n, [T, H], fp32) for n in ("gsum2", "geps", "groot"))
        assert top[0] <= kT_at
        top[0] = kT_at
        rk, rv = pair("rk", [P, C, D]), pair("rv", [P, C, D])
        cosx, sinx = at("cosx", [P, 2, HALF], fp32), at("sinx", [P, 2, HALF], fp32)

        top[0] = shared_end
        h_act = at("h_act", [P, M, TOK], fp32)
        hid = pair("hid", [P, M, TOK])
        fw = pair("fw", [P, 2, BLK])
        silu, gated = at("silu", [P, 2, HALF], fp32), at("gated", [P, 2, HALF], fp32)

        def ps(name, n):
            return ctx.enter_context(nc.psum_tensor(name, [P, n], fp32))

        psS = [ps("psS0", 2 * KA), ps("psS1", 2 * KA)]
        psT = ps("psT", 2 * KA)
        psO = ps("psO", KA)
        psJ = ps("psJ", KA)
        ln_bank = [psO[:, :], psJ[:, :]]
        tx_bank = [psS[1][:, 0:KA], psS[1][:, KA:2 * KA]]
        bank4 = [t[:, i:i + KA] for i in (0, KA) for t in psS]
        bank4b = [psT[:, 0:KA], psT[:, KA:2 * KA], psO[:, :], psJ[:, :]]

        consts_in, conv_in, small_ready = sem("consts_in"), sem("conv_in"), sem("small_ready")
        raw_in = [sem("raw_in0"), sem("raw_in1")]
        w_hi, w_split = sem("w_hi"), sem("w_split")
        dve_chain, act_chain = sem("dve_chain"), sem("act_chain")
        ln_in, ln_y, ln_stat, ln_mv = sem("ln_in"), sem("ln_y"), sem("ln_stat"), sem("ln_mv")
        ln_eps, ln_rstd, ln_x = sem("ln_eps"), sem("ln_rstd"), sem("ln_x")
        tx_mm, tx_hi, tx_lo = sem("tx_mm"), sem("tx_hi"), sem("tx_lo")
        conv_done = sem("conv_done")
        out_done = sem("out_done")
        ffn0_resid = sem("ffn0_resid")
        def sems(prefix, names):
            return namedtuple("Sems", names)(*[sem(prefix + n) for n in names.split()])

        A = [sems(f"att{L}_", "ctx_in0 ctx_in1 ctx_hi ctx_split k_mm k_hi k_lo v_mm v_hi v_lo q_mm q_done qs_hi qs_done "
                              "s_mm maxed exped t_mm pt_hi pt_lo pv_mm o_copied rinv_done rt_mm rt_copied rb_mm "
                              "o_scaled o_biased o_hi o_lo resid_done mask_in mask_done pad_done") for L in range(2)]
        F = sems("ffn0_", "p_mm p_hi p_lo h_mm h_act h_hi h_lo acc_mm q_hi q_lo")
        R = sems("ret_", "tables_in q_mm q_raw rot_mm cos sin rope zero kb_hi k_ready x_ready q_hi q_ready v_mm v_hi "
                         "v_lo s_mm decayed p_hi p_lo pv_mm g_sum g_mean g_dev g_sq g_sum2 g_eps g_root g_norm to_mm "
                         "o_affine o_hi o_lo")
        E = sems("ffn1_", "blk_used w_mm silu gated g_hi g_lo m_mm act conv_hi conv_lo")
        mx_raw, apart = sem("mx_raw"), sem("apart")

        def wait(eng, s, v):
            if isinstance(v, int) and v <= 0:
                return
            eng.wait_ge(s, v)

        def wait_apart(eng, s, v):
            wait(eng, s, v)
            if not isinstance(v, int):
                eng.sem_inc(apart, 1)

        def block_parts(name, i, w):
            n = BLOCKS[name] + i
            tall = w.hi.shape[1] if len(w.hi.shape) == 3 else 1
            wide = min(BLK, w.hi.shape[-1] * tall)
            src = raw[:, n % 2, 0:wide]
            if len(w.hi.shape) == 2:
                sl = slice(wide * i, wide * (i + 1))
                return w.hi[:, sl], w.lo[:, sl], src
            k = wide // w.hi.shape[-1]
            sl = slice(k * i, k * (i + 1))
            return w.hi[:, sl, :], w.lo[:, sl, :], src.rearrange("p (a b) -> p a b", a=k)

        FFN0_W = {"u1": u1, "v1": v1, "u2": u2, "v2": v2}

        def three(out, st, mv_, first, last, n=None):
            nc.tensor.matmul(out, st[0], mv_[0], start=first, stop=False)
            nc.tensor.matmul(out, st[0], mv_[1], start=False, stop=False)
            return nc.tensor.matmul(out, st[1], mv_[0], start=False, stop=last)

        def col(name, c):
            return cols[:, COL_AT[name] + c:COL_AT[name] + c + 1]

        def cols4(name, n):
            return cols[:, COL_AT[name]:COL_AT[name] + n]

        block = ctx.enter_context(nc.Block())

        @block.sync
        def _(sp):
            def blocks(name, k0, k):
                for i in range(k0, k0 + k):
                    n = BLOCKS[name] + i
                    wait(sp, w_split, n - 1)
                    sp.dma_start(raw[:, n % 2, :], d[name][i]).then_inc(raw_in[n % 2], 16)

            def context(a, b, cs):
                for c in cs:
                    wait(sp, a.ctx_split, 4 * b + c - 1)
                    sp.dma_start(ctx_raw[:, c % 2, :], d["ctxT"][c, :, bass.ds(b * KEYS, KEYS)])\
                      .then_inc((a.ctx_in0, a.ctx_in1)[c % 2], 16)

            def attention_loads(L):
                a = A[L]
                if L == 1:
                    with nc.sync.Fori(1, NB) as b:
                        context(a, b, range(C))
                        sp.wait_ge(a.mask_done, b)
                        sp.dma_start(mask_raw[:, :], d["mask"][bass.ds(b, 1), :].broadcast_to([T, KEYS]))\
                          .then_inc(a.mask_in, 16)
                else:
                    with nc.sync.Fori(1, NB) as b:
                        context(a, b, range(C))

            blocks("wk0", 0, 2)
            context(A[0], 0, (0,))
            sp.dma_start(cols[:, :], d["cols"]).then_inc(conv_in, 16)
            sp.dma_start(kvec[:, :, :], d["kvec"]).then_inc(conv_in, 16)
            sp.dma_start(cin[:, :, :], d["xT"]).then_inc(conv_in, 16)
            context(A[0], 0, (1,))
            sp.dma_start(ident[:, :], d["ident"]).then_inc(consts_in, 16)
            sp.dma_start(sel[:, :, :], d["sel"]).then_inc(consts_in, 16)
            for i, n in enumerate(("bo", "b2", "bproj")):
                sp.dma_start(rows[:, i, :], d[n][:, :].broadcast_to([T, D])).then_inc(consts_in, 16)
            blocks("wv0", 0, 2)
            context(A[0], 0, (2, 3))
            blocks("wq0", 0, 2)
            blocks("wo0", 0, 2)
            attention_loads(0)
            for n, k in (("u1", 1), ("v1", 2), ("u2", 2), ("v2", 1), ("rq", 2), ("rk", 2), ("rv", 2)):
                blocks(n, 0, k)
            sp.wait_ge(F.h_mm, 2 * M)
            sp.wait_ge(F.acc_mm, 2 * M)
            for t, n in ((ctab, "cos"), (stab, "sin"), (rotm, "rotm"), (decay, "decay")):
                sp.dma_start(t[:], d[n]).then_inc(R.tables_in, 16)
            blocks("ro", 0, 2)
            sp.wait_ge(R.rope, R_UNITS)
            context(A[1], 0, (0, 1))
            sp.dma_start(mask_raw[:, :], d["mask"][0:1, :].broadcast_to([T, KEYS])).then_inc(A[1].mask_in, 16)
            for n in ("wk1", "wv1", "wq1"):
                blocks(n, 0, 2)
            context(A[1], 0, (2, 3))
            blocks("wo1", 0, 2)
            attention_loads(1)
            with nc.sync.Fori(0, FFN_PAIRS) as i:
                for e in range(2):
                    sp.wait_ge(w_split, 2 * i + (BLOCKS["w12"] + e - 1))
                    sp.dma_start(raw[:, e, :], d["ffn"][bass.ds(2 * i + e, 1)].rearrange("a p n -> (a p) n"))\
                      .then_inc(raw_in[e], 16)

            for b in range(NB):
                sp.wait_ge(ln_x, LN_LAST + b + 1)
                sp.dma_start(d["out"][b], x_res[:, b, :]).then_inc(out_done, 16)
            sp.wait_ge(out_done, 16 * NB)

        @block.gpsimd
        def _(pool):
            def split_lo(name, i, w):
                n = BLOCKS[name] + i
                hi, lo, src = block_parts(name, i, w)
                pool.wait_ge(w_hi, n + 1)
                nc.gpsimd.tensor_tensor(lo, src, hi, ALU.subtract).then_inc(w_split, 1)

            def context_lo(a, b, c):
                wait_apart(pool, a.ctx_hi, 4 * b + c + 1)
                nc.gpsimd.tensor_tensor(cT.lo[:, c, :], ctx_raw[:, c % 2, :], cT.hi[:, c, :], ALU.subtract)\
                  .then_inc(a.ctx_split, 1)

            def queries_lo(a, b):
                wait_apart(pool, a.qs_hi, b + 1)
                nc.gpsimd.tensor_tensor(qs.lo[:, :, :], q_all[:, :, bass.ds(b * T, T)], qs.hi[:, :, :], ALU.subtract)\
                  .then_inc(a.qs_done, 1)

            def mask_bias(a, b):
                wait_apart(pool, a.mask_in, 16 * (b + 1))
                wait_apart(pool, a.maxed, H * b)
                nc.gpsimd.tensor_scalar(maskb[:, :], mask_raw[:, :], 0.0, MASKED, ALU.is_equal, ALU.mult)\
                  .then_inc(a.mask_done, 1)

            def root(n, s):
                wait_apart(pool, ln_mv, n + 1)
                nc.gpsimd.tensor_scalar(veps[:, s, :], mv[:, s, 1:2], EPS, None, ALU.add).then_inc(ln_eps, 1)
                wait_apart(pool, ln_eps, n + 1)
                nc.gpsimd.tensor_tensor(rstd[:, s, :], veps[:, s, :], mhalf[0:T, 0:1], ALU.pow).then_inc(ln_rstd, 1)

            def add_bias(row, b, s, n, done):
                wait_apart(pool, ln_y, n - (0 if s is None else 1))
                s = s or 0
                nc.gpsimd.tensor_tensor(resid[:, s, :], x_res[:, b, :],
                                        rows[:, row, :], ALU.add).then_inc(done, 1)

            def attention(L, row, base):
                a = A[L]

                def batch(b, last):
                    if not last:
                        for c in range(C):
                            context_lo(a, b + 1, c)
                        queries_lo(a, b + 1)
                        if L == 1:
                            mask_bias(a, b + 1)
                    elif L == 0:
                        for n, i in FFN0_BLOCKS:
                            split_lo(n, i, FFN0_W[n])
                    add_bias(row, b, None, base + b, a.resid_done)
                    root(base + b, 0)

                batch(0, False)
                with nc.gpsimd.Fori(1, NB - 1) as b:
                    batch(b, False)
                batch(NB - 1, True)

            nc.gpsimd.memset(mhalf[:, :], -0.5).then_inc(small_ready, 1)
            for i in range(2):
                split_lo("wk0", i, wk)
            for c in range(C):
                context_lo(A[0], 0, c)
            for i in range(2):
                split_lo("wv0", i, wv)
            for i in range(2):
                split_lo("wq0", i, wqo)
            pool.wait_ge(small_ready, 1)
            for b in range(NB):
                root(LN_CONV + b, b % 2)
            pool.wait_ge(conv_done, C * (NB + 1))
            nc.gpsimd.memset(p[:, :, KEYS:PK], 0.0).then_inc(A[0].pad_done, 1)
            nc.gpsimd.memset(rinv[:, H:P], 0.0).then_inc(A[0].pad_done, 1)
            queries_lo(A[0], 0)
            for i in range(2):
                split_lo("wo0", i, wqo)
            attention(0, 0, LN_ATT0)

            for n, w in (("rq", rqo), ("rk", rk), ("rv", rv)):
                for i in range(2):
                    split_lo(n, i, w)
            for b in range(NB):
                add_bias(1, b, b % 2, LN_FFN0 + b, ffn0_resid)
                root(LN_FFN0 + b, b % 2)

            wait_apart(pool, F.q_lo, 2)
            nc.gpsimd.memset(qbd.hi[:].bitcast(fp32), 0.0).then_inc(R.zero, 1)
            nc.gpsimd.memset(qbd.lo[:].bitcast(fp32), 0.0).then_inc(R.zero, 1)
            wait_apart(pool, R.tables_in, 64)

            def rope_sum(u):
                m, h = u // 2 % C, u % 2
                wait_apart(pool, R.sin, u + 1)
                wait_apart(pool, R.cos, u + 1)
                nc.gpsimd.tensor_tensor(qk[u // (2 * C)][:, m, h * HALF:(h + 1) * HALF], cosx[:, u % 2, :],
                                        sinx[:, u % 2, :], ALU.add).then_inc(R.rope, 1)

            for u in range(R_UNITS):
                m, h = u // 2 % C, u % 2
                wait_apart(pool, R.q_raw, u + 1)
                wait_apart(pool, R.rope, u - 1)
                nc.gpsimd.tensor_tensor(cosx[:, u % 2, :].rearrange("p (b t) -> p b t", t=T),
                                        qk[u // (2 * C)][:, m, h * HALF:(h + 1) * HALF]
                                        .rearrange("p (b t) -> p b t", t=T),
                                        ctab[:, :].unsqueeze(1).to_broadcast([P, NB // 2, T]), ALU.mult)\
                  .then_inc(R.cos, 1)
                if u >= 1:
                    rope_sum(u - 1)
            rope_sum(R_UNITS - 1)
            for i in range(2):
                split_lo("ro", i, rqo)

            def keys_lo(b):
                wait_apart(pool, R.kb_hi, b + 1)
                nc.gpsimd.tensor_tensor(kb.lo[:, :, :], qk[1][:, :, bass.ds(b * T, T)], kb.hi[:, :, :], ALU.subtract)\
                  .then_inc(R.k_ready, 1)

            def retention_pool(b, front, back):
                if back:
                    wait_apart(pool, R.g_dev, b)
                    nc.gpsimd.tensor_tensor(gsq[:, :], gd[:, :], gd[:, :], ALU.mult).then_inc(R.g_sq, 1)
                    wait_apart(pool, R.g_sum2, b)
                    nc.gpsimd.tensor_scalar(geps[:, :], gsum2[:, :], 1.0 / HD, EPS, ALU.mult, ALU.add)\
                      .then_inc(R.g_eps, 1)
                    wait_apart(pool, R.g_eps, b)
                    nc.gpsimd.tensor_tensor(groot[:, :], geps[:, :], mhalf[0:T, :], ALU.pow).then_inc(R.g_root, 1)
                if front and not (isinstance(b, int) and b == NB - 1):
                    keys_lo(b + 1)
                if back:
                    root(LN_RET + b - 1, 0)

            keys_lo(0)
            retention_pool(0, True, False)
            with nc.gpsimd.Fori(1, NB - 1) as b:
                retention_pool(b, True, True)
            retention_pool(NB - 1, True, True)
            for n, w in (("wk1", wk), ("wv1", wv)):
                for i in range(2):
                    split_lo(n, i, w)
            retention_pool(NB, False, True)

            for c in range(C):
                context_lo(A[1], 0, c)
            for i in range(2):
                split_lo("wq1", i, wqo)
            pool.wait_ge(ln_in, LN_RET + NB)
            mask_bias(A[1], 0)
            nc.gpsimd.memset(p[:, :, KEYS:PK], 0.0).then_inc(A[1].pad_done, 1)
            nc.gpsimd.memset(rinv[:, H:P], 0.0).then_inc(A[1].pad_done, 1)
            queries_lo(A[1], 0)
            for i in range(2):
                split_lo("wo1", i, wqo)
            attention(1, 2, LN_ATT1)

            def ffn_lo(i):
                for e in range(2):
                    wait_apart(pool, w_hi, 2 * i + (BLOCKS["w12"] + e + 1))
                    nc.gpsimd.tensor_tensor(fw.lo[:, e, :], raw[:, e, :], fw.hi[:, e, :], ALU.subtract)\
                      .then_inc(w_split, 1)

            ffn_lo(0)
            with nc.gpsimd.Fori(1, FFN_PAIRS) as i:
                ffn_lo(i)
            for b in range(NB):
                root(LN_FFN1 + b, b % 2)

        @block.scalar
        def _(act):
            def transposed_hi(n, b):
                act.wait_ge(tx_mm, n + 1)
                nc.scalar.activation(xT.hi[:, :, b * T:(b + 1) * T],
                                     tx_bank[n % 2][:, 0:C * T].rearrange("p (c t) -> p c t", c=C), ACT.Copy)\
                  .then_inc(tx_hi, 1)

            def weights_hi(name, i, w):
                n = BLOCKS[name] + i
                hi, _, src = block_parts(name, i, w)
                act.wait_ge(raw_in[n % 2], 16 * (n // 2 + 1))
                nc.scalar.activation(hi, src, ACT.Copy).then_inc(w_hi, 1)

            def context_hi(a, b, c):
                act.wait_ge((a.ctx_in0, a.ctx_in1)[c % 2], 16 * (2 * b + c // 2 + 1))
                if c == 0:
                    wait(act, a.k_mm, 2 * C * b)
                nc.scalar.activation(cT.hi[:, c, :], ctx_raw[:, c % 2, :], ACT.Copy).then_inc(a.ctx_hi, 1)

            def queries_hi(a, b):
                wait_apart(act, a.s_mm, H * b)
                nc.scalar.activation(qs.hi[:, :, :], q_all[:, :, bass.ds(b * T, T)], ACT.Copy).then_inc(a.qs_hi, 1)

            def queries(a, bias):
                for i in range(2 * C):
                    m, h = i // 2, i % 2
                    act.wait_ge(a.q_mm, i + 1)
                    src = psS[i % 2][:, (i // 2 % 2) * KA:(i // 2 % 2) * KA + HALF]
                    dst = q_all[:, m, h * HALF:(h + 1) * HALF]
                    if bias:
                        nc.scalar.activation(dst, src, ACT.Identity, bias=att_bq[:, m:m + 1], scale=SCALE)\
                          .then_inc(a.q_done, 1)
                    else:
                        nc.scalar.activation(dst, src, ACT.Copy, scale=SCALE).then_inc(a.q_done, 1)

            def keys_hi(L, b, g, i):
                a = A[L]
                k0, kn = PIECES[i]
                act.wait_ge(a.k_mm, 8 * b + 2 * g + i + 1)
                dst = kT.hi[:, g % 2, k0:k0 + kn]
                if L == 0:
                    nc.scalar.activation(dst, psJ[:, 0:kn], ACT.Identity, bias=col("bk", g)).then_inc(a.k_hi, 1)
                else:
                    nc.scalar.activation(dst, psJ[:, 0:kn], ACT.Copy).then_inc(a.k_hi, 1)

            def values_hi(a, b, j):
                act.wait_ge(a.v_mm, NKC * b + j + 1)
                if j == 0:
                    wait(act, a.pv_mm, H // 2 * b)
                n = key_rows(j)
                nc.scalar.activation(vv.hi[0:n, j, :], psS[j % 2][0:n, 0:D], ACT.Copy).then_inc(a.v_hi, 1)

            def attention(L):
                a = A[L]

                def exps(b, h):
                    act.wait_ge(a.maxed, H * b + h + 1)
                    src = psS[h % 2][0:T, 0:KEYS] if L == 0 else p[:, h % 2, 0:KEYS]
                    nc.scalar.activation(p[:, h % 2, 0:KEYS], src, ACT.Exp, bias=nmax[:, h % 2:h % 2 + 1],
                                         accum_out=rsum[:, h:h + 1]).then_inc(a.exped, 1)

                def probs_hi(b, h):
                    act.wait_ge(a.t_mm, H * b + h + 1)
                    pr = h // 2
                    if h % 2 == 0:
                        wait(act, a.pv_mm, H // 2 * b + pr - 1)
                    for i in range(2):
                        nc.scalar.activation(
                            pT.hi[:, pr % 2, HK * i:HK * i + HK, (h % 2) * T:(h % 2 + 1) * T],
                            psT[:, KA * i:KA * i + HK * T].rearrange("p (k t) -> p k t", k=HK), ACT.Copy)\
                          .then_inc(a.pt_hi, 1)

                def batch(b, last):
                    for t in range(H + 1):
                        if t >= 1:
                            probs_hi(b, t - 1)
                        if t < H:
                            exps(b, t)
                        g, i = t // 4 + 1, t % 4
                        if i < 2 and g < C and t < 12:
                            keys_hi(L, b, g, i)
                        if t in (14, 15) and not last:
                            keys_hi(L, b + 1, 0, t - 14)
                        if 10 <= t < 10 + C and not last:
                            context_hi(a, b + 1, t - 10)
                        if L == 0 and last and 10 <= t < 10 + len(FFN0_BLOCKS):
                            if t == 10:
                                act.wait_ge(a.v_mm, NKC * NB)
                                act.wait_ge(a.k_mm, 2 * C * NB)
                            n, i = FFN0_BLOCKS[t - 10]
                            weights_hi(n, i, FFN0_W[n])
                    if not last:
                        queries_hi(a, b + 1)
                        values_hi(a, b + 1, 0)
                        values_hi(a, b + 1, 1)
                    act.wait_ge(a.rt_mm, b + 1)
                    nc.scalar.activation(rT[:, :], psT[0:H, 0:T], ACT.Copy).then_inc(a.rt_copied, 1)
                    if not last:
                        values_hi(a, b + 1, 2)
                        values_hi(a, b + 1, 3)
                    act.wait_ge(a.o_biased if L == 0 else a.o_scaled, b + 1)
                    nc.scalar.activation(oT.hi[:, :, :], oraw[:, :, :], ACT.Copy).then_inc(a.o_hi, 1)
                    if not last:
                        values_hi(a, b + 1, 4)
                        values_hi(a, b + 1, 5)

                if L == 0:
                    act.wait_ge(A[0].pad_done, 2)
                batch(0, False)
                with nc.scalar.Fori(1, NB - 1) as b:
                    batch(b, False)
                batch(NB - 1, True)

            for i in range(2):
                weights_hi("wk0", i, wk)
            context_hi(A[0], 0, 0)
            act.wait_ge(conv_in, 48)
            nc.scalar.activation(e1[:, :], cols4("lmlg", C), ACT.Exp).then_inc(act_chain, 1)
            context_hi(A[0], 0, 1)
            act.wait_ge(dve_chain, CH_DEC)
            nc.scalar.activation(dec[:, :, :], dec[:, :, :], ACT.Exp, scale=-1.0).then_inc(act_chain, 1)
            context_hi(A[0], 0, 2)
            act.wait_ge(dve_chain, CH_ANG)
            nc.scalar.activation(ang[:, :, :], ang[:, :, :], ACT.Sin).then_inc(act_chain, 1)
            context_hi(A[0], 0, 3)
            for i in range(2):
                weights_hi("wv0", i, wv)
            for i in range(2):
                keys_hi(0, 0, 0, i)
            for i in range(2):
                weights_hi("wq0", i, wqo)
            for j in range(NKC):
                values_hi(A[0], 0, j)
            for b in range(NB):
                transposed_hi(LN_CONV + b, b)
            act.wait_ge(tx_lo, NB)
            nc.scalar.activation(att_bq[:, :], cols4("bq", C), ACT.Copy, scale=SCALE).then_inc(act_chain, 1)
            act.wait_ge(act_chain, 4)
            queries(A[0], True)
            act.wait_ge(A[0].q_done, 2 * C)
            queries_hi(A[0], 0)
            for i in range(2):
                weights_hi("wo0", i, wqo)
            attention(0)
            act.wait_ge(ln_in, LN_ATT0 + NB)
            for i in range(2):
                weights_hi("rq", i, rqo)
            for b in range(NB):
                transposed_hi(LN_ATT0 + b, b)
            for i in range(2):
                weights_hi("rk", i, rk)

            for h in range(2):
                act.wait_ge(F.p_mm, h + 1)
                nc.scalar.activation(f_p.hi[:, h * HALF:(h + 1) * HALF], bank4[2 * h][:, 0:HALF], ACT.Copy)\
                  .then_inc(F.p_hi, 1)
            for u in range(2 * M):
                act.wait_ge(F.h_mm, u + 1)
                wait(act, F.h_lo, u - 3)
                nc.scalar.activation(f_act[:, u % 4, :], bank4b[u % 4][:, 0:HALF], ACT.Gelu_apprx_tanh,
                                     bias=col("b1", u // 2)).then_inc(F.h_act, 1)
                if u in (8, 16):
                    weights_hi("rv", u // 8 - 1, rv)
            for h in range(2):
                act.wait_ge(F.acc_mm, 2 * M - 1 + h)
                nc.scalar.activation(f_q.hi[:, h * HALF:(h + 1) * HALF], bank4[2 * h][:, 0:HALF], ACT.Copy)\
                  .then_inc(F.q_hi, 1)
            for b in range(NB):
                transposed_hi(LN_FFN0 + b, b)

            for u in range(R_UNITS):
                m, h = u // 2 % C, u % 2
                act.wait_ge(R.q_mm, u + 1)
                nc.scalar.activation(qk[u // (2 * C)][:, m, h * HALF:(h + 1) * HALF], bank4[u % 4][:, 0:HALF],
                                     ACT.Copy).then_inc(R.q_raw, 1)

            def operands_hi(b):
                ts = bass.ds(b * T, T)
                wait_apart(act, R.v_mm, b)
                nc.scalar.activation(xb.hi[:, :, :], xT.hi[:, :, ts], ACT.Copy)
                nc.scalar.activation(xb.lo[:, :, :], xT.lo[:, :, ts], ACT.Copy).then_inc(R.x_ready, 1)
                wait_apart(act, R.s_mm, C * b)
                for j in range(G):
                    r = slice(HD * j, HD * (j + 1))
                    last = nc.scalar.activation(qbd.hi[r, :, j, :], qk[0][r, :, ts], ACT.Copy)
                last.then_inc(R.q_hi, 1)
                nc.scalar.activation(kb.hi[:, :, :], qk[1][:, :, ts], ACT.Copy).then_inc(R.kb_hi, 1)

            def probs_hi(b, g):
                act.wait_ge(R.decayed, C * b + g + 1)
                wait(act, R.pv_mm, C * b + g - 1)
                nc.scalar.activation(pb.hi[:, g % 2, :], p_raw[:, g % 2, :], ACT.Copy).then_inc(R.p_hi, 1)

            def ffn_hi(i, e):
                act.wait_ge(raw_in[e], 16 * i + 16 * (BLOCKS["w12"] // 2 + 1))
                nc.scalar.activation(fw.hi[:, e, :], raw[:, e, :], ACT.Copy).then_inc(w_hi, 1)

            def retention_act(b, front, back):
                if front:
                    act.wait_ge(R.v_mm, b + 1)
                    wait(act, R.pv_mm, C * b)
                    nc.scalar.activation(vb.hi[:, :], psT[0:T, 0:D], ACT.Copy).then_inc(R.v_hi, 1)
                    probs_hi(b, 0)
                    probs_hi(b, 1)
                if back:
                    act.wait_ge(R.to_mm, b)
                    wait(act, R.o_lo, b - 1)
                    for c in range(C):
                        last = nc.scalar.activation(r_o[:, c, :], psJ[:, c * T:(c + 1) * T], ACT.Identity,
                                                    bias=col("gnb", c), scale=col("gnw", c))
                    last.then_inc(R.o_affine, 1)
                    act.wait_ge(R.o_affine, b)
                    nc.scalar.activation(r_oT.hi[:, :, :], r_o[:, :, :], ACT.Copy).then_inc(R.o_hi, 1)
                if front:
                    probs_hi(b, 2)
                    probs_hi(b, 3)
                    if not (isinstance(b, int) and b == NB - 1):
                        operands_hi(b + 1)

            act.wait_ge(R.rope, R_UNITS)
            act.wait_ge(R.zero, 2)
            operands_hi(0)
            for i in range(2):
                weights_hi("ro", i, rqo)
            retention_act(0, True, False)
            with nc.scalar.Fori(1, NB - 1) as b:
                retention_act(b, True, True)
            retention_act(NB - 1, True, True)
            for n, w in (("wk1", wk), ("wv1", wv)):
                for i in range(2):
                    weights_hi(n, i, w)
            retention_act(NB, False, True)
            act.wait_ge(ln_in, LN_RET + NB)
            for c in range(C):
                context_hi(A[1], 0, c)
            for b in range(NB):
                transposed_hi(LN_RET + b, b)

            for i in range(2):
                keys_hi(1, 0, 0, i)
            for i in range(2):
                weights_hi("wq1", i, wqo)
            for j in range(NKC):
                values_hi(A[1], 0, j)
            queries(A[1], False)
            act.wait_ge(A[1].q_done, 2 * C)
            queries_hi(A[1], 0)
            for i in range(2):
                weights_hi("wo1", i, wqo)
            attention(1)
            ffn_hi(0, 0)
            ffn_hi(0, 1)
            for b in range(NB):
                transposed_hi(LN_ATT1 + b, b)

            def silus(i):
                for q in range(4):
                    act.wait_ge(E.w_mm, 4 * i + q + 1)
                    wait_apart(act, E.gated, 4 * i + (q - 1))
                    nc.scalar.activation(silu[:, q % 2, :], bank4[q][:, 0:HALF], ACT.Silu,
                                         scale=cols[:, bass.ds(2 * i + (COL_AT["w1s"] + q // 2), 1)])\
                      .then_inc(E.silu, 1)
                    if q % 2:
                        ffn_hi(i + 1, q // 2)

            silus(0)
            with nc.scalar.Fori(1, M // 2) as i:
                silus(i)
            for stage, (name, steps, func) in enumerate((("h1s", M, ACT.Gelu), ("h2s", M, ACT.Gelu),
                                                         ("w3s", C, ACT.Copy))):
                if stage:
                    act.wait_ge(E.m_mm, 2 * M * stage)
                    act.wait_ge(E.act, 2 * M * stage)
                    for k in range(M):
                        nc.scalar.activation(hid.hi[:, k, :], h_act[:, k, :], ACT.Copy).then_inc(E.conv_hi, 1)

                def two_chunks(i, last=False, stage=stage, name=name, func=func):
                    for o in range(2):
                        ahead = not (last and o == 1)
                        if ahead:
                            act.wait_ge(E.blk_used, 2 * i + (M * stage + o + 1))
                            ffn_hi(2 * i + (M // 2 + M * stage + o + 1), 0)
                        for h in range(2):
                            wait_apart(act, E.m_mm, 4 * i + (2 * M * stage + 2 * o + h + 1))
                            if stage:
                                act.wait_ge(E.conv_lo, M * stage)
                            nc.scalar.activation(h_act[:, 2 * i + o, h * HALF:(h + 1) * HALF],
                                                 bank4[2 * o + h][:, 0:HALF], func,
                                                 scale=cols[:, bass.ds(2 * i + (COL_AT[name] + o), 1)])\
                              .then_inc(E.act, 1)
                        if ahead:
                            ffn_hi(2 * i + (M // 2 + M * stage + o + 1), 1)

                with nc.scalar.Fori(0, steps // 2 - (1 if stage == 2 else 0)) as i:
                    two_chunks(i)
                if stage == 2:
                    two_chunks(steps // 2 - 1, last=True)

        @block.vector
        def _(dve):
            link = [0]

            def chain(ins):
                link[0] += 1
                ins.then_inc(dve_chain, 1)
                dve.wait_ge(dve_chain, link[0])

            def norm_stats(n, s, src):
                nc.vector.bn_stats(stats[:, s, :], src).then_inc(ln_stat, 1)
                wait_apart(dve, ln_stat, n + 1)
                nc.vector.bn_aggr(mv[:, s, :], stats[:, s, :]).then_inc(ln_mv, 1)

            def norm_apply(n, s, src, b):
                dve.wait_ge(ln_rstd, n + 1)
                nc.vector.tensor_scalar(x_res[:, b, :], src,
                                        mv[:, s, 0:1], rstd[:, s, :], ALU.subtract, ALU.mult).then_inc(ln_x, 1)

            def transposed_lo(n, b):
                dve.wait_ge(tx_hi, n + 1)
                sl = slice(b * T, (b + 1) * T)
                nc.vector.tensor_tensor(xT.lo[:, :, sl],
                                        tx_bank[n % 2][:, 0:C * T].rearrange("p (c t) -> p c t", c=C),
                                        xT.hi[:, :, sl], ALU.subtract).then_inc(tx_lo, 1)

            def keys_lo(L, b, g, i):
                a = A[L]
                k0, kn = PIECES[i]
                dve.wait_ge(a.k_hi, 8 * b + 2 * g + i + 1)
                hi, lo = kT.hi[:, g % 2, k0:k0 + kn], kT.lo[:, g % 2, k0:k0 + kn]
                if L == 0:
                    nc.vector.scalar_tensor_tensor(lo, psJ[:, 0:kn], col("bk", g), hi, ALU.add, ALU.subtract)\
                      .then_inc(a.k_lo, 1)
                else:
                    nc.vector.tensor_tensor(lo, psJ[:, 0:kn], hi, ALU.subtract).then_inc(a.k_lo, 1)

            def values_lo(a, b, j):
                dve.wait_ge(a.v_hi, NKC * b + j + 1)
                n = key_rows(j)
                nc.vector.tensor_tensor(vv.lo[0:n, j, :], psS[j % 2][0:n, 0:D], vv.hi[0:n, j, :], ALU.subtract)\
                  .then_inc(a.v_lo, 1)

            def attention(L, base):
                a = A[L]

                def head_max(b, h):
                    wait_apart(dve, a.s_mm, H * b + h + 1)
                    m = nmax[:, h % 2:h % 2 + 1]
                    if L == 0:
                        nc.vector.tensor_reduce(m, psS[h % 2][0:T, 0:KEYS], AX.X, ALU.max, negate=True)\
                          .then_inc(a.maxed, 1)
                    else:
                        if h == 0:
                            wait_apart(dve, a.mask_done, b + 1)
                        nc.vector.tensor_tensor_reduce(out=p[:, h % 2, 0:KEYS], in0=psS[h % 2][0:T, 0:KEYS],
                                                       in1=maskb[:, :], scale=1.0, scalar=LOWEST, op0=ALU.add,
                                                       op1=ALU.max, accum_out=pmax[:, h % 2:h % 2 + 1])\
                          .then_inc(mx_raw, 1)
                        dve.wait_ge(mx_raw, H * b + h + 1)
                        nc.vector.tensor_scalar(m, pmax[:, h % 2:h % 2 + 1], -1.0, None, ALU.mult)\
                          .then_inc(a.maxed, 1)

                def probs_lo(b, h):
                    pr = h // 2
                    for i in range(2):
                        dve.wait_ge(a.pt_hi, 2 * (H * b + h) + i + 1)
                        sl = (slice(None), pr % 2, slice(HK * i, HK * i + HK), slice((h % 2) * T, (h % 2 + 1) * T))
                        nc.vector.tensor_tensor(pT.lo[sl],
                                                psT[:, KA * i:KA * i + HK * T].rearrange("p (k t) -> p k t", k=HK),
                                                pT.hi[sl], ALU.subtract).then_inc(a.pt_lo, 1)

                def heads_out(b, pr):
                    dve.wait_ge(a.pv_mm, H // 2 * b + pr + 1)
                    if pr == 0:
                        wait(dve, a.o_lo, b)
                    for e in range(2):
                        g, j = divmod(2 * pr + e, G)
                        cp = nc.vector.tensor_copy(oraw[HD * j:HD * (j + 1), g, :],
                                                   psO[HD * e:HD * (e + 1), T * e:T * (e + 1)])
                    cp.then_inc(a.o_copied, 1)

                def batch(b, last):
                    for t in range(H + 1):
                        if t < H:
                            head_max(b, t)
                        if t >= 1:
                            probs_lo(b, t - 1)
                        g, i = t // 4 + 1, t % 4
                        if i < 2 and g < C and t < 12:
                            keys_lo(L, b, g, i)
                        if t in (14, 15) and not last:
                            keys_lo(L, b + 1, 0, t - 14)
                        if t >= 3 and t % 2 == 1:
                            heads_out(b, (t - 3) // 2)
                    dve.wait_ge(a.exped, H * (b + 1))
                    nc.vector.reciprocal(rinv[:, 0:H], rsum[:, :]).then_inc(a.rinv_done, 1)
                    if not last:
                        values_lo(a, b + 1, 0)
                        values_lo(a, b + 1, 1)
                    heads_out(b, H // 2 - 1)
                    if not last:
                        values_lo(a, b + 1, 2)
                    dve.wait_ge(a.rb_mm, b + 1)
                    dve.wait_ge(a.o_copied, H // 2 * (b + 1))
                    nc.vector.tensor_tensor(oraw[:, :, :], psT[:, 0:C * T].rearrange("p (c t) -> p c t", c=C),
                                            oraw[:, :, :], ALU.mult).then_inc(a.o_scaled, 1)
                    if L == 0:
                        dve.wait_ge(a.o_scaled, b + 1)
                        nc.vector.tensor_tensor(oraw[:, :, :], oraw[:, :, :],
                                                cols4("bv", C).unsqueeze(2).to_broadcast([P, C, T]), ALU.add)\
                          .then_inc(a.o_biased, 1)
                    if not last:
                        values_lo(a, b + 1, 3)
                    dve.wait_ge(a.o_hi, b + 1)
                    nc.vector.tensor_tensor(oT.lo[:, :, :], oraw[:, :, :], oT.hi[:, :, :], ALU.subtract)\
                      .then_inc(a.o_lo, 1)
                    if not last:
                        values_lo(a, b + 1, 4)
                    dve.wait_ge(a.resid_done, b + 1)
                    dve.wait_ge(ln_in, base + b + 1)
                    dve.wait_ge(ln_x, base + b)
                    nc.vector.tensor_tensor(y[:, 0, :], psT[0:T, KA:KA + D], resid[:, 0, :], ALU.add)\
                      .then_inc(ln_y, 1)
                    if not last:
                        values_lo(a, b + 1, 5)
                    dve.wait_ge(ln_y, base + b + 1)
                    norm_stats(base + b, 0, y[:, 0, :])
                    norm_apply(base + b, 0, y[:, 0, :], b)

                batch(0, False)
                with nc.vector.Fori(1, NB - 1) as b:
                    batch(b, False)
                batch(NB - 1, True)

            TWO_PI = (6.28125, 1.9350051879882812e-03, 3.0199159819567e-07)
            MAGIC = 1.5 * 2.0 ** 23

            def reduce_angle(x, n):
                chain(nc.vector.tensor_scalar(n, x, 1.0 / 6.283185307179586, MAGIC, ALU.mult, ALU.add))
                chain(nc.vector.tensor_scalar(n, n, -MAGIC, None, ALU.add))
                for part in TWO_PI:
                    chain(nc.vector.scalar_tensor_tensor(x, n, -part, x, ALU.mult, ALU.add))

            dve.wait_ge(conv_in, 48)
            chain(nc.vector.tensor_copy(th[:, :], cols4("theta", C)))
            reduce_angle(th[:, :], thn[:, :])
            dve.wait_ge(act_chain, 1)
            chain(nc.vector.tensor_tensor(dec[:, :, :], kvec[:, :, :],
                                          e1[:, :].unsqueeze(2).to_broadcast([P, C, TAPS]), ALU.mult))
            assert link[0] == CH_DEC
            chain(nc.vector.tensor_tensor(ang[:, :, :], kvec[:, :, :],
                                          th[:, :].unsqueeze(2).to_broadcast([P, C, TAPS]), ALU.mult))
            reduce_angle(ang[:, :, :], turns[:, :, :])
            chain(nc.vector.tensor_scalar(turns[:, :, :], ang[:, :, :], -1.0, None, ALU.mult))
            chain(nc.vector.tensor_tensor(ang[:, :, :], ang[:, :, :], turns[:, :, :], ALU.max))
            chain(nc.vector.tensor_scalar(ang[:, :, :], ang[:, :, :], -1.0, 1.5707963267948966, ALU.mult, ALU.add))
            assert link[0] == CH_ANG
            dve.wait_ge(act_chain, 3)
            chain(nc.vector.tensor_tensor(taps[:, :, :], dec[:, :, :], ang[:, :, :], ALU.mult))
            chain(nc.vector.tensor_tensor(past[:, :, :], taps[:, :, 1:TAPS],
                                          cols4("init", C).unsqueeze(2).to_broadcast([P, C, NB]), ALU.mult))
            for c in range(C):
                nc.vector.tensor_tensor(acc[:, c, :].rearrange("p (n t) -> p n t", n=NB),
                                        cin[:, c, :].rearrange("p (n t) -> p n t", n=NB),
                                        past[:, c, :].unsqueeze(2).to_broadcast([P, NB, T]), ALU.add)\
                  .then_inc(conv_done, 1)
            for k in range(1, NB):
                for c in range(C):
                    dve.wait_ge(conv_done, C * (k - 1) + c + 1)
                    nc.vector.scalar_tensor_tensor(acc[:, c, k * T:TOK], cin[:, c, 0:TOK - k * T], taps[:, c, k:k + 1],
                                                   acc[:, c, k * T:TOK], ALU.mult, ALU.add).then_inc(conv_done, 1)
            for c in range(C):
                dve.wait_ge(conv_done, C * (NB - 1) + c + 1)
                nc.vector.scalar_tensor_tensor(acc[:, c, :], acc[:, c, :], 1.0, cin[:, c, :], ALU.add, ALU.mult)\
                  .then_inc(conv_done, 1)
            for i in range(2):
                keys_lo(0, 0, 0, i)
            for j in range(NKC):
                values_lo(A[0], 0, j)
            for b in range(NB):
                dve.wait_ge(ln_in, LN_CONV + b + 1)
                wait(dve, ln_x, LN_CONV + b - 1)
                nc.vector.tensor_copy(y[:, b % 2, :], ln_bank[b % 2][0:T, :]).then_inc(ln_y, 1)
                dve.wait_ge(ln_y, LN_CONV + b + 1)
                norm_stats(LN_CONV + b, b % 2, y[:, b % 2, :])
                if b >= 1:
                    norm_apply(LN_CONV + b - 1, (b - 1) % 2, y[:, (b - 1) % 2, :], b - 1)
            norm_apply(LN_CONV + NB - 1, (NB - 1) % 2, y[:, (NB - 1) % 2, :], NB - 1)
            for b in range(NB):
                transposed_lo(LN_CONV + b, b)
            attention(0, LN_ATT0)
            for b in range(NB):
                transposed_lo(LN_ATT0 + b, b)

            def norm(n, b, s, src, other):
                dve.wait_ge(ln_in, n + 1)
                dve.wait_ge(ln_x, n - 1 if s is not None else n)
                s = s or 0
                nc.vector.tensor_tensor(y[:, s, :], src, other, ALU.add).then_inc(ln_y, 1)
                dve.wait_ge(ln_y, n + 1)
                norm_stats(n, s, y[:, s, :])

            def norms(base, bank, other, before, transposed=False):
                for b in range(NB):
                    before(b)
                    norm(base + b, b, b % 2, bank(b), other(b))
                    if b >= 1:
                        norm_apply(base + b - 1, (b - 1) % 2, y[:, (b - 1) % 2, :], b - 1)
                    if transposed and b >= 3:
                        transposed_lo(base + b - 3, b - 3)
                norm_apply(base + NB - 1, (NB - 1) % 2, y[:, (NB - 1) % 2, :], NB - 1)
                if transposed:
                    for b in range(NB - 3, NB):
                        transposed_lo(base + b, b)

            for h in range(2):
                dve.wait_ge(F.p_hi, h + 1)
                sl = slice(h * HALF, (h + 1) * HALF)
                nc.vector.tensor_tensor(f_p.lo[:, sl], bank4[2 * h][:, 0:HALF], f_p.hi[:, sl], ALU.subtract)\
                  .then_inc(F.p_lo, 1)
            for u in range(2 * M):
                dve.wait_ge(F.h_act, u + 1)
                wait(dve, F.acc_mm, u - 3)
                nc.vector.tensor_copy(f_g.hi[:, u % 4, :], f_act[:, u % 4, :]).then_inc(F.h_hi, 1)
                dve.wait_ge(F.h_hi, u + 1)
                nc.vector.tensor_tensor(f_g.lo[:, u % 4, :], f_act[:, u % 4, :], f_g.hi[:, u % 4, :], ALU.subtract)\
                  .then_inc(F.h_lo, 1)
            for h in range(2):
                dve.wait_ge(F.q_hi, h + 1)
                sl = slice(h * HALF, (h + 1) * HALF)
                nc.vector.tensor_tensor(f_q.lo[:, sl], bank4[2 * h][:, 0:HALF], f_q.hi[:, sl], ALU.subtract)\
                  .then_inc(F.q_lo, 1)
            norms(LN_FFN0, lambda b: ln_bank[b % 2][0:T, :], lambda b: resid[:, b % 2, :],
                  lambda b: dve.wait_ge(ffn0_resid, b + 1), transposed=True)

            dve.wait_ge(R.tables_in, 64)
            for u in range(R_UNITS):
                dve.wait_ge(R.rot_mm, u + 1)
                wait(dve, R.rope, u - 1)
                nc.vector.tensor_tensor(sinx[:, u % 2, :].rearrange("p (b t) -> p b t", t=T),
                                        bank4b[u % 4][:, 0:HALF].rearrange("p (b t) -> p b t", t=T),
                                        stab[:, :].unsqueeze(1).to_broadcast([P, NB // 2, T]), ALU.mult)\
                  .then_inc(R.sin, 1)

            def query_blocks_lo(b):
                ts = bass.ds(b * T, T)
                dve.wait_ge(R.q_hi, b + 1)
                for j in range(G):
                    r = slice(HD * j, HD * (j + 1))
                    last = nc.vector.tensor_tensor(qbd.lo[r, :, j, :], qk[0][r, :, ts], qbd.hi[r, :, j, :],
                                                   ALU.subtract)
                last.then_inc(R.q_ready, 1)

            heads = lambda t: t.rearrange("t (h e) -> t h e", h=H)
            spread = lambda t: t[:, :].unsqueeze(2).to_broadcast([T, H, HD])

            def retention_dve(b, front, back):
                def decayed(g):
                    dve.wait_ge(R.s_mm, C * b + g + 1)
                    wait(dve, R.p_lo, C * b + g - 1)
                    nc.vector.tensor_tensor(p_raw[:, g % 2, :], bank4[g][0:T, 0:G * T],
                                            decay[:, G * g:G * (g + 1), :].rearrange("t h s -> t (h s)"), ALU.mult)\
                      .then_inc(R.decayed, 1)

                def p_lo(g):
                    dve.wait_ge(R.p_hi, C * b + g + 1)
                    nc.vector.tensor_tensor(pb.lo[:, g % 2, :], p_raw[:, g % 2, :], pb.hi[:, g % 2, :], ALU.subtract)\
                      .then_inc(R.p_lo, 1)

                if back:
                    dve.wait_ge(R.pv_mm, C * b)
                    nc.vector.tensor_reduce(gsum[:, :], heads(psO[0:T, 0:D]), AX.X, ALU.add).then_inc(R.g_sum, 1)
                    dve.wait_ge(R.g_sum, b)
                    nc.vector.tensor_scalar(gneg[:, :], gsum[:, :], -1.0 / HD, None, ALU.mult).then_inc(R.g_mean, 1)
                    dve.wait_ge(R.g_mean, b)
                    nc.vector.tensor_tensor(heads(gd[:, :]), heads(psO[0:T, 0:D]), spread(gneg), ALU.add)\
                      .then_inc(R.g_dev, 1)
                if front:
                    dve.wait_ge(R.v_hi, b + 1)
                    nc.vector.tensor_tensor(vb.lo[:, :], psT[0:T, 0:D], vb.hi[:, :], ALU.subtract).then_inc(R.v_lo, 1)
                    decayed(0)
                    decayed(1)
                if back:
                    dve.wait_ge(R.g_sq, b)
                    nc.vector.tensor_reduce(gsum2[:, :], heads(gsq[:, :]), AX.X, ALU.add).then_inc(R.g_sum2, 1)
                if front:
                    p_lo(0)
                    decayed(2)
                if back:
                    dve.wait_ge(R.g_root, b)
                    nc.vector.tensor_tensor(heads(gd[:, :]), heads(gd[:, :]), spread(groot), ALU.mult)\
                      .then_inc(R.g_norm, 1)
                if front:
                    p_lo(1)
                    decayed(3)
                if back:
                    dve.wait_ge(R.o_hi, b)
                    nc.vector.tensor_tensor(r_oT.lo[:, :, :], r_o[:, :, :], r_oT.hi[:, :, :], ALU.subtract)\
                      .then_inc(R.o_lo, 1)
                if front:
                    p_lo(2)
                    p_lo(3)
                if back:
                    n = LN_RET + b - 1
                    norm(n, b - 1, None, psT[0:T, KA:KA + D], x_res[:, b - 1, :])
                if front and not (isinstance(b, int) and b == NB - 1):
                    query_blocks_lo(b + 1)
                if back:
                    norm_apply(n, 0, y[:, 0, :], b - 1)

            query_blocks_lo(0)
            retention_dve(0, True, False)
            with nc.vector.Fori(1, NB - 1) as b:
                retention_dve(b, True, True)
            retention_dve(NB - 1, True, True)
            retention_dve(NB, False, True)
            for b in range(NB):
                transposed_lo(LN_RET + b, b)

            for i in range(2):
                keys_lo(1, 0, 0, i)
            for j in range(NKC):
                values_lo(A[1], 0, j)
            attention(1, LN_ATT1)
            for b in range(NB):
                transposed_lo(LN_ATT1 + b, b)

            def gate(i, q, first=False):
                dve.wait_ge(E.silu, 4 * i + q + 1)
                if not (first and q < 2):
                    dve.wait_ge(E.g_lo, 4 * i + q - 1)
                nc.vector.scalar_tensor_tensor(gated[:, q % 2, :], bank4b[q][:, 0:HALF],
                                               cols[:, bass.ds(2 * i + (COL_AT["w2s"] + q // 2), 1)],
                                               silu[:, q % 2, :], ALU.mult, ALU.mult).then_inc(E.gated, 1)

            def gate_parts(i, q):
                sl = (slice(None), 2 * i + q // 2, slice((q % 2) * HALF, (q % 2 + 1) * HALF))
                dve.wait_ge(E.gated, 4 * i + q + 1)
                nc.vector.tensor_copy(hid.hi[sl], gated[:, q % 2, :]).then_inc(E.g_hi, 1)
                dve.wait_ge(E.g_hi, 4 * i + q + 1)
                nc.vector.tensor_tensor(hid.lo[sl], gated[:, q % 2, :], hid.hi[sl], ALU.subtract).then_inc(E.g_lo, 1)

            def gates(i, first=False):
                for q in range(4):
                    gate(i, q, first)
                    gate_parts(i, q)

            gates(0, True)
            with nc.vector.Fori(1, M // 2) as i:
                gates(i)
            for k in range(2 * M):
                dve.wait_ge(E.conv_hi, k + 1)
                nc.vector.tensor_tensor(hid.lo[:, k % M, :], h_act[:, k % M, :], hid.hi[:, k % M, :], ALU.subtract)\
                  .then_inc(E.conv_lo, 1)
            norms(LN_FFN1, lambda b: ln_bank[b % 2][0:T, :], lambda b: x_res[:, b, :], lambda b: None)

        @block.tensor
        def _(pe):
            def keys(a, b, g, i):
                k0, kn = PIECES[i]
                wait(pe, a.k_lo, 8 * b + 2 * g + i)
                for c in range(C):
                    sl = slice(P * g, P * (g + 1))
                    mm = three(psJ[:, 0:kn], (wk.hi[:, c, sl], wk.lo[:, c, sl]),
                               (cT.hi[:, c, k0:k0 + kn], cT.lo[:, c, k0:k0 + kn]), c == 0, c == C - 1)
                mm.then_inc(a.k_mm, 1)

            def values(a, b, j):
                if j < 2:
                    wait(pe, a.exped, H * b)
                else:
                    pe.wait_ge(a.v_lo, NKC * b + j - 1)
                n, k0 = key_rows(j), KC * j
                for c in range(C):
                    mm = three(psS[j % 2][0:n, 0:D], (cT.hi[:, c, k0:k0 + n], cT.lo[:, c, k0:k0 + n]),
                               (wv.hi[:, c, :], wv.lo[:, c, :]), c == 0, c == C - 1)
                mm.then_inc(a.v_mm, 1)

            def transpose_x(n, b):
                pe.wait_ge(ln_x, n + 1)
                wait(pe, tx_lo, n - 1)
                for c in range(C):
                    mm = nc.tensor.transpose(tx_bank[n % 2][:, c * T:(c + 1) * T], x_res[:, b, c * P:(c + 1) * P],
                                             ident[0:T, 0:T])
                mm.then_inc(tx_mm, 1)

            def queries(a, w):
                for i in range(2 * C):
                    m, h = i // 2, i % 2
                    wait(pe, a.q_done, i - 3)
                    out = psS[i % 2][:, (i // 2 % 2) * KA:(i // 2 % 2) * KA + HALF]
                    for c in range(C):
                        sl, tk = slice(P * m, P * (m + 1)), slice(h * HALF, (h + 1) * HALF)
                        mm = three(out, (w.hi[:, c, sl], w.lo[:, c, sl]), (xT.hi[:, c, tk], xT.lo[:, c, tk]),
                                   c == 0, c == C - 1)
                    mm.then_inc(a.q_mm, 1)

            def attention(L, base):
                a = A[L]

                def scores(b, h):
                    g, j = divmod(h, G)
                    if h == 0:
                        pe.wait_ge(a.qs_done, b + 1)
                    if j == 0:
                        pe.wait_ge(a.k_lo, 8 * b + 2 * g + 2)
                    if h < 2:
                        pe.wait_ge(a.v_lo, NKC * (b + 1))
                    else:
                        pe.wait_ge(a.exped, H * b + h - 1)
                    rows_ = slice(HD * j, HD * (j + 1))
                    for k0, kn in PIECES:
                        mm = three(psS[h % 2][0:T, k0:k0 + kn], (qs.hi[rows_, g, :], qs.lo[rows_, g, :]),
                                   (kT.hi[rows_, g % 2, k0:k0 + kn], kT.lo[rows_, g % 2, k0:k0 + kn]), True, True)
                    mm.then_inc(a.s_mm, 1)

                def transposes(b, h):
                    pe.wait_ge(a.exped, H * b + h + 1)
                    wait(pe, a.pt_lo, 2 * (H * b + h))
                    if h == 0:
                        wait(pe, ln_y, base + b)
                    for k in range(NKC):
                        mm = nc.tensor.transpose(psT[:, KA * (k // HK) + T * (k % HK):KA * (k // HK) + T * (k % HK) + T],
                                                 p[:, h % 2, KC * k:KC * (k + 1)], ident[0:T, 0:T])
                    mm.then_inc(a.t_mm, 1)

                def weighted(b, pr):
                    pe.wait_ge(a.pt_lo, 2 * (H * b + 2 * pr + 2))
                    wait(pe, a.o_copied, H // 2 * b + pr)
                    fs = slice(2 * HD * pr, 2 * HD * (pr + 1))
                    for k in range(NKC):
                        n = key_rows(k)
                        mm = three(psO[0:2 * HD, 0:2 * T], (vv.hi[0:n, k, fs], vv.lo[0:n, k, fs]),
                                   (pT.hi[0:n, pr % 2, k, :], pT.lo[0:n, pr % 2, k, :]), k == 0, k == NKC - 1)
                    mm.then_inc(a.pv_mm, 1)

                def batch(b, last):
                    for t in range(H + 1):
                        if t < H:
                            scores(b, t)
                        if t >= 1:
                            transposes(b, t - 1)
                        g, i = t // 4 + 1, t % 4
                        if i < 2 and g < C and t < 12:
                            keys(a, b, g, i)
                        if t in (14, 15) and not last:
                            if t == 14:
                                pe.wait_ge(a.ctx_split, C * (b + 2))
                            keys(a, b + 1, 0, t - 14)
                        if t >= 3 and t % 2 == 1:
                            weighted(b, (t - 3) // 2)
                    if not last:
                        values(a, b + 1, 0)
                        values(a, b + 1, 1)
                    weighted(b, H // 2 - 1)
                    pe.wait_ge(a.rinv_done, b + 1)
                    nc.tensor.transpose(psT[:, 0:T], rinv[:, :], ident[0:T, 0:T]).then_inc(a.rt_mm, 1)
                    if not last:
                        values(a, b + 1, 2)
                    pe.wait_ge(a.rt_copied, b + 1)
                    for g in range(C):
                        mm = nc.tensor.matmul(psT[:, g * T:(g + 1) * T], sel[:, g, :], rT[:, :], start=True, stop=True)
                    mm.then_inc(a.rb_mm, 1)
                    if not last:
                        values(a, b + 1, 3)
                        values(a, b + 1, 4)
                    if isinstance(b, int) and b == 0:
                        pe.wait_ge(w_split, BLOCKS[("wo0", "wo1")[L]] + 2)
                    pe.wait_ge(a.o_lo, b + 1)
                    for c in range(C):
                        mm = three(psT[0:T, KA:KA + D], (oT.hi[:, c, :], oT.lo[:, c, :]),
                                   (wqo.hi[:, c, :], wqo.lo[:, c, :]), c == 0, c == C - 1)
                    mm.then_inc(ln_in, 1)
                    if not last:
                        values(a, b + 1, 5)

                batch(0, False)
                with nc.tensor.Fori(1, NB - 1) as b:
                    batch(b, False)
                batch(NB - 1, True)
                for b in range(NB):
                    transpose_x(base + b, b)

            pe.wait_ge(w_split, 2)
            pe.wait_ge(A[0].ctx_split, C)
            for i in range(2):
                keys(A[0], 0, 0, i)
            pe.wait_ge(w_split, 4)
            for j in range(NKC):
                values(A[0], 0, j)
            pe.wait_ge(consts_in, 80)
            for b in range(NB):
                if b == 0:
                    pe.wait_ge(conv_done, C * (NB + 1))
                wait(pe, ln_y, LN_CONV + b - 1)
                if b == 1:
                    pe.wait_ge(A[0].k_lo, 2)
                for c in range(C):
                    mm = nc.tensor.transpose(ln_bank[b % 2][0:T, c * P:(c + 1) * P], acc[:, c, b * T:(b + 1) * T],
                                             ident[:, :])
                mm.then_inc(ln_in, 1)
            for b in range(NB):
                if b == 0:
                    pe.wait_ge(A[0].v_lo, NKC)
                transpose_x(LN_CONV + b, b)
            pe.wait_ge(tx_lo, NB)
            pe.wait_ge(w_split, BLOCKS["wq0"] + 2)
            queries(A[0], wqo)
            attention(0, LN_ATT0)

            pe.wait_ge(tx_lo, LN_ATT0 + NB)
            pe.wait_ge(w_split, BLOCKS["v2"] + 1)
            for h in range(2):
                tk = slice(h * HALF, (h + 1) * HALF)
                for c in range(C):
                    mm = three(bank4[2 * h][:, 0:HALF], (u1.hi[:, c, :], u1.lo[:, c, :]),
                               (xT.hi[:, c, tk], xT.lo[:, c, tk]), c == 0, c == C - 1)
                mm.then_inc(F.p_mm, 1)
            pe.wait_ge(F.p_lo, 2)
            for u in range(2 * M + 2):
                if u < 2 * M:
                    m, h = divmod(u, 2)
                    ms, tk = slice(P * m, P * (m + 1)), slice(h * HALF, (h + 1) * HALF)
                    wait(pe, F.h_act, u - 3)
                    three(bank4b[u % 4][:, 0:HALF], (v1.hi[:, ms], v1.lo[:, ms]), (f_p.hi[:, tk], f_p.lo[:, tk]),
                          True, True).then_inc(F.h_mm, 1)
                if u >= 2:
                    m, h = divmod(u - 2, 2)
                    pe.wait_ge(F.h_lo, u - 1)
                    three(bank4[2 * h][:, 0:HALF], (u2.hi[:, m, :], u2.lo[:, m, :]),
                          (f_g.hi[:, (u - 2) % 4, :], f_g.lo[:, (u - 2) % 4, :]), m == 0, m == M - 1)\
                        .then_inc(F.acc_mm, 1)
            pe.wait_ge(F.q_lo, 2)
            for b in range(NB + 2):
                if b < NB:
                    wait(pe, ln_y, LN_FFN0 + b - 1)
                    tk = slice(b * T, (b + 1) * T)
                    three(ln_bank[b % 2][0:T, :], (f_q.hi[:, tk], f_q.lo[:, tk]), (v2.hi[:, :], v2.lo[:, :]),
                          True, True).then_inc(ln_in, 1)
                if b >= 2:
                    transpose_x(LN_FFN0 + b - 2, b - 2)

            pe.wait_ge(tx_lo, LN_FFN0 + NB)
            pe.wait_ge(w_split, BLOCKS["rk"] + 2)
            pe.wait_ge(R.tables_in, 64)
            for u in range(R_UNITS + 1):
                if u < R_UNITS:
                    m, h = u // 2 % C, u % 2
                    w = (rqo, rk)[u // (2 * C)]
                    wait(pe, R.q_raw, u - 3)
                    for c in range(C):
                        sl, tk = slice(P * m, P * (m + 1)), slice(h * HALF, (h + 1) * HALF)
                        mm = three(bank4[u % 4][:, 0:HALF], (w.hi[:, c, sl], w.lo[:, c, sl]),
                                   (xT.hi[:, c, tk], xT.lo[:, c, tk]), c == 0, c == C - 1)
                    mm.then_inc(R.q_mm, 1)
                if u >= 1:
                    v = u - 1
                    m, h = v // 2 % C, v % 2
                    pe.wait_ge(R.q_raw, v + 1)
                    wait(pe, R.sin, v - 3)
                    nc.tensor.matmul(bank4b[v % 4][:, 0:HALF], rotm[:, :],
                                     qk[v // (2 * C)][:, m, h * HALF:(h + 1) * HALF], start=True, stop=True)\
                      .then_inc(R.rot_mm, 1)

            def retention_pe(b, front, back):
                if front:
                    pe.wait_ge(R.x_ready, b + 1)
                    wait(pe, R.v_lo, b)
                    for c in range(C):
                        mm = three(psT[0:T, 0:D], (xb.hi[:, c, :], xb.lo[:, c, :]), (rv.hi[:, c, :], rv.lo[:, c, :]),
                                   c == 0, c == C - 1)
                    mm.then_inc(R.v_mm, 1)
                    pe.wait_ge(R.k_ready, b + 1)
                    pe.wait_ge(R.q_ready, b + 1)
                    for g in range(C):
                        wait(pe, R.decayed, C * b + g - C + 1)
                        three(bank4[g][0:T, 0:G * T], (kb.hi[:, g, :], kb.lo[:, g, :]),
                              (qbd.hi[:, g, :, :], qbd.lo[:, g, :, :]), True, True).then_inc(R.s_mm, 1)
                def weighted(g):
                    pe.wait_ge(R.p_lo, C * b + g + 1)
                    if g == 0:
                        wait(pe, R.g_dev, b)
                        pe.wait_ge(R.v_lo, b + 1)
                    for j in range(G):
                        hs, ts = slice(HD * (G * g + j), HD * (G * g + j + 1)), slice(T * j, T * (j + 1))
                        mm = three(psO[0:T, hs], (pb.hi[:, g % 2, ts], pb.lo[:, g % 2, ts]),
                                   (vb.hi[:, hs], vb.lo[:, hs]), True, True)
                    mm.then_inc(R.pv_mm, 1)

                if back:
                    pe.wait_ge(R.g_norm, b)
                    for c in range(C):
                        mm = nc.tensor.transpose(psJ[:, c * T:(c + 1) * T], gd[:, c * P:(c + 1) * P], ident[0:T, 0:T])
                    mm.then_inc(R.to_mm, 1)
                if front:
                    weighted(0)
                    weighted(1)
                if back:
                    pe.wait_ge(R.o_lo, b)
                    wait(pe, ln_y, LN_RET + b - 1)
                    for c in range(C):
                        mm = three(psT[0:T, KA:KA + D], (r_oT.hi[:, c, :], r_oT.lo[:, c, :]),
                                   (rqo.hi[:, c, :], rqo.lo[:, c, :]), c == 0, c == C - 1)
                    mm.then_inc(ln_in, 1)
                if front:
                    weighted(2)
                    weighted(3)

            pe.wait_ge(R.sin, R_UNITS)
            pe.wait_ge(w_split, BLOCKS["rv"] + 2)
            retention_pe(0, True, False)
            pe.wait_ge(w_split, BLOCKS["ro"] + 2)
            with nc.tensor.Fori(1, NB) as b:
                retention_pe(b, True, True)
            retention_pe(NB, False, True)
            for b in range(NB):
                transpose_x(LN_RET + b, b)

            pe.wait_ge(tx_lo, LN_RET + NB)
            pe.wait_ge(w_split, BLOCKS["wk1"] + 2)
            pe.wait_ge(A[1].ctx_split, C)
            for i in range(2):
                keys(A[1], 0, 0, i)
            pe.wait_ge(w_split, BLOCKS["wv1"] + 2)
            for j in range(NKC):
                values(A[1], 0, j)
            pe.wait_ge(A[1].v_lo, NKC)
            pe.wait_ge(w_split, BLOCKS["wq1"] + 2)
            queries(A[1], wqo)
            attention(1, LN_ATT1)

            pe.wait_ge(tx_lo, LN_ATT1 + NB)

            def gate_units(i):
                for e in range(2):
                    pe.wait_ge(w_split, 2 * i + (BLOCKS["w12"] + e + 1))
                    for h in range(2):
                        q, tk = 2 * e + h, slice(h * HALF, (h + 1) * HALF)
                        if not isinstance(i, int):
                            pe.wait_ge(E.gated, 4 * i + q - 3)
                        for k, bank in ((0, bank4[q]), (C, bank4b[q])):
                            for c in range(C):
                                ws = slice(P * (k + c), P * (k + c + 1))
                                mm = three(bank[:, 0:HALF], (fw.hi[:, e, ws], fw.lo[:, e, ws]),
                                           (xT.hi[:, c, tk], xT.lo[:, c, tk]), c == 0, c == C - 1)
                        mm.then_inc(E.w_mm, 1)

            gate_units(0)
            with nc.tensor.Fori(1, M // 2) as i:
                gate_units(i)
            pe.wait_ge(E.g_lo, 2 * M)
            pe.wait_ge(E.gated, 2 * M)
            for stage, (name, steps) in enumerate((("h1", M // 2), ("h2", M // 2), ("w3", C // 2))):
                def step(i, stage=stage, name=name):
                    for o in range(2):
                        for e in range(2):
                            pe.wait_ge(w_split, 4 * i + (BLOCKS[name] + 2 * o + e + 1))
                            if e == 0 and (stage or not isinstance(i, int)):
                                pe.wait_ge(E.act, 4 * i + (2 * M * stage + 2 * o - 2))
                            for k in range(M // 2):
                                kk = M // 2 * e + k
                                if stage and o == 0:
                                    pe.wait_ge(E.conv_lo, M * (stage - 1) + kk + 1)
                                for h in range(2):
                                    ws, tk = slice(P * k, P * (k + 1)), slice(h * HALF, (h + 1) * HALF)
                                    mm = three(bank4[2 * o + h][:, 0:HALF], (fw.hi[:, e, ws], fw.lo[:, e, ws]),
                                               (hid.hi[:, kk, tk], hid.lo[:, kk, tk]), kk == 0, kk == M - 1)
                                    if kk == M - 1:
                                        mm.then_inc(E.m_mm, 1)
                            if e == 0:
                                mm.then_inc(E.blk_used, 1)

                if stage == 0:
                    step(0)
                with nc.tensor.Fori(0 if stage else 1, steps) as i:
                    step(i)
            pe.wait_ge(E.act, 2 * (2 * M + C))
            for b in range(NB):
                wait(pe, ln_y, LN_FFN1 + b - 1)
                for c in range(C):
                    mm = nc.tensor.transpose(ln_bank[b % 2][0:T, c * P:(c + 1) * P], h_act[:, c, b * T:(b + 1) * T],
                                             ident[:, :])
                mm.then_inc(ln_in, 1)


def kernel(**inputs):
    import numpy as np
    import concourse.bacc as bacc
    from concourse.bass_utils import run_bass_kernel_spmd

    f = {k: np.asarray(v) for k, v in inputs.items()}
    feats = lambda w, n: np.ascontiguousarray(w.reshape(w.shape[0] // P, P, n).transpose(1, 0, 2))

    def halves(w):
        return np.ascontiguousarray(feats(w, D).reshape(P, 2, BLK).transpose(1, 0, 2))

    def tiles(w):
        o, i = w.shape
        return w.reshape(o // P, P, i // P, P).transpose(0, 3, 2, 1)

    def padded(w):
        out = np.zeros((1, P, BLK), w.dtype)
        out[0, :, :w.shape[1]] = w
        return out

    x = f["x"].reshape(TOK, D)
    arrays = {}
    arrays["xT"] = np.ascontiguousarray(x.T.reshape(C, P, TOK).transpose(1, 0, 2))
    arrays["ctxT"] = np.ascontiguousarray(f["ctx_1024"].reshape(NB * KEYS, D).T.reshape(C, P, NB * KEYS))
    arrays["mask"] = np.ascontiguousarray(f["mask_BxS2_ik0"])
    names = {"lmlg": "L0_attn_lmlg", "theta": "L0_attn_theta", "init": "L0_attn_last_conv_init", "bq": "L0_xattn_bq",
             "bk": "L0_xattn_bk", "bv": "L0_xattn_bv", "gnw": "L1_attn_gn_weight", "gnb": "L1_attn_gn_bias",
             "b1": "L0_ffn_b1", "w1s": "L1_ffn_w1_s", "w2s": "L1_ffn_w2_s", "h1s": "L1_ffn_h1_s",
             "h2s": "L1_ffn_h2_s", "w3s": "L1_ffn_w3_s"}
    arrays["cols"] = np.ascontiguousarray(np.concatenate([f[names[n]].reshape(k, P).T for n, k in COLUMNS], axis=1))
    for n, m in (("wk0", "L0_xattn_Wk"), ("wv0", "L0_xattn_Wv"), ("wq0", "L0_xattn_Wq"), ("wo0", "L0_xattn_Wo"),
                 ("wq1", "L1_xattn_Wq"), ("wo1", "L1_xattn_Wproj")):
        arrays[n] = halves(f[m])
    arrays["wk1"], arrays["wv1"] = halves(f["L1_xattn_Wkv"][:, :D]), halves(f["L1_xattn_Wkv"][:, D:])
    for n, m in (("rq", "Wq"), ("rk", "Wk"), ("rv", "Wv"), ("ro", "Wo")):
        arrays[n] = halves(f["L1_attn_" + m].T)
    for n, m in (("bo", "L0_xattn_bo"), ("b2", "L0_ffn_b2"), ("bproj", "L1_xattn_bproj")):
        arrays[n] = f[m].reshape(1, D)
    arrays["u1"] = padded(feats(f["L0_ffn_U1"], RANK).reshape(P, C * RANK))
    arrays["v1"] = np.ascontiguousarray(f["L0_ffn_V1"].reshape(P, 2, BLK).transpose(1, 0, 2))
    arrays["u2"] = np.ascontiguousarray(feats(f["L0_ffn_U2"], RANK).reshape(P, 2, BLK).transpose(1, 0, 2))
    arrays["v2"] = padded(f["L0_ffn_V2"])
    w1, w2 = tiles(f["L1_ffn_w1_w"]), tiles(f["L1_ffn_w2_w"])
    blocks = [np.concatenate([w1, w2], axis=2).reshape(M, P, BLK)]
    for m in ("L1_ffn_h1_w", "L1_ffn_h2_w", "L1_ffn_w3_w"):
        w = tiles(f[m])
        blocks.append(w.reshape(w.shape[0], P, 2, BLK).transpose(0, 2, 1, 3).reshape(-1, P, BLK))
    arrays["ffn"] = np.concatenate(blocks)
    arrays["ident"] = np.eye(P, dtype=np.float32)
    arrays["kvec"] = np.ascontiguousarray(np.broadcast_to(np.arange(TAPS, dtype=np.float32), (P, C, TAPS)))
    s = np.zeros((H, C, P), np.float32)
    for h in range(H):
        s[h, h // G, HD * (h % G):HD * (h % G + 1)] = 1.0
    arrays["sel"] = s
    freq = (1.0 / 10000.0 ** (np.arange(0, HD, 2, dtype=np.float32) / HD)).astype(np.float32)
    emb = np.tile(np.arange(T, dtype=np.float32)[None, :] * freq[:, None], (P // len(freq), 1))
    sign = np.where(np.arange(P) % HD < HD // 2, -1.0, 1.0).astype(np.float32)
    arrays["cos"] = np.cos(emb).astype(np.float32)
    arrays["sin"] = (np.sin(emb) * sign[:, None]).astype(np.float32)
    arrays["rotm"] = np.eye(P, dtype=np.float32)[np.arange(P) ^ (HD // 2)]
    gamma = (1.0 - 2.0 ** (-5.0 - np.arange(H, dtype=np.float32))).astype(np.float32)
    dist = np.arange(T)[None, None, :] - np.arange(T)[:, None, None]
    arrays["decay"] = np.where(dist >= 0, SCALE * gamma[None, :, None] ** np.maximum(dist, 0), 0.0).astype(np.float32)
    arrays = {n + "_dram": np.ascontiguousarray(a) for n, a in arrays.items()}

    nc = bacc.Bacc("TRN2", target_bir_lowering=False, num_devices=1)
    d = {}
    for n, a in arrays.items():
        d[n[:-5]] = nc.dram_tensor(n, a.shape, mybir.dt.from_np(a.dtype), kind="ExternalInput").ap()
    d["out"] = nc.dram_tensor("out_dram", (NB, T, D), mybir.dt.float32, kind="ExternalOutput").ap()
    decoder_kernel(nc, d)
    r = run_bass_kernel_spmd(nc, [arrays], core_ids=[0])
    return r.results[0]["out_dram"]
```

```python
import concourse.bass as bass
from concourse import mybir
from contextlib import ExitStack
from collections import namedtuple

NB, T, D = 8, 100, 512
KEYS = 722
H, HD = 16, 32
P = 128
C = D // P
TOK = NB * T
HALF = TOK // 2
G = H // C
FF = 2048
M = FF // P
EPS = 1e-5
SCALE = HD ** -0.5
BLK = 1024
KA = 512
HALVES = ((0, 362), (362, KEYS - 362))
PIECES = ((0, KA), (KA, KEYS - KA))
KC = 128
NKC = -(-KEYS // KC)
PK = NKC * KC
HK = NKC // 2
RANK = 128
TAPS = NB + 1

COLUMNS = [("lmlg", C), ("theta", C), ("init", C), ("bq", C), ("bk", C), ("bv", C), ("gnw", C), ("gnb", C),
           ("b1", M), ("w1s", M), ("w2s", M), ("h1s", M), ("h2s", M), ("w3s", C)]
COL_AT = {}
for _n, _k in COLUMNS:
    COL_AT[_n] = sum(k for _, k in COLUMNS[:len(COL_AT)])
NCOL = sum(k for _, k in COLUMNS)

LN_CONV, LN_ATT0, LN_FFN0, LN_RET, LN_ATT1, LN_FFN1 = (NB * i for i in range(6))

BLOCKS = {}
_n = 0
for _name, _k in [("wk0", 2), ("wv0", 2), ("wq0", 2), ("wo0", 2), ("u1", 1), ("v1", 2), ("u2", 2), ("v2", 1),
                  ("rq", 2), ("rk", 2), ("rv", 2), ("ro", 2), ("wk1", 2), ("wv1", 2), ("wq1", 2), ("wo1", 2),
                  ("w12", M), ("h1", 2 * M), ("h2", 2 * M), ("w3", 2 * C)]:
    BLOCKS[_name] = _n
    _n += _k


Pair = namedtuple("Pair", "hi lo")

LN_LAST = LN_FFN1
CONTEXT_AT = {10: 0, 11: 1, 13: 2, 14: 3}
CH_DEC, CH_ANG = 7, 16
MASKED = -1e38
EARLY = NB - 2
LOWEST = -3e38
FFN_PAIRS = M // 2 + 2 * M + C
FFN0_BLOCKS = [("u1", 0), ("v1", 0), ("v1", 1), ("u2", 0), ("u2", 1), ("v2", 0)]
R_UNITS = 4 * C


def key_rows(j):
    return min(KC, KEYS - j * KC)


def decoder_kernel(nc, d):
    fp32, f32r, i32 = mybir.dt.float32, mybir.dt.float32r, mybir.dt.int32
    ACT, ALU, AX = mybir.ActivationFunctionType, mybir.AluOpType, mybir.AxisListType
    top = [-(-nc.sbuf_base // 64) * 64]
    LIMIT = nc.sbuf_usable_end

    def at(name, shape, dt):
        n = 4
        for x in shape[1:]:
            n *= x
        t = nc.alloc_sbuf_tensor_at(name, shape, dt, offset=top[0])
        top[0] += -(-n // 32) * 32
        assert top[0] <= LIMIT, (name, top[0], LIMIT)
        return t

    def pair(name, shape):
        return Pair(at(name + "_hi", shape, f32r), at(name + "_lo", shape, f32r))

    ctx = ExitStack()
    with ctx:
        def sem(name):
            return ctx.enter_context(nc.semaphore(name))

        raw = at("raw", [P, 2, BLK], fp32)
        x_res = at("x_res", [T, NB, D], fp32)
        ident = at("ident", [P, P], fp32)
        cols = at("cols", [P, NCOL], fp32)
        y = at("y", [T, 2, D], fp32)
        stats = at("stats", [T, 2, 6], fp32)
        mv = at("mv", [T, 2, 2], fp32)
        veps = at("veps", [T, 2, 1], fp32)
        rstd = at("rstd", [T, 2, 1], fp32)
        mhalf = at("mhalf", [P, H], fp32)
        shared_end = top[0]
        xT = pair("xT", [P, C, TOK])
        resid = at("resid", [T, 2, D], fp32)
        rows = at("rows", [T, 3, D], fp32)
        sel = at("sel", [H, C, P], fp32)
        phase_at = top[0]

        wkv_at = top[0]
        wk, wv = pair("wk", [P, C, D]), pair("wv", [P, C, D])
        wqo_at = top[0]
        wqo = pair("wqo", [P, C, D])
        craw_at = top[0]
        ctx_raw = at("ctx_raw", [P, 2, KEYS], fp32)
        cT_at = top[0]
        cT = pair("cT", [P, C, KEYS])
        vv_at = top[0]
        vv = pair("vv", [P, NKC, D])
        kT_at = top[0]
        kT = pair("kT", [P, 2, KEYS])
        conv_at = top[0]
        top[0] = kT_at
        ctx_more = at("ctx_more", [P, 2, KEYS], fp32)
        top[0] = conv_at
        q_all = at("q_all", [P, C, TOK], fp32)
        p = at("p", [T, 2, PK], fp32)
        maskb = at("maskb", [T, KEYS], fp32)
        mask_raw = at("mask_raw", [T, KEYS], i32)
        rsum = at("rsum", [T, H], fp32)
        rinv = at("rinv", [T, P], fp32)
        nmax = at("nmax", [T, 2], fp32)
        pmax = at("pmax", [T, 2], fp32)
        rT = at("rT", [H, T], fp32)
        att_bq = at("att_bq", [P, C], fp32)
        oT = pair("oT", [P, C, T])
        top[0] = shared_end
        pT = pair("pT", [P, 2, NKC, 2 * T])
        qs = pair("qs", [P, C, T])
        oraw = at("oraw", [P, C, T], fp32)
        assert top[0] <= shared_end + 2 * 4 * C * TOK

        top[0] = conv_at
        cin = at("cin", [P, C, TOK], fp32)
        small = lambda n, *s: at(n, [P, *s], fp32)
        e1, th, thn = small("e1", C), small("th", C), small("thn", C)
        kvec, turns, ang, dec, taps = (small(n, C, TAPS) for n in ("kvec", "turns", "ang", "dec", "taps"))
        past = small("past", C, NB)
        top[0] = shared_end
        acc = at("acc", [P, C, TOK], fp32)

        top[0] = wkv_at
        v1, u2 = pair("v1", [P, FF]), pair("u2", [P, M, RANK])
        assert top[0] <= wqo_at
        top[0] = cT_at
        u1, v2 = pair("u1", [P, C, RANK]), pair("v2", [P, D])
        f_p, f_q = pair("f_p", [P, TOK]), pair("f_q", [P, TOK])
        assert top[0] <= vv_at
        top[0] = vv_at
        f_act, f_g = at("f_act", [P, 4, HALF], fp32), pair("f_g", [P, 4, HALF])
        assert top[0] <= kT_at

        top[0] = wkv_at
        qk = [at("q_rope", [P, C, TOK], fp32), at("k_rope", [P, C, TOK], fp32)]
        kb, xb = pair("kb", [P, C, T]), pair("xb", [P, C, T])
        assert top[0] <= wqo_at
        top[0] = wqo_at
        rqo = pair("rqo", [P, C, D])
        assert top[0] <= craw_at
        ctab, stab = at("ctab", [P, T], fp32), at("stab", [P, T], fp32)
        rotm = at("rotm", [P, P], fp32)
        assert top[0] <= cT_at
        top[0] = cT_at
        qbd = pair("qbd", [P, C, G, T])
        vb = pair("vb", [T, D])
        r_o, r_oT = at("r_o", [P, C, T], fp32), pair("r_oT", [P, C, T])
        assert top[0] <= vv_at
        top[0] = vv_at
        decay = at("decay", [T, H, T], fp32)
        p_raw, pb = at("p_raw", [T, 2, G * T], fp32), pair("pb", [T, 2, G * T])
        gd, gsq = at("gd", [T, D], fp32), at("gsq", [T, D], fp32)
        gsum, gneg, gvar = (at(n, [T, H], fp32) for n in ("gsum", "gneg", "gvar"))
        gsum2, geps, groot = (at(n, [T, H], fp32) for n in ("gsum2", "geps", "groot"))
        assert top[0] <= kT_at
        top[0] = kT_at
        rk, rv = pair("rk", [P, C, D]), pair("rv", [P, C, D])
        cosx, sinx = at("cosx", [P, 2, HALF], fp32), at("sinx", [P, 2, HALF], fp32)

        top[0] = shared_end
        h_act = at("h_act", [P, M, TOK], fp32)
        hid = pair("hid", [P, M, TOK])
        fw = pair("fw", [P, 2, BLK])
        silu, gated = at("silu", [P, 2, HALF], fp32), at("gated", [P, 2, HALF], fp32)

        def ps(name, n):
            return ctx.enter_context(nc.psum_tensor(name, [P, n], fp32))

        psS = [ps("psS0", 2 * KA), ps("psS1", 2 * KA)]
        psT = ps("psT", 2 * KA)
        psO = ps("psO", KA)
        psJ = ps("psJ", KA)
        ln_bank = [psO[:, :], psJ[:, :]]
        bank4 = [t[:, i:i + KA] for i in (0, KA) for t in psS]
        tx_bank = bank4
        bank4b = [psT[:, 0:KA], psT[:, KA:2 * KA], psO[:, :], psJ[:, :]]

        consts_in, conv_in, x_in, small_ready = sem("consts_in"), sem("conv_in"), sem("x_in"), sem("small_ready")
        raw_in = [sem("raw_in0"), sem("raw_in1")]
        w_hi, w_split = sem("w_hi"), sem("w_split")
        dve_chain, act_chain = sem("dve_chain"), sem("act_chain")
        ln_in, ln_y, ln_stat, ln_mv = sem("ln_in"), sem("ln_y"), sem("ln_stat"), sem("ln_mv")
        ln_eps, ln_rstd, ln_x = sem("ln_eps"), sem("ln_rstd"), sem("ln_x")
        tx_mm, tx_hi, tx_lo = sem("tx_mm"), sem("tx_hi"), sem("tx_lo")
        conv_done = sem("conv_done")
        out_done = sem("out_done")
        ffn0_resid = sem("ffn0_resid")

        def sems(prefix, names):
            return namedtuple("Sems", names)(*[sem(prefix + n) for n in names.split()])

        A = [sems(f"att{L}_", "ctx_in0 ctx_in1 more_in ctx_hi ctx_split k_mm k_hi k_lo v_mm v_hi v_lo q_mm q_done "
                              "qs_hi qs_done s_mm maxed exped t_mm pt_hi pt_lo pv_mm o_copied rinv_done rt_mm "
                              "rt_copied rb_mm o_scaled "
                              "o_biased o_hi o_lo resid_done mask_in mask_done pad_done") for L in range(2)]
        F = sems("ffn0_", "p_mm p_hi p_lo h_mm h_act h_hi h_lo acc_mm q_hi q_lo")
        R = sems("ret_", "tables_in q_mm q_raw rot_mm cos sin rope zero kb_hi k_ready x_ready q_hi q_ready v_mm v_hi "
                         "v_lo s_mm decayed p_hi p_lo pv_mm g_sum g_mean g_dev g_sq g_sum2 g_eps g_root g_norm to_mm "
                         "o_affine o_hi o_lo")
        E = sems("ffn1_", "blk_used w_mm silu gated g_hi g_lo m_mm act conv_hi conv_lo")
        mx_raw, apart = sem("mx_raw"), sem("apart")

        def wait(eng, s, v):
            if isinstance(v, int) and v <= 0:
                return
            eng.wait_ge(s, v)

        def wait_apart(eng, s, v):
            wait(eng, s, v)
            if not isinstance(v, int):
                eng.sem_inc(apart, 1)

        def block_parts(name, i, w):
            n = BLOCKS[name] + i
            tall = w.hi.shape[1] if len(w.hi.shape) == 3 else 1
            wide = min(BLK, w.hi.shape[-1] * tall)
            src = raw[:, n % 2, 0:wide]
            if len(w.hi.shape) == 2:
                sl = slice(wide * i, wide * (i + 1))
                return w.hi[:, sl], w.lo[:, sl], src
            k = wide // w.hi.shape[-1]
            sl = slice(k * i, k * (i + 1))
            return w.hi[:, sl, :], w.lo[:, sl, :], src.rearrange("p (a b) -> p a b", a=k)

        FFN0_W = {"u1": u1, "v1": v1, "u2": u2, "v2": v2}

        def three(out, st, mv_, first, last, n=None):
            nc.tensor.matmul(out, st[0], mv_[0], start=first, stop=False)
            nc.tensor.matmul(out, st[0], mv_[1], start=False, stop=False)
            return nc.tensor.matmul(out, st[1], mv_[0], start=False, stop=last)

        def col(name, c):
            return cols[:, COL_AT[name] + c:COL_AT[name] + c + 1]

        def cols4(name, n):
            return cols[:, COL_AT[name]:COL_AT[name] + n]

        block = ctx.enter_context(nc.Block())

        @block.sync
        def _(sp):
            def blocks(name, k0, k):
                for i in range(k0, k0 + k):
                    n = BLOCKS[name] + i
                    wait(sp, w_split, n - 1)
                    sp.dma_start(raw[:, n % 2, :], d[name][i]).then_inc(raw_in[n % 2], 16)

            def context(a, b, cs):
                for c in cs:
                    wait(sp, a.ctx_split, 4 * b + c - 1)
                    sp.dma_start(ctx_raw[:, c % 2, :], d["ctxT"][c, :, bass.ds(b * KEYS, KEYS)])\
                      .then_inc((a.ctx_in0, a.ctx_in1)[c % 2], 16)

            def context_more(a):
                for c in range(2, C):
                    sp.dma_start(ctx_more[:, c % 2, :], d["ctxT"][c, :, 0:KEYS]).then_inc(a.more_in, 16)

            def attention_loads(L):
                a = A[L]
                if L == 1:
                    with nc.sync.Fori(1, NB) as b:
                        context(a, b, range(C))
                        sp.wait_ge(a.mask_done, b)
                        sp.dma_start(mask_raw[:, :], d["mask"][bass.ds(b, 1), :].broadcast_to([T, KEYS]))\
                          .then_inc(a.mask_in, 16)
                else:
                    with nc.sync.Fori(1, NB) as b:
                        context(a, b, range(C))

            sp.dma_start(cols[:, :], d["cols"]).then_inc(conv_in, 16)
            sp.dma_start(kvec[:, :, :], d["kvec"]).then_inc(conv_in, 16)
            blocks("wk0", 0, 2)
            context(A[0], 0, (0,))
            sp.dma_start(cin[:, :, :], d["xT"]).then_inc(x_in, 16)
            context(A[0], 0, (1,))
            context_more(A[0])
            sp.dma_start(ident[:, :], d["ident"]).then_inc(consts_in, 16)
            sp.dma_start(sel[:, :, :], d["sel"]).then_inc(consts_in, 16)
            for i, n in enumerate(("bo", "b2", "bproj")):
                sp.dma_start(rows[:, i, :], d[n][:, :].broadcast_to([T, D])).then_inc(consts_in, 16)
            blocks("wv0", 0, 2)
            blocks("wq0", 0, 2)
            blocks("wo0", 0, 2)
            attention_loads(0)
            for n, k in (("u1", 1), ("v1", 2), ("u2", 2), ("v2", 1), ("rq", 2), ("rk", 2), ("rv", 2)):
                blocks(n, 0, k)
            sp.wait_ge(F.h_mm, 2 * M)
            sp.wait_ge(F.acc_mm, 2 * M)
            for t, n in ((ctab, "cos"), (stab, "sin"), (rotm, "rotm"), (decay, "decay")):
                sp.dma_start(t[:], d[n]).then_inc(R.tables_in, 16)
            blocks("ro", 0, 2)
            sp.wait_ge(R.rope, R_UNITS)
            context(A[1], 0, (0, 1))
            context_more(A[1])
            sp.dma_start(mask_raw[:, :], d["mask"][0:1, :].broadcast_to([T, KEYS])).then_inc(A[1].mask_in, 16)
            for n in ("wk1", "wv1", "wq1"):
                blocks(n, 0, 2)
            blocks("wo1", 0, 2)
            attention_loads(1)
            with nc.sync.Fori(0, FFN_PAIRS) as i:
                for e in range(2):
                    sp.wait_ge(w_split, 2 * i + (BLOCKS["w12"] + e - 1))
                    sp.dma_start(raw[:, e, :], d["ffn"][bass.ds(2 * i + e, 1)].rearrange("a p n -> (a p) n"))\
                      .then_inc(raw_in[e], 16)

            for b in range(NB):
                sp.wait_ge(ln_x, LN_LAST + b + 1)
                sp.dma_start(d["out"][b], x_res[:, b, :]).then_inc(out_done, 16)
            sp.wait_ge(out_done, 16 * NB)

        @block.gpsimd
        def _(pool):
            def split_lo(name, i, w):
                n = BLOCKS[name] + i
                hi, lo, src = block_parts(name, i, w)
                pool.wait_ge(w_hi, n + 1)
                nc.gpsimd.tensor_tensor(lo, src, hi, ALU.subtract).then_inc(w_split, 1)

            def context_lo(a, b, c):
                wait_apart(pool, a.ctx_hi, 4 * b + c + 1)
                src = ctx_more if isinstance(b, int) and b == 0 and c >= 2 else ctx_raw
                nc.gpsimd.tensor_tensor(cT.lo[:, c, :], src[:, c % 2, :], cT.hi[:, c, :], ALU.subtract)\
                  .then_inc(a.ctx_split, 1)

            def queries_lo(a, b):
                wait_apart(pool, a.qs_hi, b + 1)
                nc.gpsimd.tensor_tensor(qs.lo[:, :, :], q_all[:, :, bass.ds(b * T, T)], qs.hi[:, :, :], ALU.subtract)\
                  .then_inc(a.qs_done, 1)

            def mask_bias(a, b):
                wait_apart(pool, a.mask_in, 16 * (b + 1))
                wait_apart(pool, a.maxed, H * b)
                nc.gpsimd.tensor_scalar(maskb[:, :], mask_raw[:, :], 0.0, MASKED, ALU.is_equal, ALU.mult)\
                  .then_inc(a.mask_done, 1)

            def root(n, s):
                wait_apart(pool, ln_mv, n + 1)
                nc.gpsimd.tensor_scalar(veps[:, s, :], mv[:, s, 1:2], EPS, None, ALU.add).then_inc(ln_eps, 1)
                wait_apart(pool, ln_eps, n + 1)
                nc.gpsimd.tensor_tensor(rstd[:, s, :], veps[:, s, :], mhalf[0:T, 0:1], ALU.pow).then_inc(ln_rstd, 1)

            def add_bias(row, b, s, n, done):
                wait_apart(pool, ln_y, n - (0 if s is None else 1))
                s = s or 0
                nc.gpsimd.tensor_tensor(resid[:, s, :], x_res[:, b, :],
                                        rows[:, row, :], ALU.add).then_inc(done, 1)

            def attention(L, row, base):
                a = A[L]

                def batch(b, last, first=False):
                    if not first:
                        root(base + b - 1, 0)
                    if not last:
                        for c in range(C):
                            context_lo(a, b + 1, c)
                        queries_lo(a, b + 1)
                        if L == 1:
                            mask_bias(a, b + 1)
                    elif L == 0:
                        for n, i in FFN0_BLOCKS:
                            split_lo(n, i, FFN0_W[n])
                    add_bias(row, b, None, base + b, a.resid_done)

                batch(0, False, first=True)
                with nc.gpsimd.Fori(1, NB - 1) as b:
                    batch(b, False)
                batch(NB - 1, True)
                root(base + NB - 1, 0)

            nc.gpsimd.memset(mhalf[:, :], -0.5).then_inc(small_ready, 1)
            for i in range(2):
                split_lo("wk0", i, wk)
            for c in range(C):
                context_lo(A[0], 0, c)
            for i in range(2):
                split_lo("wv0", i, wv)
            for i in range(2):
                split_lo("wq0", i, wqo)
            pool.wait_ge(small_ready, 1)
            for b in range(NB):
                root(LN_CONV + b, b % 2)
            pool.wait_ge(conv_done, C * (NB + 1))
            nc.gpsimd.memset(p[:, :, KEYS:PK], 0.0).then_inc(A[0].pad_done, 1)
            nc.gpsimd.memset(rinv[:, H:P], 0.0).then_inc(A[0].pad_done, 1)
            queries_lo(A[0], 0)
            for i in range(2):
                split_lo("wo0", i, wqo)
            attention(0, 0, LN_ATT0)

            for n, w in (("rq", rqo), ("rk", rk), ("rv", rv)):
                for i in range(2):
                    split_lo(n, i, w)
            for b in range(NB):
                add_bias(1, b, b % 2, LN_FFN0 + b, ffn0_resid)
                root(LN_FFN0 + b, b % 2)

            wait_apart(pool, F.q_lo, 2)
            nc.gpsimd.memset(qbd.hi[:].bitcast(fp32), 0.0).then_inc(R.zero, 1)
            nc.gpsimd.memset(qbd.lo[:].bitcast(fp32), 0.0).then_inc(R.zero, 1)
            wait_apart(pool, R.tables_in, 64)

            def rope_sum(u):
                m, h = u // 2 % C, u % 2
                wait_apart(pool, R.sin, u + 1)
                wait_apart(pool, R.cos, u + 1)
                nc.gpsimd.tensor_tensor(qk[u // (2 * C)][:, m, h * HALF:(h + 1) * HALF], cosx[:, u % 2, :],
                                        sinx[:, u % 2, :], ALU.add).then_inc(R.rope, 1)

            for u in range(R_UNITS):
                m, h = u // 2 % C, u % 2
                wait_apart(pool, R.q_raw, u + 1)
                wait_apart(pool, R.rope, u - 1)
                nc.gpsimd.tensor_tensor(cosx[:, u % 2, :].rearrange("p (b t) -> p b t", t=T),
                                        qk[u // (2 * C)][:, m, h * HALF:(h + 1) * HALF]
                                        .rearrange("p (b t) -> p b t", t=T),
                                        ctab[:, :].unsqueeze(1).to_broadcast([P, NB // 2, T]), ALU.mult)\
                  .then_inc(R.cos, 1)
                if u >= 1:
                    rope_sum(u - 1)
            rope_sum(R_UNITS - 1)
            for i in range(2):
                split_lo("ro", i, rqo)

            def keys_lo(b):
                wait_apart(pool, R.kb_hi, b + 1)
                nc.gpsimd.tensor_tensor(kb.lo[:, :, :], qk[1][:, :, bass.ds(b * T, T)], kb.hi[:, :, :], ALU.subtract)\
                  .then_inc(R.k_ready, 1)

            def retention_pool(b, prev=True, before=True, after=True):
                if prev:
                    wait_apart(pool, R.g_dev, b)
                    nc.gpsimd.tensor_tensor(gsq[:, :], gd[:, :], gd[:, :], ALU.mult).then_inc(R.g_sq, 1)
                    wait_apart(pool, R.g_sum2, b)
                    nc.gpsimd.tensor_scalar(geps[:, :], gsum2[:, :], 1.0 / HD, EPS, ALU.mult, ALU.add)\
                      .then_inc(R.g_eps, 1)
                    wait_apart(pool, R.g_eps, b)
                    nc.gpsimd.tensor_tensor(groot[:, :], geps[:, :], mhalf[0:T, :], ALU.pow).then_inc(R.g_root, 1)
                if before:
                    root(LN_RET + b - 2, 0)
                if after:
                    keys_lo(b + 1)

            keys_lo(0)
            retention_pool(0, prev=False, before=False)
            retention_pool(1, before=False)
            with nc.gpsimd.Fori(2, NB - 1) as b:
                retention_pool(b)
            retention_pool(NB - 1, after=False)
            retention_pool(NB, after=False)
            for i in range(2):
                split_lo("wk1", i, wk)
            retention_pool(NB + 1, prev=False, after=False)

            for i in range(2):
                split_lo("wv1", i, wv)
            for i in range(2):
                split_lo("wq1", i, wqo)
            pool.wait_ge(ln_in, LN_RET + NB)
            mask_bias(A[1], 0)
            nc.gpsimd.memset(p[:, :, KEYS:PK], 0.0).then_inc(A[1].pad_done, 1)
            nc.gpsimd.memset(rinv[:, H:P], 0.0).then_inc(A[1].pad_done, 1)
            queries_lo(A[1], 0)
            for i in range(2):
                split_lo("wo1", i, wqo)
            attention(1, 2, LN_ATT1)

            def ffn_lo(i):
                for e in range(2):
                    wait_apart(pool, w_hi, 2 * i + (BLOCKS["w12"] + e + 1))
                    nc.gpsimd.tensor_tensor(fw.lo[:, e, :], raw[:, e, :], fw.hi[:, e, :], ALU.subtract)\
                      .then_inc(w_split, 1)

            ffn_lo(0)
            with nc.gpsimd.Fori(1, FFN_PAIRS) as i:
                ffn_lo(i)
            for b in range(NB):
                root(LN_FFN1 + b, b % 2)

        @block.scalar
        def _(act):
            def transposed_hi(n, b):
                act.wait_ge(tx_mm, n + 1)
                nc.scalar.activation(xT.hi[:, :, b * T:(b + 1) * T],
                                     tx_bank[n % 4][:, 0:C * T].rearrange("p (c t) -> p c t", c=C), ACT.Copy)\
                  .then_inc(tx_hi, 1)

            def weights_hi(name, i, w):
                n = BLOCKS[name] + i
                hi, _, src = block_parts(name, i, w)
                act.wait_ge(raw_in[n % 2], 16 * (n // 2 + 1))
                nc.scalar.activation(hi, src, ACT.Copy).then_inc(w_hi, 1)

            def context_hi(a, b, c):
                src = ctx_raw
                if not isinstance(b, int) or b:
                    act.wait_ge((a.ctx_in0, a.ctx_in1)[c % 2], 16 * (2 * b + c // 2))
                elif c < 2:
                    act.wait_ge((a.ctx_in0, a.ctx_in1)[c], 16)
                else:
                    act.wait_ge(a.more_in, 32)
                    src = ctx_more
                if c == 0:
                    wait(act, a.k_mm, 2 * C * b)
                nc.scalar.activation(cT.hi[:, c, :], src[:, c % 2, :], ACT.Copy).then_inc(a.ctx_hi, 1)

            def queries_hi(a, b):
                wait_apart(act, a.s_mm, H * b)
                nc.scalar.activation(qs.hi[:, :, :], q_all[:, :, bass.ds(b * T, T)], ACT.Copy).then_inc(a.qs_hi, 1)

            def queries(a, bias):
                for i in range(2 * C):
                    m, h = i // 2, i % 2
                    act.wait_ge(a.q_mm, i + 1)
                    src = psS[i % 2][:, (i // 2 % 2) * KA:(i // 2 % 2) * KA + HALF]
                    dst = q_all[:, m, h * HALF:(h + 1) * HALF]
                    if bias:
                        nc.scalar.activation(dst, src, ACT.Identity, bias=att_bq[:, m:m + 1], scale=SCALE)\
                          .then_inc(a.q_done, 1)
                    else:
                        nc.scalar.activation(dst, src, ACT.Copy, scale=SCALE).then_inc(a.q_done, 1)

            def keys_hi(L, b, g, i):
                a = A[L]
                k0, kn = HALVES[i]
                act.wait_ge(a.k_mm, 8 * b + 2 * g + i + 1)
                dst = kT.hi[:, g % 2, k0:k0 + kn]
                if L == 0:
                    nc.scalar.activation(dst, psJ[:, 0:kn], ACT.Identity, bias=col("bk", g)).then_inc(a.k_hi, 1)
                else:
                    nc.scalar.activation(dst, psJ[:, 0:kn], ACT.Copy).then_inc(a.k_hi, 1)

            def values_hi(a, b, j):
                act.wait_ge(a.v_mm, NKC * b + j + 1)
                if j == 0:
                    wait(act, a.pv_mm, H // 2 * b)
                n = key_rows(j)
                nc.scalar.activation(vv.hi[0:n, j, :], psS[j % 2][0:n, 0:D], ACT.Copy).then_inc(a.v_hi, 1)

            def attention(L):
                a = A[L]

                def exps(b, h):
                    act.wait_ge(a.maxed, H * b + h + 1)
                    nc.scalar.activation(p[:, h % 2, 0:KEYS], psS[h % 2][0:T, 0:KEYS], ACT.Exp,
                                         bias=nmax[:, h % 2:h % 2 + 1], accum_out=rsum[:, h:h + 1]).then_inc(a.exped, 1)

                def probs_hi(b, h):
                    act.wait_ge(a.t_mm, H * b + h + 1)
                    pr = h // 2
                    if h % 2 == 0:
                        wait(act, a.pv_mm, H // 2 * b + pr - 1)
                    for i in range(2):
                        nc.scalar.activation(
                            pT.hi[:, pr % 2, HK * i:HK * i + HK, (h % 2) * T:(h % 2 + 1) * T],
                            psT[:, KA * i:KA * i + HK * T].rearrange("p (k t) -> p k t", k=HK), ACT.Copy)\
                          .then_inc(a.pt_hi, 1)

                def batch(b, last):
                    for t in range(H + 1):
                        if t >= 1:
                            probs_hi(b, t - 1)
                        if t < H:
                            exps(b, t)
                        g, i = t // 4 + 1, t % 4
                        if i < 2 and g < C and t < 12:
                            keys_hi(L, b, g, i)
                        if t >= H - 1 and not last:
                            keys_hi(L, b + 1, 0, t - H + 1)
                        if t in CONTEXT_AT and not last:
                            context_hi(a, b + 1, CONTEXT_AT[t])
                        if L == 0 and last and 10 <= t < 10 + len(FFN0_BLOCKS):
                            if t == 10:
                                act.wait_ge(a.v_mm, NKC * NB)
                                act.wait_ge(a.k_mm, 2 * C * NB)
                            n, i = FFN0_BLOCKS[t - 10]
                            weights_hi(n, i, FFN0_W[n])
                    if not last:
                        queries_hi(a, b + 1)
                        values_hi(a, b + 1, 0)
                        values_hi(a, b + 1, 1)
                    act.wait_ge(a.rt_mm, b + 1)
                    nc.scalar.activation(rT[:, :], psT[0:H, 0:T], ACT.Copy).then_inc(a.rt_copied, 1)
                    if not last:
                        values_hi(a, b + 1, 2)
                        values_hi(a, b + 1, 3)
                    act.wait_ge(a.o_biased if L == 0 else a.o_scaled, b + 1)
                    nc.scalar.activation(oT.hi[:, :, :], oraw[:, :, :], ACT.Copy).then_inc(a.o_hi, 1)
                    if not last:
                        values_hi(a, b + 1, 4)
                        values_hi(a, b + 1, 5)

                if L == 0:
                    act.wait_ge(A[0].pad_done, 2)
                batch(0, False)
                with nc.scalar.Fori(1, NB - 1) as b:
                    batch(b, False)
                batch(NB - 1, True)

            act.wait_ge(conv_in, 32)
            nc.scalar.activation(e1[:, :], cols4("lmlg", C), ACT.Exp).then_inc(act_chain, 1)
            for i in range(2):
                weights_hi("wk0", i, wk)
            act.wait_ge(dve_chain, CH_DEC)
            nc.scalar.activation(dec[:, :, :], dec[:, :, :], ACT.Exp, scale=-1.0).then_inc(act_chain, 1)
            context_hi(A[0], 0, 0)
            act.wait_ge(dve_chain, CH_ANG)
            nc.scalar.activation(ang[:, :, :], ang[:, :, :], ACT.Sin).then_inc(act_chain, 1)
            for c in range(1, C):
                context_hi(A[0], 0, c)
            for i in range(2):
                weights_hi("wv0", i, wv)
            for i in range(2):
                keys_hi(0, 0, 0, i)
            for i in range(2):
                weights_hi("wq0", i, wqo)
            for j in range(NKC):
                values_hi(A[0], 0, j)
            for b in range(NB):
                act.wait_ge(ln_in, LN_CONV + b + 1)
                wait(act, ln_x, LN_CONV + b - 1)
                nc.scalar.activation(y[:, b % 2, :], ln_bank[b % 2][0:T, :], ACT.Copy).then_inc(ln_y, 1)
            for b in range(NB):
                transposed_hi(LN_CONV + b, b)
            act.wait_ge(tx_lo, NB)
            nc.scalar.activation(att_bq[:, :], cols4("bq", C), ACT.Copy, scale=SCALE).then_inc(act_chain, 1)
            act.wait_ge(act_chain, 4)
            queries(A[0], True)
            act.wait_ge(A[0].q_done, 2 * C)
            queries_hi(A[0], 0)
            for i in range(2):
                weights_hi("wo0", i, wqo)
            attention(0)
            act.wait_ge(ln_in, LN_ATT0 + NB)
            for i in range(2):
                weights_hi("rq", i, rqo)
            for b in range(NB):
                transposed_hi(LN_ATT0 + b, b)
            for i in range(2):
                weights_hi("rk", i, rk)

            for h in range(2):
                act.wait_ge(F.p_mm, h + 1)
                nc.scalar.activation(f_p.hi[:, h * HALF:(h + 1) * HALF], bank4[2 * h][:, 0:HALF], ACT.Copy)\
                  .then_inc(F.p_hi, 1)
            for u in range(2 * M):
                act.wait_ge(F.h_mm, u + 1)
                wait(act, F.h_lo, u - 3)
                nc.scalar.activation(f_act[:, u % 4, :], bank4b[u % 4][:, 0:HALF], ACT.Gelu_apprx_tanh,
                                     bias=col("b1", u // 2)).then_inc(F.h_act, 1)
                if u in (8, 16):
                    weights_hi("rv", u // 8 - 1, rv)
            for h in range(2):
                act.wait_ge(F.acc_mm, 2 * M - 1 + h)
                nc.scalar.activation(f_q.hi[:, h * HALF:(h + 1) * HALF], bank4[2 * h][:, 0:HALF], ACT.Copy)\
                  .then_inc(F.q_hi, 1)
            for b in range(NB):
                transposed_hi(LN_FFN0 + b, b)

            for u in range(R_UNITS):
                m, h = u // 2 % C, u % 2
                act.wait_ge(R.q_mm, u + 1)
                nc.scalar.activation(qk[u // (2 * C)][:, m, h * HALF:(h + 1) * HALF], bank4[u % 4][:, 0:HALF],
                                     ACT.Copy).then_inc(R.q_raw, 1)

            def operands_hi(b):
                ts = bass.ds(b * T, T)
                wait_apart(act, R.v_mm, b)
                nc.scalar.activation(xb.hi[:, :, :], xT.hi[:, :, ts], ACT.Copy)
                nc.scalar.activation(xb.lo[:, :, :], xT.lo[:, :, ts], ACT.Copy).then_inc(R.x_ready, 1)
                wait_apart(act, R.s_mm, C * b)
                for j in range(G):
                    r = slice(HD * j, HD * (j + 1))
                    last = nc.scalar.activation(qbd.hi[r, :, j, :], qk[0][r, :, ts], ACT.Copy)
                last.then_inc(R.q_hi, 1)
                nc.scalar.activation(kb.hi[:, :, :], qk[1][:, :, ts], ACT.Copy).then_inc(R.kb_hi, 1)

            def probs_hi(b, g):
                act.wait_ge(R.decayed, C * b + g + 1)
                wait(act, R.pv_mm, C * b + g - 1)
                nc.scalar.activation(pb.hi[:, g % 2, :], p_raw[:, g % 2, :], ACT.Copy).then_inc(R.p_hi, 1)

            def ffn_hi(i, e):
                act.wait_ge(raw_in[e], 16 * i + 16 * (BLOCKS["w12"] // 2 + 1))
                nc.scalar.activation(fw.hi[:, e, :], raw[:, e, :], ACT.Copy).then_inc(w_hi, 1)

            def retention_values_hi(b):
                act.wait_ge(R.v_mm, b + 1)
                wait(act, R.pv_mm, C * b)
                nc.scalar.activation(vb.hi[:, :], psT[0:T, 0:D], ACT.Copy).then_inc(R.v_hi, 1)

            def retention_act(b, cur=True, prev=True, after=True):
                if cur:
                    probs_hi(b, 0)
                    probs_hi(b, 1)
                if after:
                    operands_hi(b + 1)
                if cur:
                    probs_hi(b, 2)
                    probs_hi(b, 3)
                if prev:
                    act.wait_ge(R.to_mm, b)
                    wait(act, R.o_lo, b - 1)
                    for c in range(C):
                        last = nc.scalar.activation(r_o[:, c, :], psJ[:, c * T:(c + 1) * T], ACT.Identity,
                                                    bias=col("gnb", c), scale=col("gnw", c))
                    last.then_inc(R.o_affine, 1)
                    act.wait_ge(R.o_affine, b)
                    nc.scalar.activation(r_oT.hi[:, :, :], r_o[:, :, :], ACT.Copy).then_inc(R.o_hi, 1)
                if after:
                    retention_values_hi(b + 1)

            act.wait_ge(R.rope, R_UNITS)
            act.wait_ge(R.zero, 2)
            operands_hi(0)
            for i in range(2):
                weights_hi("ro", i, rqo)
            retention_values_hi(0)
            retention_act(0, prev=False)
            retention_act(1)
            with nc.scalar.Fori(2, NB - 1) as b:
                retention_act(b)
            retention_act(NB - 1, after=False)
            for b in range(EARLY):
                transposed_hi(LN_RET + b, b)
            for i in range(2):
                weights_hi("wk1", i, wk)
            for c in range(C):
                context_hi(A[1], 0, c)
            retention_act(NB, cur=False, after=False)
            for i in range(2):
                weights_hi("wv1", i, wv)

            for i in range(2):
                keys_hi(1, 0, 0, i)
            for b in range(EARLY, NB):
                transposed_hi(LN_RET + b, b)
            for i in range(2):
                weights_hi("wq1", i, wqo)
            for j in range(NKC):
                values_hi(A[1], 0, j)
            queries(A[1], False)
            act.wait_ge(A[1].q_done, 2 * C)
            queries_hi(A[1], 0)
            for i in range(2):
                weights_hi("wo1", i, wqo)
            attention(1)
            ffn_hi(0, 0)
            ffn_hi(0, 1)
            for b in range(NB):
                transposed_hi(LN_ATT1 + b, b)

            def silus(i):
                for q in range(4):
                    act.wait_ge(E.w_mm, 4 * i + q + 1)
                    wait_apart(act, E.gated, 4 * i + (q - 1))
                    nc.scalar.activation(silu[:, q % 2, :], bank4[q][:, 0:HALF], ACT.Silu,
                                         scale=cols[:, bass.ds(2 * i + (COL_AT["w1s"] + q // 2), 1)])\
                      .then_inc(E.silu, 1)
                    if q % 2:
                        ffn_hi(i + 1, q // 2)

            silus(0)
            with nc.scalar.Fori(1, M // 2) as i:
                silus(i)
            for stage, (name, steps, func) in enumerate((("h1s", M, ACT.Gelu), ("h2s", M, ACT.Gelu),
                                                         ("w3s", C, ACT.Copy))):
                if stage:
                    act.wait_ge(E.m_mm, 2 * M * stage)
                    act.wait_ge(E.act, 2 * M * stage)
                    for k in range(M):
                        nc.scalar.activation(hid.hi[:, k, :], h_act[:, k, :], ACT.Copy).then_inc(E.conv_hi, 1)

                def two_chunks(i, last=False, stage=stage, name=name, func=func):
                    for o in range(2):
                        ahead = not (last and o == 1)
                        if ahead:
                            act.wait_ge(E.blk_used, 2 * i + (M * stage + o + 1))
                            ffn_hi(2 * i + (M // 2 + M * stage + o + 1), 0)
                        for h in range(2):
                            wait_apart(act, E.m_mm, 4 * i + (2 * M * stage + 2 * o + h + 1))
                            if stage:
                                act.wait_ge(E.conv_lo, M * stage)
                            nc.scalar.activation(h_act[:, 2 * i + o, h * HALF:(h + 1) * HALF],
                                                 bank4[2 * o + h][:, 0:HALF], func,
                                                 scale=cols[:, bass.ds(2 * i + (COL_AT[name] + o), 1)])\
                              .then_inc(E.act, 1)
                        if ahead:
                            ffn_hi(2 * i + (M // 2 + M * stage + o + 1), 1)

                with nc.scalar.Fori(0, steps // 2 - (1 if stage == 2 else 0)) as i:
                    two_chunks(i)
                if stage == 2:
                    two_chunks(steps // 2 - 1, last=True)

        @block.vector
        def _(dve):
            link = [0]

            def chain(ins):
                link[0] += 1
                ins.then_inc(dve_chain, 1)
                dve.wait_ge(dve_chain, link[0])

            def norm_stats(n, s, src):
                nc.vector.bn_stats(stats[:, s, :], src).then_inc(ln_stat, 1)
                wait_apart(dve, ln_stat, n + 1)
                nc.vector.bn_aggr(mv[:, s, :], stats[:, s, :]).then_inc(ln_mv, 1)

            def norm_apply(n, s, src, b):
                dve.wait_ge(ln_rstd, n + 1)
                nc.vector.tensor_scalar(x_res[:, b, :], src,
                                        mv[:, s, 0:1], rstd[:, s, :], ALU.subtract, ALU.mult).then_inc(ln_x, 1)

            def transposed_lo(n, b):
                dve.wait_ge(tx_hi, n + 1)
                sl = slice(b * T, (b + 1) * T)
                nc.vector.tensor_tensor(xT.lo[:, :, sl],
                                        tx_bank[n % 4][:, 0:C * T].rearrange("p (c t) -> p c t", c=C),
                                        xT.hi[:, :, sl], ALU.subtract).then_inc(tx_lo, 1)

            def keys_lo(L, b, g, i):
                a = A[L]
                k0, kn = HALVES[i]
                dve.wait_ge(a.k_hi, 8 * b + 2 * g + i + 1)
                hi, lo = kT.hi[:, g % 2, k0:k0 + kn], kT.lo[:, g % 2, k0:k0 + kn]
                if L == 0:
                    nc.vector.scalar_tensor_tensor(lo, psJ[:, 0:kn], col("bk", g), hi, ALU.add, ALU.subtract)\
                      .then_inc(a.k_lo, 1)
                else:
                    nc.vector.tensor_tensor(lo, psJ[:, 0:kn], hi, ALU.subtract).then_inc(a.k_lo, 1)

            def values_lo(a, b, j):
                dve.wait_ge(a.v_hi, NKC * b + j + 1)
                n = key_rows(j)
                nc.vector.tensor_tensor(vv.lo[0:n, j, :], psS[j % 2][0:n, 0:D], vv.hi[0:n, j, :], ALU.subtract)\
                  .then_inc(a.v_lo, 1)

            def attention(L, base):
                a = A[L]

                def head_max(b, h):
                    wait_apart(dve, a.s_mm, H * b + h + 1)
                    m = nmax[:, h % 2:h % 2 + 1]
                    if L == 0:
                        nc.vector.tensor_reduce(m, psS[h % 2][0:T, 0:KEYS], AX.X, ALU.max, negate=True)\
                          .then_inc(a.maxed, 1)
                    else:
                        if h == 0:
                            wait_apart(dve, a.mask_done, b + 1)
                        nc.vector.tensor_tensor_reduce(out=psS[h % 2][0:T, 0:KEYS], in0=psS[h % 2][0:T, 0:KEYS],
                                                       in1=maskb[:, :], scale=1.0, scalar=LOWEST, op0=ALU.add,
                                                       op1=ALU.max, accum_out=pmax[:, h % 2:h % 2 + 1])\
                          .then_inc(mx_raw, 1)
                        dve.wait_ge(mx_raw, H * b + h + 1)
                        nc.vector.tensor_scalar(m, pmax[:, h % 2:h % 2 + 1], -1.0, None, ALU.mult)\
                          .then_inc(a.maxed, 1)

                def probs_lo(b, h):
                    pr = h // 2
                    for i in range(2):
                        dve.wait_ge(a.pt_hi, 2 * (H * b + h) + i + 1)
                        sl = (slice(None), pr % 2, slice(HK * i, HK * i + HK), slice((h % 2) * T, (h % 2 + 1) * T))
                        nc.vector.tensor_tensor(pT.lo[sl],
                                                psT[:, KA * i:KA * i + HK * T].rearrange("p (k t) -> p k t", k=HK),
                                                pT.hi[sl], ALU.subtract).then_inc(a.pt_lo, 1)

                def heads_out(b, pr):
                    dve.wait_ge(a.pv_mm, H // 2 * b + pr + 1)
                    if pr == 0:
                        wait(dve, a.o_lo, b)
                    for e in range(2):
                        g, j = divmod(2 * pr + e, G)
                        cp = nc.vector.tensor_copy(oraw[HD * j:HD * (j + 1), g, :],
                                                   psO[HD * e:HD * (e + 1), T * e:T * (e + 1)])
                    cp.then_inc(a.o_copied, 1)

                def batch(b, last, first=False):
                    for t in range(H + 1):
                        if t < H:
                            head_max(b, t)
                        if t >= 1:
                            probs_lo(b, t - 1)
                        if t == 1 and not first:
                            norm_stats(base + b - 1, 0, y[:, 0, :])
                        if t == 5 and not first:
                            norm_apply(base + b - 1, 0, y[:, 0, :], b - 1)
                        g, i = t // 4 + 1, t % 4
                        if i < 2 and g < C and t < 12:
                            keys_lo(L, b, g, i)
                        if t >= H - 1 and not last:
                            keys_lo(L, b + 1, 0, t - H + 1)
                        if t >= 4 and t % 2 == 0:
                            heads_out(b, (t - 4) // 2)
                    dve.wait_ge(a.exped, H * (b + 1))
                    nc.vector.reciprocal(rinv[:, 0:H], rsum[:, :]).then_inc(a.rinv_done, 1)
                    if not last:
                        values_lo(a, b + 1, 0)
                        values_lo(a, b + 1, 1)
                    heads_out(b, H // 2 - 1)
                    if not last:
                        values_lo(a, b + 1, 2)
                    dve.wait_ge(a.rb_mm, b + 1)
                    dve.wait_ge(a.o_copied, H // 2 * (b + 1))
                    nc.vector.tensor_tensor(oraw[:, :, :], psT[:, 0:C * T].rearrange("p (c t) -> p c t", c=C),
                                            oraw[:, :, :], ALU.mult).then_inc(a.o_scaled, 1)
                    if L == 0:
                        dve.wait_ge(a.o_scaled, b + 1)
                        nc.vector.tensor_tensor(oraw[:, :, :], oraw[:, :, :],
                                                cols4("bv", C).unsqueeze(2).to_broadcast([P, C, T]), ALU.add)\
                          .then_inc(a.o_biased, 1)
                    if not last:
                        values_lo(a, b + 1, 3)
                    dve.wait_ge(a.o_hi, b + 1)
                    nc.vector.tensor_tensor(oT.lo[:, :, :], oraw[:, :, :], oT.hi[:, :, :], ALU.subtract)\
                      .then_inc(a.o_lo, 1)
                    if not last:
                        values_lo(a, b + 1, 4)
                        values_lo(a, b + 1, 5)
                    dve.wait_ge(a.resid_done, b + 1)
                    dve.wait_ge(ln_in, base + b + 1)
                    dve.wait_ge(ln_x, base + b)
                    nc.vector.tensor_tensor(y[:, 0, :], psT[0:T, KA:KA + D], resid[:, 0, :], ALU.add)\
                      .then_inc(ln_y, 1)
                    dve.wait_ge(ln_y, base + b + 1)

                batch(0, False, first=True)
                with nc.vector.Fori(1, NB - 1) as b:
                    batch(b, False)
                batch(NB - 1, True)
                norm_stats(base + NB - 1, 0, y[:, 0, :])
                norm_apply(base + NB - 1, 0, y[:, 0, :], NB - 1)

            TWO_PI = (6.28125, 1.9350051879882812e-03, 3.0199159819567e-07)
            MAGIC = 1.5 * 2.0 ** 23

            def reduce_angle(x, n):
                chain(nc.vector.tensor_scalar(n, x, 1.0 / 6.283185307179586, MAGIC, ALU.mult, ALU.add))
                chain(nc.vector.tensor_scalar(n, n, -MAGIC, None, ALU.add))
                for part in TWO_PI:
                    chain(nc.vector.scalar_tensor_tensor(x, n, -part, x, ALU.mult, ALU.add))

            dve.wait_ge(conv_in, 32)
            chain(nc.vector.tensor_copy(th[:, :], cols4("theta", C)))
            reduce_angle(th[:, :], thn[:, :])
            dve.wait_ge(act_chain, 1)
            chain(nc.vector.tensor_tensor(dec[:, :, :], kvec[:, :, :],
                                          e1[:, :].unsqueeze(2).to_broadcast([P, C, TAPS]), ALU.mult))
            assert link[0] == CH_DEC
            chain(nc.vector.tensor_tensor(ang[:, :, :], kvec[:, :, :],
                                          th[:, :].unsqueeze(2).to_broadcast([P, C, TAPS]), ALU.mult))
            reduce_angle(ang[:, :, :], turns[:, :, :])
            chain(nc.vector.tensor_scalar(turns[:, :, :], ang[:, :, :], -1.0, None, ALU.mult))
            chain(nc.vector.tensor_tensor(ang[:, :, :], ang[:, :, :], turns[:, :, :], ALU.max))
            chain(nc.vector.tensor_scalar(ang[:, :, :], ang[:, :, :], -1.0, 1.5707963267948966, ALU.mult, ALU.add))
            assert link[0] == CH_ANG
            dve.wait_ge(act_chain, 3)
            chain(nc.vector.tensor_tensor(taps[:, :, :], dec[:, :, :], ang[:, :, :], ALU.mult))
            chain(nc.vector.tensor_tensor(past[:, :, :], taps[:, :, 1:TAPS],
                                          cols4("init", C).unsqueeze(2).to_broadcast([P, C, NB]), ALU.mult))
            dve.wait_ge(x_in, 16)
            for c in range(C):
                nc.vector.tensor_tensor(acc[:, c, :].rearrange("p (n t) -> p n t", n=NB),
                                        cin[:, c, :].rearrange("p (n t) -> p n t", n=NB),
                                        past[:, c, :].unsqueeze(2).to_broadcast([P, NB, T]), ALU.add)\
                  .then_inc(conv_done, 1)
            for k in range(1, NB):
                for c in range(C):
                    dve.wait_ge(conv_done, C * (k - 1) + c + 1)
                    nc.vector.scalar_tensor_tensor(acc[:, c, k * T:TOK], cin[:, c, 0:TOK - k * T], taps[:, c, k:k + 1],
                                                   acc[:, c, k * T:TOK], ALU.mult, ALU.add).then_inc(conv_done, 1)
                if k in (3, 4):
                    keys_lo(0, 0, 0, k - 3)
                if k >= 5:
                    values_lo(A[0], 0, k - 5)
            for c in range(C):
                dve.wait_ge(conv_done, C * (NB - 1) + c + 1)
                nc.vector.scalar_tensor_tensor(acc[:, c, :], acc[:, c, :], 1.0, cin[:, c, :], ALU.add, ALU.mult)\
                  .then_inc(conv_done, 1)
            for j in range(3, NKC):
                values_lo(A[0], 0, j)
            for b in range(NB):
                dve.wait_ge(ln_y, LN_CONV + b + 1)
                norm_stats(LN_CONV + b, b % 2, y[:, b % 2, :])
                if b >= 1:
                    norm_apply(LN_CONV + b - 1, (b - 1) % 2, y[:, (b - 1) % 2, :], b - 1)
            norm_apply(LN_CONV + NB - 1, (NB - 1) % 2, y[:, (NB - 1) % 2, :], NB - 1)
            for b in range(NB):
                transposed_lo(LN_CONV + b, b)
            attention(0, LN_ATT0)
            for b in range(NB):
                transposed_lo(LN_ATT0 + b, b)

            def norm(n, b, s, src, other):
                dve.wait_ge(ln_in, n + 1)
                dve.wait_ge(ln_x, n - 1 if s is not None else n)
                s = s or 0
                nc.vector.tensor_tensor(y[:, s, :], src, other, ALU.add).then_inc(ln_y, 1)
                dve.wait_ge(ln_y, n + 1)
                norm_stats(n, s, y[:, s, :])

            def norms(base, bank, other, before, transposed=False):
                for b in range(NB):
                    before(b)
                    norm(base + b, b, b % 2, bank(b), other(b))
                    if b >= 1:
                        norm_apply(base + b - 1, (b - 1) % 2, y[:, (b - 1) % 2, :], b - 1)
                    if transposed and b >= 4:
                        transposed_lo(base + b - 4, b - 4)
                norm_apply(base + NB - 1, (NB - 1) % 2, y[:, (NB - 1) % 2, :], NB - 1)
                if transposed:
                    for b in range(NB - 4, NB):
                        transposed_lo(base + b, b)

            for h in range(2):
                dve.wait_ge(F.p_hi, h + 1)
                sl = slice(h * HALF, (h + 1) * HALF)
                nc.vector.tensor_tensor(f_p.lo[:, sl], bank4[2 * h][:, 0:HALF], f_p.hi[:, sl], ALU.subtract)\
                  .then_inc(F.p_lo, 1)
            for u in range(2 * M):
                dve.wait_ge(F.h_act, u + 1)
                wait(dve, F.acc_mm, u - 3)
                nc.vector.tensor_copy(f_g.hi[:, u % 4, :], f_act[:, u % 4, :]).then_inc(F.h_hi, 1)
                dve.wait_ge(F.h_hi, u + 1)
                nc.vector.tensor_tensor(f_g.lo[:, u % 4, :], f_act[:, u % 4, :], f_g.hi[:, u % 4, :], ALU.subtract)\
                  .then_inc(F.h_lo, 1)
            for h in range(2):
                dve.wait_ge(F.q_hi, h + 1)
                sl = slice(h * HALF, (h + 1) * HALF)
                nc.vector.tensor_tensor(f_q.lo[:, sl], bank4[2 * h][:, 0:HALF], f_q.hi[:, sl], ALU.subtract)\
                  .then_inc(F.q_lo, 1)
            norms(LN_FFN0, lambda b: ln_bank[b % 2][0:T, :], lambda b: resid[:, b % 2, :],
                  lambda b: dve.wait_ge(ffn0_resid, b + 1), transposed=True)

            dve.wait_ge(R.tables_in, 64)
            for u in range(R_UNITS):
                dve.wait_ge(R.rot_mm, u + 1)
                wait(dve, R.rope, u - 1)
                nc.vector.tensor_tensor(sinx[:, u % 2, :].rearrange("p (b t) -> p b t", t=T),
                                        bank4b[u % 4][:, 0:HALF].rearrange("p (b t) -> p b t", t=T),
                                        stab[:, :].unsqueeze(1).to_broadcast([P, NB // 2, T]), ALU.mult)\
                  .then_inc(R.sin, 1)

            def query_blocks_lo(b):
                ts = bass.ds(b * T, T)
                dve.wait_ge(R.q_hi, b + 1)
                for j in range(G):
                    r = slice(HD * j, HD * (j + 1))
                    last = nc.vector.tensor_tensor(qbd.lo[r, :, j, :], qk[0][r, :, ts], qbd.hi[r, :, j, :],
                                                   ALU.subtract)
                last.then_inc(R.q_ready, 1)

            heads = lambda t: t.rearrange("t (h e) -> t h e", h=H)
            spread = lambda t: t[:, :].unsqueeze(2).to_broadcast([T, H, HD])

            def first_context_lo(c):
                dve.wait_ge(A[1].ctx_hi, c + 1)
                nc.vector.tensor_tensor(cT.lo[:, c, :], (ctx_more if c >= 2 else ctx_raw)[:, c % 2, :], cT.hi[:, c, :],
                                        ALU.subtract).then_inc(A[1].ctx_split, 1)

            def retention_values_lo(b):
                dve.wait_ge(R.v_hi, b + 1)
                nc.vector.tensor_tensor(vb.lo[:, :], psT[0:T, 0:D], vb.hi[:, :], ALU.subtract).then_inc(R.v_lo, 1)

            def retention_dve(b, cur=True, prev=True, before=True, after=True):
                def decayed(g):
                    dve.wait_ge(R.s_mm, C * b + g + 1)
                    wait(dve, R.p_lo, C * b + g - 1)
                    nc.vector.tensor_tensor(p_raw[:, g % 2, :], bank4[g][0:T, 0:G * T],
                                            decay[:, G * g:G * (g + 1), :].rearrange("t h s -> t (h s)"), ALU.mult)\
                      .then_inc(R.decayed, 1)

                def p_lo(g):
                    dve.wait_ge(R.p_hi, C * b + g + 1)
                    nc.vector.tensor_tensor(pb.lo[:, g % 2, :], p_raw[:, g % 2, :], pb.hi[:, g % 2, :], ALU.subtract)\
                      .then_inc(R.p_lo, 1)

                if cur:
                    decayed(0)
                    decayed(1)
                    p_lo(0)
                    p_lo(1)
                if prev:
                    dve.wait_ge(R.g_sq, b)
                    nc.vector.tensor_reduce(gsum2[:, :], heads(gsq[:, :]), AX.X, ALU.add).then_inc(R.g_sum2, 1)
                if cur:
                    decayed(2)
                if cur:
                    decayed(3)
                if before:
                    norm(LN_RET + b - 2, b - 2, None, psT[0:T, KA:KA + D], x_res[:, b - 2, :])
                if cur:
                    p_lo(2)
                if prev:
                    dve.wait_ge(R.g_root, b)
                    nc.vector.tensor_tensor(heads(gd[:, :]), heads(gd[:, :]), spread(groot), ALU.mult)\
                      .then_inc(R.g_norm, 1)
                if cur:
                    p_lo(3)
                if after:
                    query_blocks_lo(b + 1)
                if before:
                    norm_apply(LN_RET + b - 2, 0, y[:, 0, :], b - 2)
                if prev and not cur:
                    for n in range(EARLY):
                        transposed_lo(LN_RET + n, n)
                    first_context_lo(0)
                if prev:
                    dve.wait_ge(R.o_hi, b)
                    nc.vector.tensor_tensor(r_oT.lo[:, :, :], r_o[:, :, :], r_oT.hi[:, :, :], ALU.subtract)\
                      .then_inc(R.o_lo, 1)
                if cur:
                    dve.wait_ge(R.pv_mm, C * b + C)
                    nc.vector.tensor_reduce(gsum[:, :], heads(psO[0:T, 0:D]), AX.X, ALU.add).then_inc(R.g_sum, 1)
                    dve.wait_ge(R.g_sum, b + 1)
                    nc.vector.tensor_scalar(gneg[:, :], gsum[:, :], -1.0 / HD, None, ALU.mult).then_inc(R.g_mean, 1)
                    dve.wait_ge(R.g_mean, b + 1)
                    nc.vector.tensor_tensor(heads(gd[:, :]), heads(psO[0:T, 0:D]), spread(gneg), ALU.add)\
                      .then_inc(R.g_dev, 1)
                if after:
                    retention_values_lo(b + 1)

            query_blocks_lo(0)
            retention_values_lo(0)
            retention_dve(0, prev=False, before=False)
            retention_dve(1, before=False)
            with nc.vector.Fori(2, NB - 1) as b:
                retention_dve(b)
            retention_dve(NB - 1, after=False)
            retention_dve(NB, cur=False, after=False)
            dve.wait_ge(ln_in, LN_RET + NB)
            for c in range(1, C):
                first_context_lo(c)
            retention_dve(NB + 1, cur=False, prev=False, after=False)
            for i in range(2):
                keys_lo(1, 0, 0, i)
            for b in range(EARLY, NB):
                transposed_lo(LN_RET + b, b)
            for j in range(NKC):
                values_lo(A[1], 0, j)
            attention(1, LN_ATT1)
            for b in range(NB):
                transposed_lo(LN_ATT1 + b, b)

            def gate(i, q, first=False):
                dve.wait_ge(E.silu, 4 * i + q + 1)
                if not (first and q < 2):
                    dve.wait_ge(E.g_lo, 4 * i + q - 1)
                nc.vector.scalar_tensor_tensor(gated[:, q % 2, :], bank4b[q][:, 0:HALF],
                                               cols[:, bass.ds(2 * i + (COL_AT["w2s"] + q // 2), 1)],
                                               silu[:, q % 2, :], ALU.mult, ALU.mult).then_inc(E.gated, 1)

            def gate_parts(i, q):
                sl = (slice(None), 2 * i + q // 2, slice((q % 2) * HALF, (q % 2 + 1) * HALF))
                dve.wait_ge(E.gated, 4 * i + q + 1)
                nc.vector.tensor_copy(hid.hi[sl], gated[:, q % 2, :]).then_inc(E.g_hi, 1)
                dve.wait_ge(E.g_hi, 4 * i + q + 1)
                nc.vector.tensor_tensor(hid.lo[sl], gated[:, q % 2, :], hid.hi[sl], ALU.subtract).then_inc(E.g_lo, 1)

            def gates(i, first=False):
                for q in range(4):
                    gate(i, q, first)
                    gate_parts(i, q)

            gates(0, True)
            with nc.vector.Fori(1, M // 2) as i:
                gates(i)
            for k in range(2 * M):
                dve.wait_ge(E.conv_hi, k + 1)
                nc.vector.tensor_tensor(hid.lo[:, k % M, :], h_act[:, k % M, :], hid.hi[:, k % M, :], ALU.subtract)\
                  .then_inc(E.conv_lo, 1)
            norms(LN_FFN1, lambda b: ln_bank[b % 2][0:T, :], lambda b: x_res[:, b, :], lambda b: None)

        @block.tensor
        def _(pe):
            def keys(a, b, g, i, fresh=False, weights=None):
                k0, kn = HALVES[i]
                wait(pe, a.k_lo, 8 * b + 2 * g + i)
                for c in range(C):
                    if weights:
                        pe.wait_ge(w_split, BLOCKS[weights] + c // 2 + 1)
                    if fresh:
                        pe.wait_ge(a.ctx_split, C * b + (c + 1))
                    sl = slice(P * g, P * (g + 1))
                    mm = three(psJ[:, 0:kn], (wk.hi[:, c, sl], wk.lo[:, c, sl]),
                               (cT.hi[:, c, k0:k0 + kn], cT.lo[:, c, k0:k0 + kn]), c == 0, c == C - 1)
                mm.then_inc(a.k_mm, 1)

            def values(a, b, j):
                if j < 2:
                    wait(pe, a.exped, H * b)
                else:
                    pe.wait_ge(a.v_lo, NKC * b + j - 1)
                n, k0 = key_rows(j), KC * j
                for c in range(C):
                    mm = three(psS[j % 2][0:n, 0:D], (cT.hi[:, c, k0:k0 + n], cT.lo[:, c, k0:k0 + n]),
                               (wv.hi[:, c, :], wv.lo[:, c, :]), c == 0, c == C - 1)
                mm.then_inc(a.v_mm, 1)

            def transpose_x(n, b):
                pe.wait_ge(ln_x, n + 1)
                wait(pe, tx_lo, n - 3)
                for c in range(C):
                    mm = nc.tensor.transpose(tx_bank[n % 4][:, c * T:(c + 1) * T], x_res[:, b, c * P:(c + 1) * P],
                                             ident[0:T, 0:T])
                mm.then_inc(tx_mm, 1)

            def queries(a, w):
                for i in range(2 * C):
                    m, h = i // 2, i % 2
                    wait(pe, a.q_done, i - 3)
                    out = psS[i % 2][:, (i // 2 % 2) * KA:(i // 2 % 2) * KA + HALF]
                    for c in range(C):
                        sl, tk = slice(P * m, P * (m + 1)), slice(h * HALF, (h + 1) * HALF)
                        mm = three(out, (w.hi[:, c, sl], w.lo[:, c, sl]), (xT.hi[:, c, tk], xT.lo[:, c, tk]),
                                   c == 0, c == C - 1)
                    mm.then_inc(a.q_mm, 1)

            def attention(L, base):
                a = A[L]

                def scores(b, h):
                    g, j = divmod(h, G)
                    if h == 0:
                        pe.wait_ge(a.qs_done, b + 1)
                    if j == 0:
                        pe.wait_ge(a.k_lo, 8 * b + 2 * g + 2)
                    if h < 2:
                        pe.wait_ge(a.v_lo, NKC * (b + 1))
                    else:
                        pe.wait_ge(a.exped, H * b + h - 1)
                    rows_ = slice(HD * j, HD * (j + 1))
                    for k0, kn in PIECES:
                        mm = three(psS[h % 2][0:T, k0:k0 + kn], (qs.hi[rows_, g, :], qs.lo[rows_, g, :]),
                                   (kT.hi[rows_, g % 2, k0:k0 + kn], kT.lo[rows_, g % 2, k0:k0 + kn]), True, True)
                    mm.then_inc(a.s_mm, 1)

                def transposes(b, h):
                    pe.wait_ge(a.exped, H * b + h + 1)
                    wait(pe, a.pt_lo, 2 * (H * b + h))
                    if h == 0:
                        wait(pe, ln_y, base + b)
                    for k in range(NKC):
                        k0 = KA * (k // HK) + T * (k % HK)
                        mm = nc.tensor.transpose(psT[:, k0:k0 + T], p[:, h % 2, KC * k:KC * (k + 1)], ident[0:T, 0:T])
                    mm.then_inc(a.t_mm, 1)

                def weighted(b, pr, half):
                    if half == 0:
                        pe.wait_ge(a.pt_lo, 2 * (H * b + 2 * pr + 2))
                        wait(pe, a.o_copied, H // 2 * b + pr)
                    fs = slice(2 * HD * pr, 2 * HD * (pr + 1))
                    for k in range(HK * half, HK * (half + 1)):
                        n = key_rows(k)
                        mm = three(psO[0:2 * HD, 0:2 * T], (vv.hi[0:n, k, fs], vv.lo[0:n, k, fs]),
                                   (pT.hi[0:n, pr % 2, k, :], pT.lo[0:n, pr % 2, k, :]), k == 0, k == NKC - 1)
                    if half == 1:
                        mm.then_inc(a.pv_mm, 1)

                def batch(b, last):
                    for t in range(H + 1):
                        if t < H:
                            scores(b, t)
                        if t >= 1:
                            transposes(b, t - 1)
                        if t >= 3:
                            weighted(b, (t - 3) // 2, (t - 3) % 2)
                        g, i = t // 4 + 1, t % 4
                        if i < 2 and g < C and t < 12:
                            keys(a, b, g, i)
                        if t >= H - 1 and not last:
                            keys(a, b + 1, 0, t - H + 1, fresh=t == H - 1)
                    if not last:
                        values(a, b + 1, 0)
                    weighted(b, H // 2 - 1, 0)
                    weighted(b, H // 2 - 1, 1)
                    if not last:
                        values(a, b + 1, 1)
                    pe.wait_ge(a.rinv_done, b + 1)
                    nc.tensor.transpose(psT[:, 0:T], rinv[:, :], ident[0:T, 0:T]).then_inc(a.rt_mm, 1)
                    if not last:
                        values(a, b + 1, 2)
                    pe.wait_ge(a.rt_copied, b + 1)
                    for g in range(C):
                        mm = nc.tensor.matmul(psT[:, g * T:(g + 1) * T], sel[:, g, :], rT[:, :], start=True, stop=True)
                    mm.then_inc(a.rb_mm, 1)
                    if not last:
                        for j in range(3, NKC):
                            values(a, b + 1, j)
                    if isinstance(b, int) and b == 0:
                        pe.wait_ge(w_split, BLOCKS[("wo0", "wo1")[L]] + 2)
                    pe.wait_ge(a.o_lo, b + 1)
                    for c in range(C):
                        mm = three(psT[0:T, KA:KA + D], (oT.hi[:, c, :], oT.lo[:, c, :]),
                                   (wqo.hi[:, c, :], wqo.lo[:, c, :]), c == 0, c == C - 1)
                    mm.then_inc(ln_in, 1)

                batch(0, False)
                with nc.tensor.Fori(1, NB - 1) as b:
                    batch(b, False)
                batch(NB - 1, True)
                for b in range(NB):
                    transpose_x(base + b, b)

            for i in range(2):
                keys(A[0], 0, 0, i, fresh=i == 0, weights=None if i else "wk0")
            pe.wait_ge(w_split, 4)
            for j in range(NKC):
                values(A[0], 0, j)
            pe.wait_ge(consts_in, 80)
            for b in range(NB):
                if b == 0:
                    pe.wait_ge(conv_done, C * (NB + 1))
                wait(pe, ln_y, LN_CONV + b - 1)
                if b == 1:
                    pe.wait_ge(A[0].k_lo, 2)
                for c in range(C):
                    mm = nc.tensor.transpose(ln_bank[b % 2][0:T, c * P:(c + 1) * P], acc[:, c, b * T:(b + 1) * T],
                                             ident[:, :])
                mm.then_inc(ln_in, 1)
            for b in range(NB):
                if b == 0:
                    pe.wait_ge(A[0].v_lo, NKC)
                transpose_x(LN_CONV + b, b)
            pe.wait_ge(tx_lo, NB)
            pe.wait_ge(w_split, BLOCKS["wq0"] + 2)
            queries(A[0], wqo)
            attention(0, LN_ATT0)

            pe.wait_ge(tx_lo, LN_ATT0 + NB)
            pe.wait_ge(w_split, BLOCKS["v2"] + 1)
            for h in range(2):
                tk = slice(h * HALF, (h + 1) * HALF)
                for c in range(C):
                    mm = three(bank4[2 * h][:, 0:HALF], (u1.hi[:, c, :], u1.lo[:, c, :]),
                               (xT.hi[:, c, tk], xT.lo[:, c, tk]), c == 0, c == C - 1)
                mm.then_inc(F.p_mm, 1)
            pe.wait_ge(F.p_lo, 2)
            for u in range(2 * M + 2):
                if u < 2 * M:
                    m, h = divmod(u, 2)
                    ms, tk = slice(P * m, P * (m + 1)), slice(h * HALF, (h + 1) * HALF)
                    wait(pe, F.h_act, u - 3)
                    three(bank4b[u % 4][:, 0:HALF], (v1.hi[:, ms], v1.lo[:, ms]), (f_p.hi[:, tk], f_p.lo[:, tk]),
                          True, True).then_inc(F.h_mm, 1)
                if u >= 2:
                    m, h = divmod(u - 2, 2)
                    pe.wait_ge(F.h_lo, u - 1)
                    three(bank4[2 * h][:, 0:HALF], (u2.hi[:, m, :], u2.lo[:, m, :]),
                          (f_g.hi[:, (u - 2) % 4, :], f_g.lo[:, (u - 2) % 4, :]), m == 0, m == M - 1)\
                        .then_inc(F.acc_mm, 1)
            pe.wait_ge(F.q_lo, 2)
            for b in range(NB + 3):
                if b < NB:
                    wait(pe, ln_y, LN_FFN0 + b - 1)
                    tk = slice(b * T, (b + 1) * T)
                    three(ln_bank[b % 2][0:T, :], (f_q.hi[:, tk], f_q.lo[:, tk]), (v2.hi[:, :], v2.lo[:, :]),
                          True, True).then_inc(ln_in, 1)
                if b >= 3:
                    transpose_x(LN_FFN0 + b - 3, b - 3)

            pe.wait_ge(tx_lo, LN_FFN0 + NB)
            pe.wait_ge(w_split, BLOCKS["rk"] + 2)
            pe.wait_ge(R.tables_in, 64)
            for u in range(R_UNITS + 1):
                if u < R_UNITS:
                    m, h = u // 2 % C, u % 2
                    w = (rqo, rk)[u // (2 * C)]
                    wait(pe, R.q_raw, u - 3)
                    for c in range(C):
                        sl, tk = slice(P * m, P * (m + 1)), slice(h * HALF, (h + 1) * HALF)
                        mm = three(bank4[u % 4][:, 0:HALF], (w.hi[:, c, sl], w.lo[:, c, sl]),
                                   (xT.hi[:, c, tk], xT.lo[:, c, tk]), c == 0, c == C - 1)
                    mm.then_inc(R.q_mm, 1)
                if u >= 1:
                    v = u - 1
                    m, h = v // 2 % C, v % 2
                    pe.wait_ge(R.q_raw, v + 1)
                    wait(pe, R.sin, v - 3)
                    nc.tensor.matmul(bank4b[v % 4][:, 0:HALF], rotm[:, :],
                                     qk[v // (2 * C)][:, m, h * HALF:(h + 1) * HALF], start=True, stop=True)\
                      .then_inc(R.rot_mm, 1)

            def retention_values(b):
                pe.wait_ge(R.x_ready, b + 1)
                wait(pe, R.v_lo, b)
                for c in range(C):
                    mm = three(psT[0:T, 0:D], (xb.hi[:, c, :], xb.lo[:, c, :]), (rv.hi[:, c, :], rv.lo[:, c, :]),
                               c == 0, c == C - 1)
                mm.then_inc(R.v_mm, 1)

            def retention_scores(b):
                pe.wait_ge(R.k_ready, b + 1)
                pe.wait_ge(R.q_ready, b + 1)
                for g in range(C):
                    wait(pe, R.decayed, C * b + g - C + 1)
                    three(bank4[g][0:T, 0:G * T], (kb.hi[:, g, :], kb.lo[:, g, :]),
                          (qbd.hi[:, g, :, :], qbd.lo[:, g, :, :]), True, True).then_inc(R.s_mm, 1)

            def retention_pe(b, cur=True, prev=True, after=True):
                def weighted(g):
                    pe.wait_ge(R.p_lo, C * b + g + 1)
                    if g == 0:
                        wait(pe, R.g_dev, b)
                        pe.wait_ge(R.v_lo, b + 1)
                    for j in range(G):
                        hs, ts = slice(HD * (G * g + j), HD * (G * g + j + 1)), slice(T * j, T * (j + 1))
                        mm = three(psO[0:T, hs], (pb.hi[:, g % 2, ts], pb.lo[:, g % 2, ts]),
                                   (vb.hi[:, hs], vb.lo[:, hs]), True, True)
                    mm.then_inc(R.pv_mm, 1)

                if cur:
                    weighted(0)
                    weighted(1)
                if cur:
                    weighted(2)
                if prev:
                    pe.wait_ge(R.g_norm, b)
                    for c in range(C):
                        mm = nc.tensor.transpose(psJ[:, c * T:(c + 1) * T], gd[:, c * P:(c + 1) * P], ident[0:T, 0:T])
                    mm.then_inc(R.to_mm, 1)
                if cur:
                    weighted(3)
                if after:
                    retention_values(b + 1)
                    retention_scores(b + 1)
                if prev:
                    pe.wait_ge(R.o_lo, b)
                    wait(pe, ln_y, LN_RET + b - 1)
                    for c in range(C):
                        mm = three(psT[0:T, KA:KA + D], (r_oT.hi[:, c, :], r_oT.lo[:, c, :]),
                                   (rqo.hi[:, c, :], rqo.lo[:, c, :]), c == 0, c == C - 1)
                    mm.then_inc(ln_in, 1)

            pe.wait_ge(R.sin, R_UNITS)
            pe.wait_ge(w_split, BLOCKS["rv"] + 2)
            retention_values(0)
            retention_scores(0)
            retention_pe(0, prev=False)
            pe.wait_ge(w_split, BLOCKS["ro"] + 2)
            with nc.tensor.Fori(1, NB - 1) as b:
                retention_pe(b)
            retention_pe(NB - 1, after=False)
            for b in range(EARLY):
                transpose_x(LN_RET + b, b)
            retention_pe(NB, cur=False, after=False)

            for i in range(2):
                keys(A[1], 0, 0, i, fresh=i == 0, weights=None if i else "wk1")
            for b in range(EARLY, NB):
                transpose_x(LN_RET + b, b)
            pe.wait_ge(tx_lo, LN_RET + NB)
            pe.wait_ge(w_split, BLOCKS["wv1"] + 2)
            for j in range(NKC):
                values(A[1], 0, j)
            pe.wait_ge(A[1].v_lo, NKC)
            pe.wait_ge(w_split, BLOCKS["wq1"] + 2)
            queries(A[1], wqo)
            attention(1, LN_ATT1)

            pe.wait_ge(tx_lo, LN_ATT1 + NB)

            def gate_units(i):
                for e in range(2):
                    pe.wait_ge(w_split, 2 * i + (BLOCKS["w12"] + e + 1))
                    for h in range(2):
                        q, tk = 2 * e + h, slice(h * HALF, (h + 1) * HALF)
                        if not isinstance(i, int):
                            pe.wait_ge(E.gated, 4 * i + q - 3)
                        for k, bank in ((0, bank4[q]), (C, bank4b[q])):
                            for c in range(C):
                                ws = slice(P * (k + c), P * (k + c + 1))
                                mm = three(bank[:, 0:HALF], (fw.hi[:, e, ws], fw.lo[:, e, ws]),
                                           (xT.hi[:, c, tk], xT.lo[:, c, tk]), c == 0, c == C - 1)
                        mm.then_inc(E.w_mm, 1)

            gate_units(0)
            with nc.tensor.Fori(1, M // 2) as i:
                gate_units(i)
            pe.wait_ge(E.g_lo, 2 * M)
            pe.wait_ge(E.gated, 2 * M)
            for stage, (name, steps) in enumerate((("h1", M // 2), ("h2", M // 2), ("w3", C // 2))):
                def step(i, stage=stage, name=name):
                    for o in range(2):
                        for e in range(2):
                            pe.wait_ge(w_split, 4 * i + (BLOCKS[name] + 2 * o + e + 1))
                            if e == 0 and (stage or not isinstance(i, int)):
                                pe.wait_ge(E.act, 4 * i + (2 * M * stage + 2 * o - 2))
                            for k in range(M // 2):
                                kk = M // 2 * e + k
                                if stage and o == 0:
                                    pe.wait_ge(E.conv_lo, M * (stage - 1) + kk + 1)
                                for h in range(2):
                                    ws, tk = slice(P * k, P * (k + 1)), slice(h * HALF, (h + 1) * HALF)
                                    mm = three(bank4[2 * o + h][:, 0:HALF], (fw.hi[:, e, ws], fw.lo[:, e, ws]),
                                               (hid.hi[:, kk, tk], hid.lo[:, kk, tk]), kk == 0, kk == M - 1)
                                    if kk == M - 1:
                                        mm.then_inc(E.m_mm, 1)
                            if e == 0:
                                mm.then_inc(E.blk_used, 1)

                if stage == 0:
                    step(0)
                with nc.tensor.Fori(0 if stage else 1, steps) as i:
                    step(i)
            pe.wait_ge(E.act, 2 * (2 * M + C))
            for b in range(NB):
                wait(pe, ln_y, LN_FFN1 + b - 1)
                for c in range(C):
                    mm = nc.tensor.transpose(ln_bank[b % 2][0:T, c * P:(c + 1) * P], h_act[:, c, b * T:(b + 1) * T],
                                             ident[:, :])
                mm.then_inc(ln_in, 1)


def kernel(**inputs):
    import numpy as np
    import concourse.bacc as bacc
    from concourse.bass_utils import run_bass_kernel_spmd

    f = {k: np.asarray(v) for k, v in inputs.items()}
    feats = lambda w, n: np.ascontiguousarray(w.reshape(w.shape[0] // P, P, n).transpose(1, 0, 2))

    def halves(w):
        return np.ascontiguousarray(feats(w, D).reshape(P, 2, BLK).transpose(1, 0, 2))

    def tiles(w):
        o, i = w.shape
        return w.reshape(o // P, P, i // P, P).transpose(0, 3, 2, 1)

    def padded(w):
        out = np.zeros((1, P, BLK), w.dtype)
        out[0, :, :w.shape[1]] = w
        return out

    x = f["x"].reshape(TOK, D)
    arrays = {}
    arrays["xT"] = np.ascontiguousarray(x.T.reshape(C, P, TOK).transpose(1, 0, 2))
    arrays["ctxT"] = np.ascontiguousarray(f["ctx_1024"].reshape(NB * KEYS, D).T.reshape(C, P, NB * KEYS))
    arrays["mask"] = np.ascontiguousarray(f["mask_BxS2_ik0"])
    names = {"lmlg": "L0_attn_lmlg", "theta": "L0_attn_theta", "init": "L0_attn_last_conv_init", "bq": "L0_xattn_bq",
             "bk": "L0_xattn_bk", "bv": "L0_xattn_bv", "gnw": "L1_attn_gn_weight", "gnb": "L1_attn_gn_bias",
             "b1": "L0_ffn_b1", "w1s": "L1_ffn_w1_s", "w2s": "L1_ffn_w2_s", "h1s": "L1_ffn_h1_s",
             "h2s": "L1_ffn_h2_s", "w3s": "L1_ffn_w3_s"}
    arrays["cols"] = np.ascontiguousarray(np.concatenate([f[names[n]].reshape(k, P).T for n, k in COLUMNS], axis=1))
    for n, m in (("wk0", "L0_xattn_Wk"), ("wv0", "L0_xattn_Wv"), ("wq0", "L0_xattn_Wq"), ("wo0", "L0_xattn_Wo"),
                 ("wq1", "L1_xattn_Wq"), ("wo1", "L1_xattn_Wproj")):
        arrays[n] = halves(f[m])
    arrays["wk1"], arrays["wv1"] = halves(f["L1_xattn_Wkv"][:, :D]), halves(f["L1_xattn_Wkv"][:, D:])
    for n, m in (("rq", "Wq"), ("rk", "Wk"), ("rv", "Wv"), ("ro", "Wo")):
        arrays[n] = halves(f["L1_attn_" + m].T)
    for n, m in (("bo", "L0_xattn_bo"), ("b2", "L0_ffn_b2"), ("bproj", "L1_xattn_bproj")):
        arrays[n] = f[m].reshape(1, D)
    arrays["u1"] = padded(feats(f["L0_ffn_U1"], RANK).reshape(P, C * RANK))
    arrays["v1"] = np.ascontiguousarray(f["L0_ffn_V1"].reshape(P, 2, BLK).transpose(1, 0, 2))
    arrays["u2"] = np.ascontiguousarray(feats(f["L0_ffn_U2"], RANK).reshape(P, 2, BLK).transpose(1, 0, 2))
    arrays["v2"] = padded(f["L0_ffn_V2"])
    w1, w2 = tiles(f["L1_ffn_w1_w"]), tiles(f["L1_ffn_w2_w"])
    blocks = [np.concatenate([w1, w2], axis=2).reshape(M, P, BLK)]
    for m in ("L1_ffn_h1_w", "L1_ffn_h2_w", "L1_ffn_w3_w"):
        w = tiles(f[m])
        blocks.append(w.reshape(w.shape[0], P, 2, BLK).transpose(0, 2, 1, 3).reshape(-1, P, BLK))
    arrays["ffn"] = np.concatenate(blocks)
    arrays["ident"] = np.eye(P, dtype=np.float32)
    arrays["kvec"] = np.ascontiguousarray(np.broadcast_to(np.arange(TAPS, dtype=np.float32), (P, C, TAPS)))
    s = np.zeros((H, C, P), np.float32)
    for h in range(H):
        s[h, h // G, HD * (h % G):HD * (h % G + 1)] = 1.0
    arrays["sel"] = s
    freq = (1.0 / 10000.0 ** (np.arange(0, HD, 2, dtype=np.float32) / HD)).astype(np.float32)
    emb = np.tile(np.arange(T, dtype=np.float32)[None, :] * freq[:, None], (P // len(freq), 1))
    sign = np.where(np.arange(P) % HD < HD // 2, -1.0, 1.0).astype(np.float32)
    arrays["cos"] = np.cos(emb).astype(np.float32)
    arrays["sin"] = (np.sin(emb) * sign[:, None]).astype(np.float32)
    arrays["rotm"] = np.eye(P, dtype=np.float32)[np.arange(P) ^ (HD // 2)]
    gamma = (1.0 - 2.0 ** (-5.0 - np.arange(H, dtype=np.float32))).astype(np.float32)
    dist = np.arange(T)[None, None, :] - np.arange(T)[:, None, None]
    arrays["decay"] = np.where(dist >= 0, SCALE * gamma[None, :, None] ** np.maximum(dist, 0), 0.0).astype(np.float32)
    arrays = {n + "_dram": np.ascontiguousarray(a) for n, a in arrays.items()}

    nc = bacc.Bacc("TRN2", target_bir_lowering=False, num_devices=1)
    d = {}
    for n, a in arrays.items():
        d[n[:-5]] = nc.dram_tensor(n, a.shape, mybir.dt.from_np(a.dtype), kind="ExternalInput").ap()
    d["out"] = nc.dram_tensor("out_dram", (NB, T, D), mybir.dt.float32, kind="ExternalOutput").ap()
    decoder_kernel(nc, d)
    r = run_bass_kernel_spmd(nc, [arrays], core_ids=[0])
    return r.results[0]["out_dram"]
```
